# Optimizing a Trainium2 kernel written in Bass

```python
import numpy as np
import jax
import jax.numpy as jnp

def _softmax(x, axis=-1):
    return jax.nn.softmax(x, axis=axis)

def _gelu(x):
    return jax.nn.gelu(x, approximate=True)

def _silu(x):
    return jax.nn.silu(x)

def _sigmoid(x):
    return jax.nn.sigmoid(x)

def _layernorm(x, axis=-1, eps=1e-05):
    m = jnp.mean(x, axis=axis, keepdims=True)
    v = jnp.var(x, axis=axis, keepdims=True)
    return (x - m) / jnp.sqrt(v + eps)

def _scatter_add(tgt, idx, src, axis=0):
    return tgt.at[idx].add(src)

def _segment_sum(src, seg, n):
    return jax.ops.segment_sum(src, seg, n)
kernel_name = 'mk_gnn_ffn_d1_gnn_r32_36e6e0'

def setup_inputs(seed: int=0):
    np.random.seed(seed)
    _w = jnp.asarray

    def _rec_inputs():
        import jax
        import jax.numpy as jnp
        _gk = jax.random.key(seed)
        x = -0.0002117 + 1 * jax.random.normal(jax.random.fold_in(_gk, 1), (3125, 256), jnp.float32)
        src = jax.random.randint(jax.random.fold_in(_gk, 2), (50000,), 0, 3125, jnp.int32)
        dst = jax.random.randint(jax.random.fold_in(_gk, 3), (50000,), 0, 3125, jnp.int32)
        _o = jnp.argsort(dst, stable=True)
        src = src[_o]
        dst = dst[_o]
        return (x, src, dst)
    x, src, dst = _rec_inputs()

    def _L0_gnn_setup():
        import jax, jax.numpy as jnp
        import numpy as np
        N_NODES = 3125
        N_EDGES = 50000
        D_IN = 256
        D_HID = 256
        BN_EPS = 1e-05
        key = jax.random.key(seed)
        ks = jax.random.split(key, 10)
        s_in = 1.0 / np.sqrt(D_IN)
        s_hid = 1.0 / np.sqrt(D_HID)
        return {'x': jax.random.normal(ks[0], (N_NODES, D_IN), dtype=jnp.float32), 'edge_index': jax.random.randint(ks[1], (2, N_EDGES), 0, N_NODES, dtype=jnp.int64), 'gcn_W': jax.random.normal(ks[2], (D_IN, D_HID), dtype=jnp.float32) * s_in, 'gcn_b': jnp.zeros((D_HID,), dtype=jnp.float32), 'lin_W': jax.random.normal(ks[3], (D_IN, D_HID), dtype=jnp.float32) * s_in, 'lin_b': jnp.zeros((D_HID,), dtype=jnp.float32), 'gate_W': jax.random.normal(ks[4], (D_HID, D_HID), dtype=jnp.float32) * s_hid, 'gate_b': jnp.zeros((D_HID,), dtype=jnp.float32), 'bn_gamma': jnp.ones((D_HID,), dtype=jnp.float32), 'bn_beta': jnp.zeros((D_HID,), dtype=jnp.float32)}
    _L0_gnn_all = _L0_gnn_setup()
    _L0_gnn_in = {k: v for k, v in _L0_gnn_all.items() if k in ('gcn_W', 'gcn_b', 'lin_W', 'lin_b', 'gate_W', 'gate_b', 'bn_gamma', 'bn_beta')}
    del _L0_gnn_all

    def _L0_ffn_setup():
        import math
        import jax, jax.numpy as jnp
        import numpy as np
        CAPACITY_FACTOR = 1.25
        key = jax.random.key(seed)
        ks = jax.random.split(key, 5)
        B, L, D, F, E = (8, 256, 256, 1024, 8)
        h = jax.random.normal(ks[0], (B, L, D), dtype=jnp.float32)
        gate_w = jax.random.normal(ks[1], (D, E), dtype=jnp.float32) * 0.02
        gate_b = jnp.zeros((E,), dtype=jnp.float32)
        w1 = jax.random.normal(ks[2], (E, D, F), dtype=jnp.float32) * (1.0 / math.sqrt(D))
        b1 = jnp.zeros((E, F), dtype=jnp.float32)
        w2 = jax.random.normal(ks[3], (E, F, D), dtype=jnp.float32) * (1.0 / math.sqrt(F))
        b2 = jnp.zeros((E, D), dtype=jnp.float32)
        return {'h': h, 'gate_w': gate_w, 'gate_b': gate_b, 'w1': w1, 'b1': b1, 'w2': w2, 'b2': b2}
    _L0_ffn_all = _L0_ffn_setup()
    _L0_ffn_in = {k: v for k, v in _L0_ffn_all.items() if k in ('gate_w', 'gate_b', 'w1', 'b1', 'w2', 'b2')}
    del _L0_ffn_all
    return {'x': x, 'src': src, 'dst': dst, 'L0_gnn_gcn_W': _L0_gnn_in['gcn_W'], 'L0_gnn_gcn_b': _L0_gnn_in['gcn_b'], 'L0_gnn_lin_W': _L0_gnn_in['lin_W'], 'L0_gnn_lin_b': _L0_gnn_in['lin_b'], 'L0_gnn_gate_W': _L0_gnn_in['gate_W'], 'L0_gnn_gate_b': _L0_gnn_in['gate_b'], 'L0_gnn_bn_gamma': _L0_gnn_in['bn_gamma'], 'L0_gnn_bn_beta': _L0_gnn_in['bn_beta'], 'L0_ffn_gate_w': _L0_ffn_in['gate_w'], 'L0_ffn_gate_b': _L0_ffn_in['gate_b'], 'L0_ffn_w1': _L0_ffn_in['w1'], 'L0_ffn_b1': _L0_ffn_in['b1'], 'L0_ffn_w2': _L0_ffn_in['w2'], 'L0_ffn_b2': _L0_ffn_in['b2']}

def reference(x, src, dst, L0_gnn_gcn_W, L0_gnn_gcn_b, L0_gnn_lin_W, L0_gnn_lin_b, L0_gnn_gate_W, L0_gnn_gate_b, L0_gnn_bn_gamma, L0_gnn_bn_beta, L0_ffn_gate_w, L0_ffn_gate_b, L0_ffn_w1, L0_ffn_b1, L0_ffn_w2, L0_ffn_b2):
    import jax
    import jax.numpy as jnp

    def _L0_gnn_ref(x, edge_index, gcn_W, gcn_b, lin_W, lin_b, gate_W, gate_b, bn_gamma, bn_beta):
        import jax, jax.numpy as jnp
        import numpy as np
        N_NODES = 3125
        N_EDGES = 50000
        D_IN = 256
        D_HID = 256
        BN_EPS = 1e-05
        N = x.shape[0]
        loops = jnp.arange(N, dtype=edge_index.dtype)
        row = jnp.concatenate([edge_index[0], loops])
        col = jnp.concatenate([edge_index[1], loops])
        ones = jnp.ones(row.shape[0], dtype=x.dtype)
        deg = jax.ops.segment_sum(ones, col, num_segments=N)
        dinv = jnp.where(deg > 0, jax.lax.rsqrt(deg), 0.0)
        norm = dinv[row] * dinv[col]
        xw = x @ gcn_W
        msgs = xw[row] * norm[:, None]
        z = jax.ops.segment_sum(msgs, col, num_segments=N) + gcn_b
        z = jnp.tanh(z)
        g = jax.nn.sigmoid(z @ gate_W + gate_b)
        xl = x @ lin_W + lin_b
        h = jax.nn.relu((1.0 - g) * xl + g * z)
        mean = h.mean(axis=0)
        var = h.var(axis=0)
        h = (h - mean) * jax.lax.rsqrt(var + BN_EPS) * bn_gamma + bn_beta
        return h

    def _L0_ffn_ref(h, gate_w, gate_b, w1, b1, w2, b2):
        import math
        import jax, jax.numpy as jnp
        import numpy as np
        CAPACITY_FACTOR = 1.25
        B, L, D = h.shape
        E = gate_w.shape[1]
        T = B * L
        C = max(1, math.ceil(CAPACITY_FACTOR * T / E))
        x = h.reshape(T, D)
        logits = x @ gate_w + gate_b
        probs = jax.nn.softmax(logits, axis=-1)
        idx = jnp.argmax(probs, axis=-1)
        prb = jnp.take_along_axis(probs, idx[:, None], axis=1)[:, 0]
        one_hot = jax.nn.one_hot(idx, E, dtype=jnp.float32)
        pos = (jnp.cumsum(one_hot, axis=0) * one_hot).sum(-1).astype(jnp.int32) - 1
        kept = pos < C
        pos_safe = jnp.where(kept, pos, C)
        buf = jnp.zeros((E, C, D), dtype=h.dtype).at[idx, pos_safe].set(x, mode='drop')
        hmid = jax.nn.relu(jnp.einsum('ecd,edf->ecf', buf, w1) + b1[:, None, :])
        ybuf = jnp.einsum('ecf,efd->ecd', hmid, w2) + b2[:, None, :]
        pos_g = jnp.minimum(pos, C - 1)
        y_tok = ybuf[idx, pos_g] * (prb * kept)[:, None]
        y = y_tok.reshape(B, L, D)
        y = jnp.nan_to_num(y, nan=0.0, posinf=10000.0, neginf=-10000.0)
        return y
    edge_index = jnp.stack([src, dst])
    x = x + _L0_gnn_ref(_layernorm(x, axis=-1), edge_index, L0_gnn_gcn_W, L0_gnn_gcn_b, L0_gnn_lin_W, L0_gnn_lin_b, L0_gnn_gate_W, L0_gnn_gate_b, L0_gnn_bn_gamma, L0_gnn_bn_beta)
    x = x + _L0_ffn_ref(_layernorm(x, axis=-1)[None], L0_ffn_gate_w, L0_ffn_gate_b, L0_ffn_w1, L0_ffn_b1, L0_ffn_w2, L0_ffn_b2)[0]
    return x

_drawn_inputs = setup_inputs


def setup_inputs(seed=0):
    import zlib

    import numpy as np

    out = dict(_drawn_inputs(seed))
    spreads = {'L0_gnn_gcn_b': (0.0, 0.1),
     'L0_gnn_lin_b': (0.0, 0.1),
     'L0_gnn_gate_b': (0.0, 0.332),
     'L0_gnn_bn_gamma': (1.0, 0.2),
     'L0_gnn_bn_beta': (0.0, 0.1),
     'L0_ffn_gate_b': (0.0, 0.1),
     'L0_ffn_b1': (0.0, 0.8),
     'L0_ffn_b2': (0.0, 0.617)}
    factors = {}
    for name, (base, spread) in spreads.items():
        noise = np.random.default_rng([zlib.crc32(name.encode()), seed]).standard_normal(out[name].shape)
        drawn = base * np.exp(spread * noise) if base else spread * noise
        out[name] = jnp.asarray(drawn.astype(out[name].dtype))
    for name, factor in factors.items():
        out[name] = (out[name] * factor).astype(out[name].dtype)
    return out
```

```python
import concourse.bass as bass
from concourse import mybir
from contextlib import ExitStack

F32 = mybir.dt.float32
F16 = mybir.dt.float16
I32 = mybir.dt.int32
ALU = mybir.AluOpType
ACT = mybir.ActivationFunctionType
AX = mybir.AxisListType

P = 128
N_NODES, N_EDGES, D = 3125, 50000, 256
E, F, CAP = 8, 1024, 489
LN_EPS = BN_EPS = 1e-5
H = D // P
NT = -(-N_NODES // P)
TAIL = N_NODES - (NT - 1) * P
NPAD = NT * P
ROWS, RCOLS = 125, 400
LOOPC = N_NODES // ROWS
WN = 5
NW = N_NODES // WN
WB = NW // ROWS
SLOTS = P - WN
KEYS = NT * WN
NOKEY = 1000.0
GI = 24
GW = 4 * GI
GN = GW * WN
G = -(-NW // GW)
LASTI = 2 * -(-(NW - (G - 1) * GW) // 8)
LASTN = LASTI * 4 * WN
WPAD = (G - 1) * GW + LASTI * 4
XSC = 64.0
SROW = 512
CW = 2 * D + 2
NOROW = 1.0e6
POSINF = 1.0e4


def gnn_ffn(nc, x, src, dst, gcn_W, gcn_b, lin_W, lin_b, gate_W, gate_b, bn_gamma, bn_beta,
            fgate_w, fgate_b, w1, b1, w2, b2, out):
    xs_d = nc.dram_tensor("xs_table", (NPAD, 2 * D), F16, kind="Internal").ap()
    buf_d = nc.dram_tensor("dispatch", (E * SROW, CW), F32, kind="Internal").ap()
    src_flat = src.rearrange("(n o) -> n o", o=1)
    dst_flat = dst.rearrange("(n o) -> n o", o=1)
    ctx = ExitStack()
    with ctx:
        def sb(name, shape, dt):
            return ctx.enter_context(nc.sbuf_tensor(name, shape, dt))

        def sem(name):
            return ctx.enter_context(nc.semaphore(name))

        XX = sb("XX", [P, NT * CW], F32)
        xn = XX[:, 0:NT * D].rearrange("p (a d) -> p a d", d=D)
        xs = XX[:, NT * D:2 * NT * D].bitcast(F16).rearrange("p (a d) -> p a d", d=2 * D)
        comb = XX[:, :].rearrange("p (a c) -> p a c", c=CW)
        XL = sb("XL", [P, H, NPAD], F32)
        DB = sb("DB", [P, NPAD], F32)
        R = sb("R", [P, 51200], F16)

        def at(byte, n, dt):
            size = 2 if dt == F16 else 4
            v = R[:, byte // 2:(byte + n * size) // 2]
            return v if dt == F16 else v.bitcast(dt)

        oh_lo = at(0, P * RCOLS, F16).rearrange("p (v c) -> p v c", c=RCOLS)
        oh_hi = XX[:, NT * D:NT * D + NT * RCOLS // 2].bitcast(F16).rearrange("p (v c) -> p v c", c=RCOLS)
        A = [at(24000 * k, NT * GN, F16).rearrange("p (a n) -> p a n", n=GN) for k in range(2)]
        degB = at(48000, NPAD, F32)
        aggT = [at(60800 + 3840 * k, H * GN, F32).rearrange("p (h n) -> p h n", n=GN) for k in range(2)]
        zT = [at(68480 + 3840 * k, H * GN, F32).rearrange("p (h n) -> p h n", n=GN) for k in range(2)]
        gT = at(76160, H * GN, F32).rearrange("p (h n) -> p h n", n=GN)
        mT = at(80000, H * GN, F32).rearrange("p (h n) -> p h n", n=GN)
        keyw = [at(76160 + 2560 * k, WB * P, F32).rearrange("p (j s) -> p j s", s=P) for k in range(6)]
        diag = at(91520, 4 * P, F32).rearrange("p (q n) -> p q n", n=P)
        ohb = at(93568, 8 * P, F16).rearrange("p (w n) -> p w n", n=P)
        ohk = at(95616, 8 * KEYS, F16).rearrange("p (w n) -> p w n", n=KEYS)
        lnT = at(97664, H * 512, F32).rearrange("p (h n) -> p h n", n=512)
        edges_s = at(24000, WB * SLOTS, I32).rearrange("p (j s) -> p j s", s=SLOTS)
        edges_d = at(26464, WB * SLOTS, I32).rearrange("p (j s) -> p j s", s=SLOTS)
        gath = at(0, 2 * D, F16)
        dsel = at(1024, GN, F16)
        io480 = at(2048, GN, F16)
        w1s = [at(8192 * k, H * F, F32).rearrange("p (h f) -> p h f", f=F) for k in range(2)]
        w2s = [at(16384 + 8192 * k, 8 * D, F32).rearrange("p (f d) -> p f d", d=D) for k in range(2)]
        hid = [at(32768 + 15648 * k, 8 * CAP, F32).rearrange("p (f s) -> p f s", s=CAP) for k in range(2)]
        xb = [at(64064 + 8224 * k, 4 * CW, F32).rearrange("p (j c) -> p j c", c=CW) for k in range(2)]
        xbT = [at(80512 + 4096 * k, H * 512, F32).rearrange("p (h s) -> p h s", s=512) for k in range(2)]
        yt = [at(88704 + 4096 * k, 4 * D, F32).rearrange("p (j d) -> p j d", d=D) for k in range(2)]
        xnT = [at(48416 + 4096 * k, H * 512, F32).rearrange("p (h s) -> p h s", s=512) for k in range(2)]
        b2B = DB[:, 0:E * D].rearrange("p (e d) -> p e d", d=D)
        tmp_y = DB[:, E * D:E * D + D]
        tmp_m = DB[:, E * D + D:E * D + 2 * D]
        zero_y = DB[:, E * D + 2 * D:E * D + 3 * D]

        gcnW = sb("gcnW", [P, H, D], F32)
        linW = sb("linW", [P, H, D], F32)
        gateW = sb("gateW", [P, H, D], F32)
        ident = sb("ident", [P, P], F32)
        ones = sb("ones", [P, P], F32)
        onesH = sb("onesH", [P, P], F16)
        triH = sb("triH", [P, P], F16)
        iotaH = sb("iotaH", [P, P], F16)
        iotaI = R[:, 0:2 * P].bitcast(I32)
        srcI = sb("srcI", [ROWS, RCOLS + LOOPC], I32)
        dstI = sb("dstI", [ROWS, RCOLS + LOOPC], I32)
        lo16 = XL[0:ROWS, 0, 800:1000].bitcast(F16)
        hi16 = XL[0:ROWS, 0, 1000:1200].bitcast(F16)
        tmpI = XL[0:ROWS, 0, 0:RCOLS].bitcast(I32)
        tmpI2 = XL[0:ROWS, 0, RCOLS:2 * RCOLS].bitcast(I32)
        VR = sb("VR", [E * F // P + 10, P], F32)
        VT = sb("VT", [P, E * F // P + 10], F32)
        fgw = sb("fgw", [P, H, E], F32)
        fgb = sb("fgb", [P, E], F32)
        keyT = sb("keyT", [P, WPAD], F32)
        lowT = sb("lowT", [P, WPAD], F32)
        stats = sb("stats", [P, NT, 6], F32)
        mv = sb("mv", [P, NT, 2], F32)
        rs = sb("rs", [P, 4, NT], F32)
        dinvx = sb("dinvx", [P, 2, NT], F32)
        degR = sb("degR", [P, NT], F32)
        wI = sb("wI", [ROWS, WB], I32)
        wIdx = sb("wIdx", [ROWS, WB], I32)
        selfI = sb("selfI", [ROWS, 3, WB * WN], I32)
        cs = XL[:, 1, 0:NW + 1]
        wF = sb("wF", [ROWS, 2, WB], F32)
        fb = sb("fb", [P, 4], F32)
        flagF = sb("flagF", [1, 1], F32)
        flagI = sb("flagI", [1, 1], I32)
        idxc = sb("idxc", [ROWS, 1], I32)
        dcol = sb("dcol", [ROWS, 1], F32)
        bnst = sb("bnst", [P, H, G, 6], F32)
        bnmv = sb("bnmv", [P, H, 2], F32)
        bnc = sb("bnc", [P, 6, H], F32)
        nodeI = sb("nodeI", [P, NT], I32)
        slotI = sb("slotI", [P, NT], I32)
        iota8 = sb("iota8", [P, E], F32)
        tokI = [sb(f"tokI{k}", [P, 4], I32) for k in range(2)]
        def rt(k):
            return XL[:, 0, 200 * k:200 * k + NT * E].rearrange("p (a e) -> p a e", e=E)
        def rc(k):
            return XL[:, 1, NT * k:NT * (k + 1)]
        ohH = XL[:, 1, 1000:1100].bitcast(F16).rearrange("p (a e) -> p a e", e=E)
        fill = XL[:, 1, 2000:2000 + CW]

        PS = [ctx.enter_context(nc.psum_tensor(f"PS{k}", [P, 512], F32)) for k in range(8)]

        s_dst, s_src, s_x, s_w, s_vec, s_fg, s_x2, s_b2 = [sem(n) for n in (
            "dst_loaded", "src_loaded", "x_loaded", "weights_loaded", "vectors_loaded", "router_loaded",
            "x_reloaded", "b2_loaded")]
        s_const = sem("consts_ready")
        s_iota = sem("iota_ready")
        s_iota_f = sem("iota_cast")
        s_split = sem("dst_split")
        s_ohlo, s_ohhi = sem("onehot_low_ready"), sem("onehot_high_ready")
        s_hist = sem("histogram_done")
        s_diag, s_bc, s_bcc = sem("diag_ready"), sem("broadcast_done"), sem("broadcast_copied")
        s_sq, s_sqi = sem("sqrt_done"), sem("sqrt_input_ready")
        s_start, s_gs, s_gd = sem("window_starts_ready"), sem("sources_gathered"), sem("dests_gathered")
        s_key, s_keyp, s_keyc = sem("keys_ready"), sem("keys_transposed"), sem("keys_copied")
        s_cnt, s_flag = sem("matched_counted"), sem("flag_ready")
        s_ln, s_lnt, s_lnc, s_lin, s_linc = (sem("ln_ready"), sem("ln_transposed"), sem("ln_copied"),
                                             sem("lin_done"), sem("lin_copied"))
        s_dx, s_hi, s_lo = sem("source_scale_ready"), sem("source_high_ready"), sem("source_low_ready")
        s_vT, s_vTc = sem("vectors_transposed"), sem("vectors_copied")
        s_oh, s_bld, s_ev = sem("window_onehots_ready"), sem("windows_built"), sem("adjacency_copied")
        s_agg, s_aggc = sem("aggregated"), sem("aggregate_scaled")
        s_gcn, s_z, s_gate, s_g = sem("gcn_done"), sem("z_ready"), sem("gate_done"), sem("g_ready")
        s_diff, s_h = sem("mix_difference_ready"), sem("h_ready")
        s_tab, s_gidx, s_grow, s_sel, s_gmm, s_io480 = (sem("table_stored"), sem("gather_index_ready"),
                sem("rows_gathered"), sem("selector_ready"), sem("general_step_done"), sem("iota480_ready"))
        s_dcol = sem("dest_column_ready")
        s_ptick = sem("pool_tick")
        s_loops = sem("loops_ready")
        s_bn, s_yT, s_x1 = sem("bn_applied"), sem("y_transposed"), sem("x1_ready")
        s_xn2, s_xnp, s_xnc, s_log = sem("ln2_ready"), sem("ln2_transposed"), sem("ln2_copied"), sem("logits_done")
        s_expi, s_exp, s_ohr, s_pos, s_posc = (sem("exp_input_ready"), sem("exp_done"), sem("route_ready"),
                                              sem("positions_done"), sem("totals_copied"))
        s_fillr, s_filled, s_slot, s_disp = sem("fill_ready"), sem("buffer_filled"), sem("slots_ready"), sem("dispatched")
        s_out0, s_outs = sem("residual_stored"), [sem(f"rows_stored{k}") for k in range(2)]
        s_wl = [sem(f"expert_weights{k}") for k in range(2)]
        s_wfree = [sem(f"expert_weights_used{k}") for k in range(2)]
        s_xb = [sem(f"expert_rows{k}") for k in range(2)]
        s_xbfree = [sem(f"expert_rows_used{k}") for k in range(2)]
        s_xbp, s_xbc0, s_xbc1 = sem("rows_transposed"), sem("rows_copied_low"), sem("rows_copied_high")
        s_up, s_hid, s_down, s_y = sem("up_done"), sem("hidden_ready"), sem("down_done"), sem("y_ready")
        s_fix = sem("y_step")
        dch, pch, ach = sem("vector_chain"), sem("pool_chain"), sem("scalar_chain")

        block = ctx.enter_context(nc.Block())

        def bcast_src(v, shape):
            return v.to_broadcast(shape)

        @block.sync
        def _(sp):
            sp.dma_start(dstI[:, 0:RCOLS], dst.rearrange("(r c) -> r c", c=RCOLS)).then_inc(s_dst, 16)
            full = (NT - 1) * P
            sp.wait_ge(s_const, 1)
            sp.dma_start(xn[:, 0:NT - 1, :], x[0:full, :].rearrange("(a p) d -> p a d", p=P)).then_inc(s_x, 16)
            sp.dma_start(xn[0:TAIL, NT - 1, :], x[full:N_NODES, :]).then_inc(s_x, 16)
            sp.dma_start(srcI[:, 0:RCOLS], src.rearrange("(r c) -> r c", c=RCOLS)).then_inc(s_src, 16)
            for w_sb, w in ((linW, lin_W), (gcnW, gcn_W), (gateW, gate_W)):
                sp.dma_start(w_sb[:, :, :], w.rearrange("(h p) n -> p h n", p=P)).then_inc(s_w, 16)
            nb = E * F // P
            sp.dma_start(VR[0:nb, :], b1.rearrange("e (f p) -> (e f) p", p=P)).then_inc(s_vec, 16)
            for k, v in enumerate((gcn_b, lin_b, gate_b, bn_gamma, bn_beta)):
                sp.dma_start(VR[nb + 2 * k:nb + 2 * k + 2, :], v.rearrange("(h p) -> h p", p=P)).then_inc(s_vec, 16)
            sp.dma_start(fgw[:, :, :], fgate_w.rearrange("(h p) e -> p h e", p=P)).then_inc(s_fg, 16)
            sp.dma_start(fgb[:, :], fgate_b.rearrange("(o e) -> o e", o=1).to_broadcast([P, E])).then_inc(s_fg, 16)
            sp.wait_ge(s_agg, G)
            sp.wait_ge(s_const, 3)
            sp.dma_start(comb[:, 0:NT - 1, D:2 * D], x[0:full, :].rearrange("(a p) d -> p a d", p=P)).then_inc(s_x2, 16)
            sp.dma_start(comb[0:TAIL, NT - 1, D:2 * D], x[full:N_NODES, :]).then_inc(s_x2, 16)
            sp.wait_ge(s_aggc, G)
            sp.dma_start(DB[:, 0:E * D], b2.rearrange("(o e) d -> o (e d)", o=1).to_broadcast([P, E * D])).then_inc(s_b2, 16)
            sp.wait_ge(s_fillr, 1)
            sp.dma_start(buf_d.rearrange("(j p) c -> p j c", p=P),
                         fill.rearrange("p (o c) -> p o c", o=1).to_broadcast([P, E * SROW // P, CW])).then_inc(s_filled, 16)
            sp.wait_ge(s_x1, NT)
            sp.dma_start(out[0:full, :].rearrange("(a p) d -> p a d", p=P), comb[:, 0:NT - 1, D:2 * D]).then_inc(s_out0, 16)
            sp.dma_start(out[full:N_NODES, :], comb[0:TAIL, NT - 1, D:2 * D]).then_inc(s_out0, 16)
            w1_v = w1.rearrange("e (h p) f -> e p h f", p=P)
            w2_v = w2.rearrange("e (f p) d -> e p f d", p=P)
            buf_v = buf_d.rearrange("(e j p) c -> e p j c", p=P, j=4)
            sp.wait_ge(s_h, H * G)
            for e in range(E):
                u = e % 2
                if e >= 2:
                    sp.wait_ge(s_wfree[u], e // 2)
                sp.dma_start(w1s[u], w1_v[e]).then_inc(s_wl[u], 16)
                sp.dma_start(w2s[u], w2_v[e]).then_inc(s_wl[u], 16)
                if e == 0:
                    sp.wait_ge(s_disp, 16 * NT)
                if e >= 2:
                    sp.wait_ge(s_xbfree[u], e // 2)
                sp.dma_start(xb[u], buf_v[e]).then_inc(s_xb[u], 16)
            sp.wait_ge(s_out0, 32)
            sp.wait_ge(s_src, 16)

        @block.gpsimd
        def _(pool):
            g = nc.gpsimd
            n = [0]

            def step(ins):
                n[0] += 1
                ins.then_inc(pch, 1)

            def settle():
                pool.wait_ge(pch, n[0])

            g.memset(xn[:, NT - 1, :], 0.0).then_inc(s_const, 1)
            g.iota(iotaI, [[1, P]], base=0, channel_multiplier=0).then_inc(s_iota, 1)
            step(g.memset(ident[:, :], 0.0))
            step(g.memset(triH[:, :], 1.0))
            step(g.memset(ones[:, :], 1.0))
            step(g.memset(onesH[:, :], 1.0))
            step(g.iota(srcI[:, RCOLS:], [[ROWS, LOOPC]], base=0, channel_multiplier=1))
            step(g.iota(dstI[:, RCOLS:], [[ROWS, LOOPC]], base=0, channel_multiplier=1))
            step(g.iota(nodeI[:, :], [[P, NT]], base=0, channel_multiplier=1))
            step(g.iota(selfI[:, 0, :].rearrange("p (j r) -> p j r", r=WN), [[WN * ROWS, WB], [1, WN]], base=0,
                        channel_multiplier=WN))
            step(g.iota(wI[:, :], [[WN * ROWS, WB]], base=0, channel_multiplier=WN))
            step(g.memset(keyT[:, NW:WPAD], NOKEY))
            step(g.memset(lowT[:, NW:WPAD], NOKEY))
            settle()
            step(g.affine_select(out=ident[:, :], in_=ident[:, :], compare_op=ALU.not_equal, fill=1.0, base=0,
                                 pattern=[[-1, P]], channel_multiplier=1))
            step(g.affine_select(out=triH[:, :], in_=triH[:, :], compare_op=ALU.is_ge, fill=0.0, base=0,
                                 pattern=[[1, P]], channel_multiplier=-1))
            settle()
            g.memset(fb[:, 0:1], 1.0).then_inc(s_const, 1)
            pool.wait_ge(s_split, 2)
            for v in range(HI_POOL):
                ins = g.tensor_scalar(oh_hi[0:ROWS, v, :], hi16, float(v), None, ALU.is_equal)
                step(ins)
            settle()
            g.memset(fb[:, 1:2], 1.0).then_inc(s_ohhi, 1)
            pool.wait_ge(s_start, 1)
            for j in range(WB):
                g.indirect_dma_start(out=edges_s[0:ROWS, j, :], out_offset=None, in_=src_flat[:, 0:1],
                                     in_offset=bass.IndirectOffsetOnAxis(ap=wIdx[:, j:j + 1], axis=0),
                                     bounds_check=N_EDGES - 1, oob_is_err=False).then_inc(s_gs, 16)
                g.indirect_dma_start(out=edges_d[0:ROWS, j, :], out_offset=None, in_=dst_flat[:, 0:1],
                                     in_offset=bass.IndirectOffsetOnAxis(ap=wIdx[:, j:j + 1], axis=0),
                                     bounds_check=N_EDGES - 1, oob_is_err=False).then_inc(s_gd, 16)
            pool.wait_ge(s_flag, 1)
            fast = pool.value_load(flagI[0:1, 0:1], min_val=0, max_val=1)
            for gr in range(G + 2):
                if gr < G:
                    with pool.If(fast == 1):
                        pool.nop()
                    with pool.Else():
                        if gr == 0:
                            g.iota(io480, [[1, GN]], base=0, channel_multiplier=0,
                                   allow_small_or_imprecise_dtypes=True).then_inc(s_io480, 1)
                            pool.wait_ge(s_lo, 1)
                            pool.wait_ge(s_src, 16)
                            g.dma_start(xs_d.rearrange("(a p) d -> p a d", p=P), xs).then_inc(s_tab, 16)
                            pool.wait_ge(s_tab, 16)
                        NC = RCOLS + LOOPC
                        with pool.Fori(0, NC) as c:
                            pool.wait_ge(s_gmm, c + gr * NC)
                            pool.sem_inc(s_ptick, 1)
                            g.tensor_copy(idxc[:, :], srcI[:, bass.ds(c, 1)]).then_inc(s_gidx, 1)
                            pool.wait_ge(s_gidx, c + (gr * NC + 1))
                            pool.sem_inc(s_ptick, 1)
                            g.indirect_dma_start(out=gath[0:ROWS, :], out_offset=None, in_=xs_d,
                                                 in_offset=bass.IndirectOffsetOnAxis(ap=idxc[:, 0:1], axis=0),
                                                 bounds_check=NPAD - 1, oob_is_err=False).then_inc(s_grow, 16)
                q = gr - 1
                if 0 <= q < G:
                    nn = GN if q < G - 1 else LASTN
                    pool.wait_ge(s_z, H * (q + 1))
                    if q >= 1:
                        pool.wait_ge(s_h, H * q)
                    for h in range(H):
                        g.tensor_tensor(mT[:, h, 0:nn], zT[q % 2][:, h, 0:nn],
                                        XL[:, h, GN * q:GN * q + nn], ALU.subtract).then_inc(s_diff, 1)
            pool.wait_ge(s_agg, G)
            g.memset(comb[:, NT - 1, D:2 * D], 0.0).then_inc(s_const, 1)
            pool.wait_ge(s_slot, 1)
            pool.wait_ge(s_filled, 16)
            for a in range(NT):
                g.indirect_dma_start(out=buf_d, out_offset=bass.IndirectOffsetOnAxis(ap=slotI[:, a:a + 1], axis=0),
                                     in_=comb[:, a, :], in_offset=None,
                                     bounds_check=E * SROW - 1, oob_is_err=False).then_inc(s_disp, 16)
            pool.wait_ge(s_out0, 32)
            for e in range(E):
                u = e % 2
                for j in range(4):
                    pool.wait_ge(s_y, 4 * e + j + 1)
                    g.indirect_dma_start(out=out, out_offset=bass.IndirectOffsetOnAxis(ap=tokI[u][:, j:j + 1], axis=0),
                                         in_=yt[u][:, j, :], in_offset=None,
                                         bounds_check=N_NODES - 1, oob_is_err=False).then_inc(s_outs[u], 16)
            for u in range(2):
                pool.wait_ge(s_outs[u], 16 * 4 * E // 2)

        @block.vector
        def _(dve):
            v = nc.vector
            n = [0]

            def step(ins):
                n[0] += 1
                ins.then_inc(dch, 1)

            def settle():
                dve.wait_ge(dch, n[0])

            def link(ins):
                step(ins)
                settle()

            dve.wait_ge(s_iota, 1)
            link(v.tensor_copy(iotaH[:, :], iotaI))
            dve.wait_ge(s_dst, 16)
            step(v.tensor_single_scalar(tmpI, dstI[:, 0:RCOLS], P - 1, ALU.bitwise_and))
            step(v.tensor_single_scalar(tmpI2, dstI[:, 0:RCOLS], 7, ALU.arith_shift_right))
            settle()
            v.tensor_copy(hi16, tmpI2).then_inc(s_split, 1)
            v.tensor_copy(lo16, tmpI).then_inc(s_split, 1)
            dve.wait_ge(s_split, 2)
            for k in range(P):
                step(v.tensor_scalar(oh_lo[0:ROWS, k, :], lo16, float(k), None, ALU.is_equal))
            for k in range(HI_POOL, NT):
                step(v.tensor_scalar(oh_hi[0:ROWS, k, :], hi16, float(k), None, ALU.is_equal))
            settle()
            v.memset(fb[:, 2:3], 1.0).then_inc(s_ohlo, 1)

            def rsqrt(width, mark):
                val, sq, r, t = [rs[:, k, 0:width] for k in range(4)]
                settle()
                v.memset(fb[:, 3:4], 0.0).then_inc(s_sqi, 1)
                dve.wait_ge(s_sq, mark)
                link(v.reciprocal(r, sq))
                link(v.tensor_tensor(t, r, r, ALU.mult))
                link(v.tensor_tensor(t, t, val, ALU.mult))
                link(v.tensor_scalar(t, t, -0.5, 1.5, ALU.mult, ALU.add))
                link(v.tensor_tensor(r, r, t, ALU.mult))
                return r

            dve.wait_ge(s_x, 32)
            for a in range(NT):
                step(v.bn_stats(stats[:, a, :], xn[:, a, :]))
            settle()
            for a in range(NT):
                step(v.bn_aggr(mv[:, a, :], stats[:, a, :]))
            settle()
            link(v.tensor_scalar(rs[:, 0, :], mv[:, :, 1], LN_EPS, None, ALU.add))
            r = rsqrt(NT, 1)
            for a in range(NT):
                step(v.tensor_scalar(xn[:, a, :], xn[:, a, :], mv[:, a, 0:1], r[:, a:a + 1], ALU.subtract, ALU.mult))
            settle()
            v.memset(fb[:, 3:4], 0.0).then_inc(s_ln, 1)

            dve.wait_ge(s_const, 2)
            dve.wait_ge(s_hist, 1)
            link(v.tensor_copy(degR[:, :], PS[0][:, 0:NT]))

            def spread(vec, done):
                for q in range(7):
                    m = min(4, NT - 4 * q)
                    if done + q >= 1:
                        dve.wait_ge(s_bc, done + q)
                    v.tensor_tensor(diag[:, 0:m, :], ident[:, :].unsqueeze(1).to_broadcast([P, m, P]),
                                    vec[:, 4 * q:4 * q + m].unsqueeze(2).to_broadcast([P, m, P]),
                                    ALU.mult).then_inc(s_diag, 1)

            spread(degR, 0)
            link(v.tensor_scalar(rs[:, 0, :], degR[:, :], 1.0, None, ALU.add))
            r = rsqrt(NT, 2)
            link(v.tensor_scalar(dinvx[:, 0, :], r, XSC, None, ALU.mult))
            link(v.tensor_scalar(dinvx[:, 1, :], r, 1.0 / XSC, None, ALU.mult))
            v.memset(fb[:, 3:4], 0.0).then_inc(s_dx, 1)
            dve.wait_ge(s_bcc, 7)
            step(v.memset(cs[:, 0:1], 0.0))
            link(v.tensor_reduce(cs[:, 1:NW + 1], degB[:, 0:N_NODES].rearrange("p (w r) -> p w r", r=WN),
                                 AX.X, ALU.add))
            link(v.tensor_tensor_scan(degB[:, 0:NW], cs[:, 0:NW], cs[:, 0:NW], 0.0, ALU.add, ALU.max))
            pick = XL[0:ROWS, 1, 700:700 + NW].rearrange("p (j w) -> p j w", w=ROWS)
            link(v.tensor_tensor(pick, degB[0:ROWS, 0:NW].rearrange("p (j w) -> p j w", w=ROWS),
                                 ident[0:ROWS, 0:ROWS].unsqueeze(1).to_broadcast([ROWS, WB, ROWS]), ALU.mult))
            link(v.tensor_reduce(wF[:, 0, :], pick, AX.X, ALU.add))
            link(v.tensor_scalar(wF[:, 0, :], wF[:, 0, :], float(N_EDGES - SLOTS), None, ALU.min))
            v.tensor_copy(wIdx[:, :], wF[:, 0, :]).then_inc(s_start, 1)
            spread(dinvx[:, 1, :], 7)
            so = WB * WN
            step(v.tensor_single_scalar(selfI[:, 1, :], selfI[:, 0, :], P - 1, ALU.bitwise_and))
            step(v.tensor_single_scalar(selfI[:, 2, :], selfI[:, 0, :], 7, ALU.arith_shift_right))
            settle()
            low, high, dl, t0, valid, key = keyw
            self3 = lambda k: selfI[:, k, :].rearrange("p (j r) -> p j r", r=WN)
            step(v.tensor_copy(low[0:ROWS, :, SLOTS:P], self3(1)))
            step(v.tensor_copy(high[0:ROWS, :, SLOTS:P], self3(2)))
            step(v.tensor_copy(wF[:, 1, :], wI[:, :]))
            settle()
            first = wF[:, 1, :].unsqueeze(2)
            step(v.tensor_tensor(dl[0:ROWS, :, SLOTS:P], self3(0), first.to_broadcast([ROWS, WB, WN]), ALU.subtract))
            settle()
            step(v.scalar_tensor_tensor(key[0:ROWS, :, SLOTS:P], high[0:ROWS, :, SLOTS:P], float(WN),
                                        dl[0:ROWS, :, SLOTS:P], ALU.mult, ALU.add))
            for a in range(NT):
                dve.wait_ge(s_hi, a + 1)
                step(v.scalar_tensor_tensor(xs[:, a, D:2 * D], xn[:, a, :], dinvx[:, 0, a:a + 1],
                                            xs[:, a, 0:D], ALU.mult, ALU.subtract))
            settle()
            v.memset(fb[:, 3:4], 0.0).then_inc(s_lo, 1)
            S = slice(0, SLOTS)
            dve.wait_ge(s_gs, 16 * WB)
            dve.wait_ge(s_gd, 16 * WB)
            eI = [XL[0:ROWS, 1, 700 + 615 * k:700 + 615 * (k + 1)].bitcast(I32).rearrange("p (j s) -> p j s", s=SLOTS)
                  for k in range(2)]
            es, ed = edges_s[0:ROWS], edges_d[0:ROWS]
            step(v.tensor_single_scalar(eI[0], es, P - 1, ALU.bitwise_and))
            step(v.tensor_single_scalar(eI[1], es, 7, ALU.arith_shift_right))
            step(v.tensor_tensor(dl[0:ROWS, :, S], ed, first.to_broadcast([ROWS, WB, SLOTS]), ALU.subtract))
            settle()
            step(v.tensor_copy(low[0:ROWS, :, S], eI[0]))
            step(v.tensor_copy(high[0:ROWS, :, S], eI[1]))
            step(v.tensor_scalar(t0[0:ROWS, :, S], dl[0:ROWS, :, S], 0.0, None, ALU.is_ge))
            settle()
            step(v.scalar_tensor_tensor(valid[0:ROWS, :, S], dl[0:ROWS, :, S], float(WN), t0[0:ROWS, :, S],
                                        ALU.is_lt, ALU.mult))
            step(v.scalar_tensor_tensor(key[0:ROWS, :, S], high[0:ROWS, :, S], float(WN), dl[0:ROWS, :, S],
                                        ALU.mult, ALU.add))
            settle()
            step(v.scalar_tensor_tensor(key[0:ROWS, :, S], key[0:ROWS, :, S], -NOKEY, valid[0:ROWS, :, S],
                                        ALU.add, ALU.mult))
            link(v.tensor_reduce(fb[0:ROWS, 0:1], valid[0:ROWS, :, S], AX.XY, ALU.add))
            link(v.tensor_scalar(key[0:ROWS, :, S], key[0:ROWS, :, S], NOKEY, None, ALU.add))
            v.memset(fb[:, 3:4], 0.0).then_inc(s_key, 1)
            dve.wait_ge(s_cnt, 1)
            link(v.tensor_scalar(flagF[:, :], PS[7][0:1, 0:1], float(N_EDGES), None, ALU.is_equal))
            v.tensor_copy(flagI[:, :], flagF[:, :]).then_inc(s_flag, 1)
            dve.wait_ge(s_flag, 1)
            fast = dve.value_load(flagI[0:1, 0:1], min_val=0, max_val=1)
            dve.wait_ge(s_keyc, 4)

            def onehots(i, w, u):
                for q in range(4):
                    v.tensor_scalar(ohb[:, 4 * u + q, :], iotaH[:, :], lowT[:, bass.ds(w + q, 1)], None, ALU.is_equal)
                    ins = v.tensor_scalar(ohk[:, 4 * u + q, :], iotaH[:, 0:KEYS], keyT[:, bass.ds(w + q, 1)], None,
                                          ALU.is_equal)
                ins.then_inc(s_oh, 1)

            def onehot_group(gr):
                pairs = (GI if gr < G - 1 else LASTI) // 2
                lo = 0
                if gr == 0:
                    for u in range(2):
                        onehots(u, 4 * u, u)
                    lo = 1
                with dve.Fori(lo, pairs) as m:
                    for u in range(2):
                        dve.wait_ge(s_bld, 2 * m + (GI * gr + u - 1))
                        onehots(None, 8 * m + (4 * GI * gr + 4 * u), u)

            for gr in range(-1, G + 2):
                if gr + 1 < G:
                    with dve.If(fast == 1):
                        onehot_group(gr + 1)
                    with dve.Else():
                        dve.nop()
                if 0 <= gr < G:
                    with dve.If(fast == 1):
                        dve.nop()
                    with dve.Else():
                        if gr == 0:
                            dve.wait_ge(s_io480, 1)
                        NC = RCOLS + LOOPC
                        with dve.Fori(0, NC) as c:
                            dve.wait_ge(s_gmm, c + gr * NC)
                            v.tensor_scalar(dcol[:, :], dstI[:, bass.ds(c, 1)], float(-GN * gr), None,
                                            ALU.add).then_inc(s_dcol, 1)
                            dve.wait_ge(s_dcol, c + (gr * NC + 1))
                            v.tensor_scalar(dsel[0:ROWS, :], io480[0:ROWS, :], dcol[:, 0:1], None,
                                            ALU.is_equal).then_inc(s_sel, 1)
                q = gr - 2
                if 0 <= q < G:
                    nn = GN if q < G - 1 else LASTN
                    nv = min(GN, N_NODES - GN * q)
                    for h in range(H):
                        dve.wait_ge(s_g, H * q + h + 1)
                        dve.wait_ge(s_diff, H * q + h + 1)
                        hx = XL[:, h, GN * q:GN * q + nn]
                        link(v.tensor_tensor(mT[:, h, 0:nn], mT[:, h, 0:nn], gT[:, h, 0:nn], ALU.mult))
                        link(v.tensor_tensor(mT[:, h, 0:nn], mT[:, h, 0:nn], hx, ALU.add))
                        v.tensor_scalar(hx, mT[:, h, 0:nn], 0.0, None, ALU.max).then_inc(s_h, 1)
                        dve.wait_ge(s_h, H * q + h + 1)
                        step(v.bn_stats(bnst[:, h, q, :], XL[:, h, GN * q:GN * q + nv]))
                if 0 <= gr < G:
                    nn = GN if gr < G - 1 else LASTN
                    dve.wait_ge(s_agg, gr + 1)
                    if gr >= 2:
                        dve.wait_ge(s_gcn, gr - 1)
                    for h in range(H):
                        ins = v.tensor_tensor(aggT[gr % 2][:, h, 0:nn], PS[2 + 2 * (gr % 2) + h][:, 0:nn],
                                              DB[:, GN * gr:GN * gr + nn], ALU.mult)
                        if h == 0:
                            step(ins)
                    ins.then_inc(s_aggc, 1)
            settle()
            for h in range(H):
                step(v.bn_aggr(bnmv[:, h, :], bnst[:, h, :, :].rearrange("p g s -> p (g s)")))
            settle()
            link(v.tensor_scalar(rs[:, 0, 0:H], bnmv[:, :, 1], BN_EPS, None, ALU.add))
            r = rsqrt(H, 3)
            nb = E * F // P
            gamma, beta = VT[:, nb + 6:nb + 8], VT[:, nb + 8:nb + 10]
            link(v.tensor_tensor(bnc[:, 0, :], r, gamma, ALU.mult))
            link(v.tensor_tensor(bnc[:, 1, :], bnmv[:, :, 0], bnc[:, 0, :], ALU.mult))
            link(v.tensor_tensor(bnc[:, 2, :], beta, bnc[:, 1, :], ALU.subtract))
            for h in range(H):
                step(v.tensor_scalar(XL[:, h, :], XL[:, h, :], bnc[:, 0, h:h + 1], bnc[:, 2, h:h + 1],
                                     ALU.mult, ALU.add))
            settle()
            v.memset(fb[:, 3:4], 0.0).then_inc(s_bn, 1)
            dve.wait_ge(s_x2, 32)
            for a in range(NT):
                x1 = comb[:, a, D:2 * D]
                dve.wait_ge(s_yT, a + 1)
                v.tensor_tensor(x1, PS[a % 4][:, 0:D], x1, ALU.add).then_inc(s_x1, 1)
                dve.wait_ge(s_x1, a + 1)
                step(v.bn_stats(stats[:, a, :], x1))
            settle()
            for a in range(NT):
                step(v.bn_aggr(mv[:, a, :], stats[:, a, :]))
            settle()
            link(v.tensor_scalar(rs[:, 0, :], mv[:, :, 1], LN_EPS, None, ALU.add))
            r = rsqrt(NT, 4)
            for a in range(NT):
                v.tensor_scalar(comb[:, a, 0:D], comb[:, a, D:2 * D], mv[:, a, 0:1], r[:, a:a + 1],
                                ALU.subtract, ALU.mult).then_inc(s_xn2, 1)
            step(v.memset(fill[:, 0:CW - 1], 0.0))
            step(v.memset(fill[:, CW - 1:CW], NOROW))
            step(v.tensor_copy(rc(0), nodeI[:, :]))
            step(v.tensor_copy(iota8[:, :], iotaH[:, 0:E]))
            settle()
            v.memset(fb[:, 3:4], 0.0).then_inc(s_fillr, 1)
            node, live = rc(0), rc(1)
            link(v.tensor_scalar(live, node, float(N_NODES), None, ALU.is_lt))

            def over(vec):
                return vec.unsqueeze(2).to_broadcast([P, NT, E])

            L, ex, pr, eq = rt(0), rt(1), rt(2), rt(3)
            iota_b = iota8[:, :].unsqueeze(1).to_broadcast([P, NT, E])
            dve.wait_ge(s_fg, 32)
            dve.wait_ge(s_log, 1)
            link(v.tensor_tensor(L, PS[4][:, 0:NT * E].rearrange("p (a e) -> p a e", e=E),
                                 fgb[:, :].unsqueeze(1).to_broadcast([P, NT, E]), ALU.add))
            link(v.tensor_reduce(rc(2), L, AX.X, ALU.max))
            v.tensor_tensor(L, L, over(rc(2)), ALU.subtract).then_inc(s_expi, 1)
            dve.wait_ge(s_exp, 1)
            link(v.tensor_reduce(rc(3), ex, AX.X, ALU.add))
            link(v.reciprocal(rc(3), rc(3)))
            link(v.tensor_tensor(pr, ex, over(rc(3)), ALU.mult))
            link(v.tensor_reduce(rc(4), pr, AX.X, ALU.max))
            link(v.tensor_tensor(eq, pr, over(rc(4)), ALU.is_equal))
            link(v.scalar_tensor_tensor(eq, eq, -float(E), iota_b, ALU.mult, ALU.add))
            link(v.tensor_reduce(rc(5), eq, AX.X, ALU.min))
            link(v.tensor_scalar(rc(5), rc(5), float(E), None, ALU.add))
            link(v.tensor_tensor(eq, iota_b, over(rc(5)), ALU.is_equal))
            link(v.tensor_tensor(eq, eq, over(live), ALU.mult))
            v.tensor_copy(ohH, eq).then_inc(s_ohr, 1)
            dve.wait_ge(s_pos, 1)
            tot, before = rt(4), rt(5)
            link(v.tensor_copy(tot, PS[6][:, 0:NT * E].rearrange("p (a e) -> p a e", e=E)))
            step(v.memset(before[:, 0:1, :], 0.0))
            for e in range(E):
                step(v.tensor_tensor_scan(before[:, 1:NT, e], tot[:, 0:NT - 1, e], tot[:, 0:NT - 1, e], 0.0,
                                          ALU.add, ALU.max))
            settle()
            link(v.tensor_tensor(before, PS[5][:, 0:NT * E].rearrange("p (a e) -> p a e", e=E), before, ALU.add))
            link(v.tensor_tensor(before, before, eq, ALU.mult))
            link(v.tensor_reduce(rc(6), before, AX.X, ALU.add))
            link(v.tensor_scalar(rc(6), rc(6), -1.0, None, ALU.add))
            link(v.tensor_scalar(rc(7), rc(6), float(CAP), None, ALU.is_lt))
            link(v.tensor_tensor(rc(7), rc(7), live, ALU.mult))
            link(v.scalar_tensor_tensor(rc(6), rc(5), float(SROW), rc(6), ALU.mult, ALU.add))
            link(v.scalar_tensor_tensor(rc(6), rc(6), -NOROW, rc(7), ALU.add, ALU.mult))
            link(v.tensor_scalar(rc(6), rc(6), NOROW, None, ALU.add))
            step(v.tensor_copy(comb[:, :, 2 * D], rc(4)))
            step(v.tensor_copy(comb[:, :, 2 * D + 1], node))
            settle()
            v.tensor_copy(slotI[:, :], rc(6)).then_inc(s_slot, 1)

            dve.wait_ge(s_b2, 16)
            step(v.memset(zero_y, 0.0))
            settle()

            def rows_copied(e):
                dve.wait_ge(s_xbp, e + 1)
                v.tensor_copy(xbT[e % 2][:, 0, :], PS[0][:, :]).then_inc(s_xbc0, 1)

            rows_copied(0)
            for e in range(E):
                u = e % 2
                if e + 1 < E:
                    rows_copied(e + 1)
                if e >= 2:
                    dve.wait_ge(s_outs[u], 16 * 4 * (e // 2))
                dve.wait_ge(s_xb[u], 16 * (e // 2 + 1))
                link(v.tensor_copy(tokI[u][:, :], xb[u][:, :, 2 * D + 1]))
                for j in range(4):
                    m = min(P, CAP - P * j)
                    y, t, mask = yt[u][:, j, :], tmp_y, tmp_m.bitcast(I32)
                    if m < P:
                        step(v.memset(y, 0.0))
                    dve.wait_ge(s_down, 4 * e + j + 1)
                    link(v.tensor_tensor(t[0:m], PS[4 + j][0:m, 0:D], b2B[0:m, e, :], ALU.add))
                    link(v.tensor_scalar(t[0:m], t[0:m], xb[u][0:m, j, 2 * D:2 * D + 1], None, ALU.mult))
                    step(v.tensor_scalar(y[0:m], t[0:m], POSINF, -POSINF, ALU.min, ALU.max))
                    link(v.tensor_scalar(mask[0:m], t[0:m], 0.0, 0.0, ALU.mult, ALU.is_equal))
                    link(v.copy_predicated(y[0:m], mask[0:m], t[0:m]))
                    link(v.tensor_tensor(mask[0:m], t[0:m], t[0:m], ALU.not_equal))
                    link(v.copy_predicated(y[0:m], mask[0:m], zero_y[0:m]))
                    ins = v.tensor_tensor(y[0:m], y[0:m], xb[u][0:m, j, D:2 * D], ALU.add)
                    ins.then_inc(s_y, 1)
                dve.wait_ge(s_y, 4 * e + 4)
                v.memset(fb[:, 3:4], 0.0).then_inc(s_xbfree[u], 1)

        @block.scalar
        def _(act):
            s = nc.scalar

            def root(mark, width):
                act.wait_ge(s_sqi, mark)
                s.activation(rs[:, 1, 0:width], rs[:, 0, 0:width], ACT.Sqrt).then_inc(s_sq, 1)

            nb = E * F // P
            gcnb, linb, gateb = (VT[:, nb + 2 * k:nb + 2 * k + 2] for k in range(3))
            root(1, NT)
            act.wait_ge(s_vT, 1)
            s.activation(VT[:, :], PS[1][:, 0:nb + 10], ACT.Copy).then_inc(s_vTc, 1)
            for q in range(7):
                n = min(512, NPAD - 512 * q)
                act.wait_ge(s_bc, q + 1)
                s.activation(degB[:, 512 * q:512 * q + n], PS[2 + q % 2][:, 0:n], ACT.Copy).then_inc(s_bcc, 1)
            root(2, NT)
            act.wait_ge(s_dx, 1)
            act.wait_ge(s_ln, 1)
            for a in range(NT):
                s.activation(xs[:, a, 0:D], xn[:, a, :], ACT.Copy, scale=dinvx[:, 0, a:a + 1]).then_inc(s_hi, 1)
            for q in range(7):
                n = min(512, NPAD - 512 * q)
                act.wait_ge(s_bc, 8 + q)
                s.activation(DB[:, 512 * q:512 * q + n], PS[2 + q % 2][:, 0:n], ACT.Copy).then_inc(s_bcc, 1)
            for k, to in enumerate((lowT, keyT)):
                act.wait_ge(s_keyp, 2 * k + 1)
                s.activation(to[:, 0:500], PS[4 + 2 * k][:, 0:500], ACT.Copy).then_inc(s_keyc, 1)
                act.wait_ge(s_keyp, 2 * k + 2)
                s.activation(to[:, 500:NW], PS[5 + 2 * k][:, 0:ROWS], ACT.Copy).then_inc(s_keyc, 1)
            act.wait_ge(s_vTc, 1)
            for q in range(7):
                n = min(512, NPAD - 512 * q)
                act.wait_ge(s_lnt, q + 1)
                if q >= 1:
                    act.wait_ge(s_lin, q)
                for h in range(H):
                    s.activation(lnT[:, h, 0:n], PS[2 + h][:, 0:n], ACT.Copy).then_inc(s_lnc, 1)
                act.wait_ge(s_lin, q + 1)
                for h in range(H):
                    s.activation(XL[:, h, 512 * q:512 * q + n], PS[4 + h][:, 0:n], ACT.Identity,
                                 bias=linb[:, h:h + 1]).then_inc(s_linc, 1)
            act.wait_ge(s_flag, 1)
            fast = act.value_load(flagI[0:1, 0:1], min_val=0, max_val=1)

            def copy_built(step_from, steps, buf, col0, total_before):
                with act.Fori(step_from, step_from + steps // 2) as m:
                    for u in range(2):
                        act.wait_ge(s_bld, 2 * m + (total_before + u + 1))
                        s.activation(A[buf][:, :, bass.ds(40 * m + (20 * u), 4 * WN)].rearrange("p a (w d) -> p w a d", d=WN),
                                     PS[u][:, 0:4 * KEYS].rearrange("p (w a d) -> p w a d", w=4, d=WN),
                                     ACT.Copy).then_inc(s_ev, 1)

            for gr in range(-1, G + 2):
                if gr + 1 < G:
                    with act.If(fast == 1):
                        if gr + 1 >= 2:
                            act.wait_ge(s_agg, gr)
                        copy_built(0, GI if gr + 1 < G - 1 else LASTI, (gr + 1) % 2, 0, GI * (gr + 1))
                    with act.Else():
                        act.nop()
                q = gr - 1
                if 0 <= q < G:
                    nn = GN if q < G - 1 else LASTN
                    for h in range(H):
                        act.wait_ge(s_gcn, q + 1)
                        s.activation(zT[q % 2][:, h, 0:nn], PS[6 + h][:, 0:nn], ACT.Tanh,
                                     bias=gcnb[:, h:h + 1]).then_inc(s_z, 1)
                q = gr - 1
                if 0 <= q < G:
                    nn = GN if q < G - 1 else LASTN
                    act.wait_ge(s_gate, q + 1)
                    if q >= 1:
                        act.wait_ge(s_h, H * q)
                    for h in range(H):
                        s.activation(gT[:, h, 0:nn], PS[6 + h][:, 0:nn], ACT.Sigmoid,
                                     bias=gateb[:, h:h + 1]).then_inc(s_g, 1)
            root(3, H)
            root(4, NT)
            for q in range(7):
                n = min(512, NPAD - 512 * q)
                act.wait_ge(s_xnp, q + 1)
                for h in range(H):
                    s.activation(xnT[q % 2][:, h, 0:n], PS[2 * (q % 2) + h][:, 0:n], ACT.Copy).then_inc(s_xnc, 1)
            act.wait_ge(s_expi, 1)
            s.activation(rt(1), rt(0), ACT.Exp).then_inc(s_exp, 1)

            def rows_copied(e):
                act.wait_ge(s_xbp, e + 1)
                s.activation(xbT[e % 2][:, 1, :], PS[1][:, :], ACT.Copy).then_inc(s_xbc1, 1)

            rows_copied(0)
            for e in range(E):
                for f in range(8):
                    act.wait_ge(s_up, 8 * e + f + 1)
                    if e >= 2 and f == 0:
                        act.wait_ge(s_down, 4 * (e - 1))
                    s.activation(hid[e % 2][:, f, :], PS[2 + f % 2][:, 0:CAP], ACT.Relu,
                                 bias=VT[:, 8 * e + f:8 * e + f + 1]).then_inc(s_hid, 1)
                if e + 1 < E:
                    rows_copied(e + 1)

        @block.tensor
        def _(pe):
            t = nc.tensor
            pe.wait_ge(s_const, 2)
            nb = E * F // P + 10
            pe.wait_ge(s_vec, 16 * 6)
            t.transpose(PS[1][:, 0:nb], VR[:, :], ident[0:nb, 0:nb]).then_inc(s_vT, 1)
            pe.wait_ge(s_ohlo, 1)
            pe.wait_ge(s_ohhi, 1)
            t.matmul(PS[0][:, 0:NT], oh_lo[0:ROWS, :, 0], oh_hi[0:ROWS, :, 0], start=True, stop=False)
            with pe.Fori(0, (RCOLS - 4) // 4) as m:
                for k in range(4):
                    t.matmul(PS[0][:, 0:NT], oh_lo[0:ROWS, :, bass.ds(4 * m + (k + 1), 1)].rearrange("p v o -> p (v o)"),
                             oh_hi[0:ROWS, :, bass.ds(4 * m + (k + 1), 1)].rearrange("p v o -> p (v o)"), start=False, stop=False)
            for c in range(RCOLS - 3, RCOLS):
                ins = t.matmul(PS[0][:, 0:NT], oh_lo[0:ROWS, :, c], oh_hi[0:ROWS, :, c], start=False,
                               stop=(c == RCOLS - 1))
            ins.then_inc(s_hist, 1)
            for k in range(14):
                q = k % 7
                m = min(4, NT - 4 * q)
                pe.wait_ge(s_diag, k + 1)
                if k >= 2:
                    pe.wait_ge(s_bcc, k - 1)
                t.matmul(PS[2 + q % 2][:, 0:P * m], ones[:, :], diag[:, 0:m, :].rearrange("p q n -> p (q n)"),
                         start=True, stop=True).then_inc(s_bc, 1)
            pe.wait_ge(s_key, 1)
            low, key = keyw[0], keyw[5]
            for k, w in enumerate((low, key)):
                for j in range(WB):
                    to = PS[4 + 2 * k][:, ROWS * j:ROWS * (j + 1)] if j < 4 else PS[5 + 2 * k][:, 0:ROWS]
                    ins = t.transpose(to, w[0:ROWS, j, :], ident[0:ROWS, 0:ROWS])
                    if j >= 3:
                        ins.then_inc(s_keyp, 1)
            pe.wait_ge(s_keyc, 4)
            t.matmul(PS[7][0:1, 0:1], fb[0:ROWS, 0:1], ones[0:ROWS, 0:1], start=True, stop=True).then_inc(s_cnt, 1)
            pe.wait_ge(s_w, 48)
            pe.wait_ge(s_ln, 1)
            pe.wait_ge(s_bcc, 14)
            for q in range(7):
                tiles = min(4, NT - 4 * q)
                n = P * tiles
                if q >= 1:
                    pe.wait_ge(s_lnc, H * q)
                for h in range(H):
                    for a in range(tiles):
                        ins = t.transpose(PS[2 + h][:, P * a:P * (a + 1)], xn[:, 4 * q + a, P * h:P * (h + 1)], ident[:, :])
                ins.then_inc(s_lnt, 1)
                pe.wait_ge(s_lnc, H * (q + 1))
                if q >= 1:
                    pe.wait_ge(s_linc, H * q)
                for h in range(H):
                    for k in range(H):
                        ins = t.matmul(PS[4 + h][:, 0:n], linW[:, k, P * h:P * (h + 1)], lnT[:, k, 0:n],
                                       start=(k == 0), stop=(k == H - 1))
                ins.then_inc(s_lin, 1)
            pe.wait_ge(s_linc, H * 7)
            pe.wait_ge(s_lo, 1)
            pe.wait_ge(s_flag, 1)
            fast = pe.value_load(flagI[0:1, 0:1], min_val=0, max_val=1)

            def build(i_wait, ev_wait, u):
                pe.wait_ge(s_oh, i_wait)
                if ev_wait is not None:
                    pe.wait_ge(s_ev, ev_wait)
                for w in range(4):
                    ins = t.matmul(PS[u][:, KEYS * w:KEYS * (w + 1)], ohb[:, 4 * u + w, :], ohk[:, 4 * u + w, :],
                                   start=True, stop=True)
                ins.then_inc(s_bld, 1)

            def aggregate(gr, a, start, stop):
                nn = GN if gr < G - 1 else LASTN
                for h in range(H):
                    for part in range(2):
                        first, last = start and part == 0, stop and part == 1
                        lo = D * part + P * h
                        ins = t.matmul(PS[2 + 2 * (gr % 2) + h][:, 0:nn],
                                       xs[:, bass.ds(a, 1), lo:lo + P].rearrange("p o d -> p (o d)") if not isinstance(a, int)
                                       else xs[:, a, lo:lo + P],
                                       A[gr % 2][:, bass.ds(a, 1), 0:nn].rearrange("p o n -> p (o n)") if not isinstance(a, int)
                                       else A[gr % 2][:, a, 0:nn],
                                       start=first, stop=last)
                return ins

            def gcn(q):
                nn = GN if q < G - 1 else LASTN
                pe.wait_ge(s_aggc, q + 1)
                if q >= 1:
                    pe.wait_ge(s_g, H * q)
                for h in range(H):
                    for k in range(H):
                        ins = t.matmul(PS[6 + h][:, 0:nn], gcnW[:, k, P * h:P * (h + 1)], aggT[q % 2][:, k, 0:nn],
                                       start=(k == 0), stop=(k == H - 1))
                ins.then_inc(s_gcn, 1)

            def gate(q):
                nn = GN if q < G - 1 else LASTN
                pe.wait_ge(s_z, H * (q + 1))
                for h in range(H):
                    for k in range(H):
                        ins = t.matmul(PS[6 + h][:, 0:nn], gateW[:, k, P * h:P * (h + 1)], zT[q % 2][:, k, 0:nn],
                                       start=(k == 0), stop=(k == H - 1))
                ins.then_inc(s_gate, 1)

            with pe.If(fast == 1):
                build(1, None, 0)
                build(2, None, 1)
                with pe.Fori(1, GI // 2) as m:
                    for u in range(2):
                        build(2 * m + (u + 1), 2 * m + (u - 1), u)
            with pe.Else():
                pe.nop()
            for gr in range(G + 1):
                if gr < G:
                    nxt = gr + 1
                    nsteps = 0 if nxt >= G else GI if nxt < G - 1 else LASTI
                    if gr >= 2:
                        pe.wait_ge(s_aggc, gr - 1)
                    with pe.If(fast == 1):
                        pe.wait_ge(s_ev, GI * gr + (GI if gr < G - 1 else LASTI))
                        base = GI * nxt

                        def pair(m, first, with_build):
                            for u in range(2):
                                if with_build:
                                    build(2 * m + (base + u + 1), 2 * m + (base + u - 1), u)
                                a = 2 * m + u
                                aggregate(gr, a, first and u == 0, False)

                        pair(0, True, nsteps > 0)
                        if nsteps:
                            with pe.Fori(1, nsteps // 2) as m:
                                pair(m, False, True)
                        lo = max(1, nsteps // 2)
                        if lo < GI // 2:
                            with pe.Fori(lo, GI // 2) as m:
                                pair(m, False, False)
                        aggregate(gr, NT - 1, False, True).then_inc(s_agg, 1)
                    with pe.Else():
                        NC = RCOLS + LOOPC
                        nn = GN if gr < G - 1 else LASTN

                        def general(c, at_row, at_sel, start, stop):
                            pe.wait_ge(s_grow, at_row)
                            pe.wait_ge(s_sel, at_sel)
                            for h in range(H):
                                for part in range(2):
                                    lo = D * part + P * h
                                    ins = t.matmul(PS[2 + 2 * (gr % 2) + h][:, 0:nn], gath[0:ROWS, lo:lo + P],
                                                   dsel[0:ROWS, 0:nn], start=start and part == 0, stop=stop and part == 1)
                            return ins

                        general(0, 16 * (gr * NC + 1), gr * NC + 1, True, False).then_inc(s_gmm, 1)
                        with pe.Fori(1, NC - 1) as c:
                            general(c, 16 * c + 16 * (gr * NC + 1), c + (gr * NC + 1), False, False).then_inc(s_gmm, 1)
                        general(NC - 1, 16 * (gr + 1) * NC, (gr + 1) * NC, False, True).then_inc(s_gmm, 1)
                        pe.wait_ge(s_gmm, (gr + 1) * NC)
                        t.matmul(PS[0][0:1, 0:1], ident[:, 0:1], ident[:, 0:1], start=True, stop=True).then_inc(s_agg, 1)
                q = gr - 1
                if 0 <= q < G:
                    gcn(q)
                    gate(q)
            pe.wait_ge(s_bn, 1)
            for a in range(NT):
                if a >= 4:
                    pe.wait_ge(s_x1, a - 3)
                for h in range(H):
                    ins = t.transpose(PS[a % 4][:, P * h:P * (h + 1)], XL[:, h, P * a:P * (a + 1)], ident[:, :])
                ins.then_inc(s_yT, 1)
            pe.wait_ge(s_fg, 32)
            pe.wait_ge(s_x1, NT)

            def logits(q):
                pe.wait_ge(s_xnc, H * (q + 1))
                for a in range(min(4, NT - 4 * q)):
                    for k in range(H):
                        ins = t.matmul(PS[4][:, E * (4 * q + a):E * (4 * q + a + 1)], xnT[q % 2][:, k, P * a:P * (a + 1)],
                                       fgw[:, k, :], start=(k == 0), stop=(k == H - 1))
                return ins

            for q in range(7):
                tiles = min(4, NT - 4 * q)
                pe.wait_ge(s_xn2, 4 * q + tiles)
                for h in range(H):
                    for a in range(tiles):
                        ins = t.transpose(PS[2 * (q % 2) + h][:, P * a:P * (a + 1)], comb[:, 4 * q + a, P * h:P * (h + 1)],
                                          ident[:, :])
                ins.then_inc(s_xnp, 1)
                if q >= 1:
                    logits(q - 1)
            logits(6).then_inc(s_log, 1)
            pe.wait_ge(s_ohr, 1)
            r = ohH.rearrange("p a e -> p (a e)")
            t.matmul(PS[5][:, 0:NT * E], triH[:, :], r, start=True, stop=True)
            t.matmul(PS[6][:, 0:NT * E], onesH[:, :], r, start=True, stop=True).then_inc(s_pos, 1)

            def rows_transposed(e):
                u = e % 2
                pe.wait_ge(s_xb[u], 16 * (e // 2 + 1))
                if e >= 1:
                    pe.wait_ge(s_xbc0, e)
                    pe.wait_ge(s_xbc1, e)
                for h in range(H):
                    for j in range(4):
                        ins = t.transpose(PS[h][:, P * j:P * (j + 1)], xb[u][:, j, P * h:P * (h + 1)], ident[:, :])
                ins.then_inc(s_xbp, 1)

            rows_transposed(0)
            for e in range(E):
                u = e % 2
                pe.wait_ge(s_xbc0, e + 1)
                pe.wait_ge(s_xbc1, e + 1)
                pe.wait_ge(s_wl[u], 32 * (e // 2 + 1))
                for f in range(8):
                    if 8 * e + f >= 2:
                        pe.wait_ge(s_hid, 8 * e + f - 1)
                    for k in range(H):
                        ins = t.matmul(PS[2 + f % 2][:, 0:CAP], w1s[u][:, k, P * f:P * (f + 1)], xbT[u][:, k, 0:CAP],
                                       start=(k == 0), stop=(k == H - 1))
                    ins.then_inc(s_up, 1)
                if e + 1 < E:
                    rows_transposed(e + 1)
                pe.wait_ge(s_hid, 8 * e + 8)
                for j in range(4):
                    m = min(P, CAP - P * j)
                    if e >= 1:
                        pe.wait_ge(s_y, 4 * (e - 1) + j + 1)
                    for f in range(8):
                        ins = t.matmul(PS[4 + j][0:m, 0:D], hid[u][:, f, P * j:P * j + m], w2s[u][:, f, :],
                                       start=(f == 0), stop=(f == 7))
                    ins.then_inc(s_down, 1)
                pe.wait_ge(s_down, 4 * e + 4)
                pe.sem_inc(s_wfree[u], 1)


HI_POOL = 16

_INS = ["x", "src", "dst", "L0_gnn_gcn_W", "L0_gnn_gcn_b", "L0_gnn_lin_W", "L0_gnn_lin_b", "L0_gnn_gate_W",
        "L0_gnn_gate_b", "L0_gnn_bn_gamma", "L0_gnn_bn_beta", "L0_ffn_gate_w", "L0_ffn_gate_b", "L0_ffn_w1",
        "L0_ffn_b1", "L0_ffn_w2", "L0_ffn_b2"]


def kernel(**inputs):
    import numpy as np
    from concourse import bacc
    from concourse.bass_utils import run_bass_kernel_spmd

    nc = bacc.Bacc("TRN2", target_bir_lowering=False, num_devices=1)
    arrays, args = {}, []
    for name in _INS:
        a = np.ascontiguousarray(inputs[name])
        arrays[f"in_{name}"] = a
        args.append(nc.dram_tensor(f"in_{name}", a.shape, mybir.dt.from_np(a.dtype), kind="ExternalInput").ap())
    out = nc.dram_tensor("out", (N_NODES, D), F32, kind="ExternalOutput").ap()
    gnn_ffn(nc, *args, out)
    r = run_bass_kernel_spmd(nc, [arrays], core_ids=[0])
    return r.results[0]["out"]
```

```python
import concourse.bass as bass
from concourse import mybir
from contextlib import ExitStack

F32 = mybir.dt.float32
F32R = mybir.dt.float32r
F16 = mybir.dt.float16
I32 = mybir.dt.int32
ALU = mybir.AluOpType
ACT = mybir.ActivationFunctionType
AX = mybir.AxisListType

P = 128
N_NODES, N_EDGES, D = 3125, 50000, 256
E, F, CAP = 8, 1024, 489
LN_EPS = BN_EPS = 1e-5
H = D // P
NT = -(-N_NODES // P)
TAIL = N_NODES - (NT - 1) * P
NPAD = NT * P
ROWS, RCOLS = 125, 400
LOOPC = N_NODES // ROWS
WN = 5
NW = N_NODES // WN
WB = NW // ROWS
SLOTS = P - WN
KEYS = NT * WN
NOKEY = 1000.0
GI = 24
GW = 4 * GI
GN = GW * WN
G = -(-NW // GW)
LASTI = 2 * -(-(NW - (G - 1) * GW) // 8)
LASTN = LASTI * 4 * WN
WPAD = (G - 1) * GW + LASTI * 4
XSC = 64.0
SROW = 512
CAPE = CAP + CAP % 2
CW = 2 * D + 2
NOROW = 1.0e6
POSINF = 1.0e4


def gnn_ffn(nc, x, src, dst, gcn_W, gcn_b, lin_W, lin_b, gate_W, gate_b, bn_gamma, bn_beta,
            fgate_w, fgate_b, w1, b1, w2, b2, out):
    xs_d = nc.dram_tensor("xs_table", (NPAD, 2 * D), F16, kind="Internal").ap()
    buf_d = nc.dram_tensor("dispatch", (E * SROW, CW), F32, kind="Internal").ap()
    src_flat = src.rearrange("(n o) -> n o", o=1)
    dst_flat = dst.rearrange("(n o) -> n o", o=1)
    ctx = ExitStack()
    with ctx:
        def sb(name, shape, dt):
            return ctx.enter_context(nc.sbuf_tensor(name, shape, dt))

        def sem(name):
            return ctx.enter_context(nc.semaphore(name))

        XX_at = -(-nc.sbuf_base // 32) * 32
        XX = sb("XX", [P, NT * CW], F32)
        xn = XX[:, 0:NT * D].rearrange("p (a d) -> p a d", d=D)
        xs = XX[:, NT * D:2 * NT * D].bitcast(F16).rearrange("p (a d) -> p a d", d=2 * D)
        comb = XX[:, :].rearrange("p (a c) -> p a c", c=CW)
        XL = sb("XL", [P, H, NPAD], F32)
        DB = sb("DB", [P, NPAD], F32)
        R_at = -(-nc.sbuf_base // 32) * 32
        R = sb("R", [P, 51200], F16)

        def at(byte, n, dt):
            size = 2 if dt == F16 else 4
            v = R[:, byte // 2:(byte + n * size) // 2]
            return v if dt == F16 else v.bitcast(dt)

        oh_lo = at(0, P * RCOLS, F16).rearrange("p (v c) -> p v c", c=RCOLS)
        oh_hi = XX[:, NT * D:NT * D + NT * RCOLS // 2].bitcast(F16).rearrange("p (v c) -> p v c", c=RCOLS)
        A = [at(24000 * k, NT * GN, F16).rearrange("p (a n) -> p a n", n=GN) for k in range(2)]
        degB = at(48000, NPAD, F32)
        aggT = [at(60800 + 3840 * k, H * GN, F32).rearrange("p (h n) -> p h n", n=GN) for k in range(2)]
        zT = [at(68480 + 3840 * k, H * GN, F32).rearrange("p (h n) -> p h n", n=GN) for k in range(2)]
        gT = at(76160, H * GN, F32).rearrange("p (h n) -> p h n", n=GN)
        mT = at(80000, H * GN, F32).rearrange("p (h n) -> p h n", n=GN)
        keyw = [at(76160 + 2560 * k, WB * P, F32).rearrange("p (j s) -> p j s", s=P) for k in range(6)]
        diag = [at(30000 + 2048 * k, 4 * P, F32).rearrange("p (q n) -> p q n", n=P) for k in range(4)]
        ohb = [at(91520 + 2048 * k, 8 * P, F16).rearrange("p (w n) -> p w n", n=P) for k in range(2)]
        ohk = [at(95616 + 2000 * k, 8 * KEYS, F16).rearrange("p (w n) -> p w n", n=KEYS) for k in range(2)]
        lnT = [at(60800 + 4096 * k, H * 512, F32).rearrange("p (h n) -> p h n", n=512) for k in range(2)]
        xsf = [at(40000 + 1024 * k, D, F32) for k in range(2)]
        edges_s = at(24000, WB * SLOTS, I32).rearrange("p (j s) -> p j s", s=SLOTS)
        edges_d = at(26464, WB * SLOTS, I32).rearrange("p (j s) -> p j s", s=SLOTS)
        gath = at(0, 2 * D, F16)
        dsel = at(1024, GN, F16)
        io480 = at(2048, GN, F16)
        w1s = at(0, H * F, F32).rearrange("p (h f) -> p h f", f=F)
        w2s = at(8192, 8 * D, F32).rearrange("p (f d) -> p f d", d=D)
        w_r = [nc.alloc_sbuf_tensor_at(f"expert_weights_{n}", [P, 2, 2, 2048], F32R, offset=R_at + 16384 + 32768 * k)
               for k, n in enumerate(("even", "odd"))]
        w1r = [[w_r[k][:, 0, part, :].rearrange("p (h f) -> p h f", f=F) for part in range(2)] for k in range(2)]
        w2r = [[w_r[k][:, 1, part, :].rearrange("p (f d) -> p f d", d=D) for part in range(2)] for k in range(2)]
        hid_r = nc.alloc_sbuf_tensor_at("expert_hidden", [P, 2, 8, 512], F32R, offset=XX_at)
        hidr = [hid_r[:, part] for part in range(2)]
        rows_r = nc.alloc_sbuf_tensor_at("expert_rows", [P, 2, 2, H, 512], F32R, offset=XX_at + 32768)
        xbTr = [[rows_r[:, k, part] for part in range(2)] for k in range(2)]
        xb = [at(81920 + 8224 * k, 4 * CW, F32).rearrange("p (j c) -> p j c", c=CW) for k in range(2)]
        xnT = [at(81920 + 4096 * k, H * 512, F32).rearrange("p (h s) -> p h s", s=512) for k in range(2)]
        xl_flat = XL[:, :, :].rearrange("p h n -> p (h n)")
        yt = [xl_flat[:, 1024 * k:1024 * (k + 1)].rearrange("p (j d) -> p j d", d=D) for k in range(2)]
        hidf = xl_flat[:, 2048:2048 + 8 * CAPE].rearrange("p (f s) -> p f s", s=CAPE)
        b2B = DB[:, 0:E * D].rearrange("p (e d) -> p e d", d=D)
        tmp_y = DB[:, E * D:E * D + D]
        tmp_m = DB[:, E * D + D:E * D + 2 * D]
        zero_y = DB[:, E * D + 2 * D:E * D + 3 * D]

        gcnW = sb("gcnW", [P, H, D], F32)
        linW = sb("linW", [P, H, D], F32)
        gateW = sb("gateW", [P, H, D], F32)
        ident = sb("ident", [P, P], F32)
        ones = sb("ones", [P, P], F32)
        onesH = sb("onesH", [P, P], F16)
        triH = sb("triH", [P, P], F16)
        iotaH = sb("iotaH", [P, P], F16)
        iotaI = R[:, 0:2 * P].bitcast(I32)
        srcI = sb("srcI", [ROWS, RCOLS + LOOPC], I32)
        dstI = sb("dstI", [ROWS, RCOLS + LOOPC], I32)
        lo16 = XL[0:ROWS, 0, 800:1000].bitcast(F16)
        hi16 = XL[0:ROWS, 0, 1000:1200].bitcast(F16)
        tmpI = XL[0:ROWS, 0, 0:RCOLS].bitcast(I32)
        tmpI2 = XL[0:ROWS, 0, RCOLS:2 * RCOLS].bitcast(I32)
        VR = sb("VR", [E * F // P + 10, P], F32)
        VT = sb("VT", [P, E * F // P + 10], F32)
        fgw = sb("fgw", [P, H, E], F32)
        fgb = sb("fgb", [P, E], F32)
        keyT = sb("keyT", [P, WPAD], F32)
        lowT = sb("lowT", [P, WPAD], F32)
        stats = sb("stats", [P, NT, 6], F32)
        mv = sb("mv", [P, NT, 2], F32)
        rs = sb("rs", [P, 4, NT], F32)
        dinvx = sb("dinvx", [P, 2, NT], F32)
        degR = sb("degR", [P, NT], F32)
        wI = sb("wI", [ROWS, WB], I32)
        wIdx = sb("wIdx", [ROWS, WB], I32)
        selfI = sb("selfI", [ROWS, 3, WB * WN], I32)
        cs = XL[:, 1, 0:NW + 1]
        wF = sb("wF", [ROWS, 2, WB], F32)
        fb = sb("fb", [P, 4], F32)
        flagF = sb("flagF", [1, 1], F32)
        flagI = sb("flagI", [1, 1], I32)
        idxc = sb("idxc", [ROWS, 1], I32)
        dcol = sb("dcol", [ROWS, 1], F32)
        bnst = sb("bnst", [P, H, G, 6], F32)
        bnmv = sb("bnmv", [P, H, 2], F32)
        bnc = sb("bnc", [P, 6, H], F32)
        nodeI = sb("nodeI", [P, NT], I32)
        slotI = sb("slotI", [P, NT], I32)
        iota8 = sb("iota8", [P, E], F32)
        tokI = [sb(f"tokI{k}", [P, 4], I32) for k in range(2)]
        def rt(k):
            return XL[:, 0, 200 * k:200 * k + NT * E].rearrange("p (a e) -> p a e", e=E)
        def rc(k):
            return XL[:, 1, NT * k:NT * (k + 1)]
        ohH = XL[:, 1, 1000:1100].bitcast(F16).rearrange("p (a e) -> p a e", e=E)
        fill = XL[:, 1, 2000:2000 + CW]

        PS = [ctx.enter_context(nc.psum_tensor(f"PS{k}", [P, 512], F32)) for k in range(8)]

        s_dst, s_src, s_x, s_w, s_vec, s_fg, s_x2, s_b2 = [sem(n) for n in (
            "dst_loaded", "src_loaded", "x_loaded", "weights_loaded", "vectors_loaded", "router_loaded",
            "x_reloaded", "b2_loaded")]
        s_const = sem("consts_ready")
        s_iota = sem("iota_ready")
        s_iota_f = sem("iota_cast")
        s_split = sem("dst_split")
        s_ohlo, s_ohhi = sem("onehot_low_ready"), sem("onehot_high_ready")
        s_hist = sem("histogram_done")
        s_diag, s_bc, s_bcc = sem("diag_ready"), sem("broadcast_done"), sem("broadcast_copied")
        s_sq, s_sqi = sem("sqrt_done"), sem("sqrt_input_ready")
        s_start, s_gs, s_gd = sem("window_starts_ready"), sem("sources_gathered"), sem("dests_gathered")
        s_key, s_keyp, s_keyc = sem("keys_ready"), sem("keys_transposed"), sem("keys_copied")
        s_cnt, s_flag = sem("matched_counted"), sem("flag_ready")
        s_ln, s_lnt, s_lnc, s_lin, s_linc = (sem("ln_ready"), sem("ln_transposed"), sem("ln_copied"),
                                             sem("lin_done"), sem("lin_copied"))
        s_dx, s_hi, s_lo = sem("source_scale_ready"), sem("source_high_ready"), sem("source_low_ready")
        s_vT, s_vTc = sem("vectors_transposed"), sem("vectors_copied")
        s_oh, s_bld, s_ev = sem("window_onehots_ready"), sem("windows_built"), sem("adjacency_copied")
        s_agg, s_aggc = sem("aggregated"), sem("aggregate_scaled")
        s_gcn, s_z, s_gate, s_g = sem("gcn_done"), sem("z_ready"), sem("gate_done"), sem("g_ready")
        s_diff, s_h = sem("mix_difference_ready"), sem("h_ready")
        s_tab, s_gidx, s_grow, s_sel, s_gmm, s_io480 = (sem("table_stored"), sem("gather_index_ready"),
                sem("rows_gathered"), sem("selector_ready"), sem("general_step_done"), sem("iota480_ready"))
        s_dcol = sem("dest_column_ready")
        s_xsf, s_zx = sem("source_scaled"), sem("z_minus_xl")
        s_ptick = sem("pool_tick")
        s_loops = sem("loops_ready")
        s_bn, s_yT, s_x1 = sem("bn_applied"), sem("y_transposed"), sem("x1_ready")
        s_xn2, s_xnp, s_xnc, s_log = sem("ln2_ready"), sem("ln2_transposed"), sem("ln2_copied"), sem("logits_done")
        s_expi, s_exp, s_ohr, s_pos, s_posc = (sem("exp_input_ready"), sem("exp_done"), sem("route_ready"),
                                              sem("positions_done"), sem("totals_copied"))
        s_fillr, s_filled, s_slot, s_disp = sem("fill_ready"), sem("buffer_filled"), sem("slots_ready"), sem("dispatched")
        s_out0, s_outs = sem("residual_stored"), [sem(f"rows_stored{k}") for k in range(2)]
        s_wl = [sem(f"expert_w{k + 1}_loaded") for k in range(2)]
        s_xb = [sem(f"expert_rows{k}") for k in range(2)]
        s_xbfree = [sem(f"expert_rows_used{k}") for k in range(2)]
        s_xbp, s_xbh, s_xbl = sem("rows_transposed"), sem("rows_high_ready"), sem("rows_low_ready")
        s_wh, s_wlow = sem("weights_high_ready"), sem("weights_low_ready")
        s_up, s_hidf, s_hidh, s_hidl = (sem("up_done"), sem("hidden_ready"), sem("hidden_high_ready"),
                                        sem("hidden_low_ready"))
        s_down, s_y, s_pad = sem("down_done"), sem("y_ready"), sem("hidden_padded")
        s_fix = sem("y_step")
        dch, pch, ach = sem("vector_chain"), sem("pool_chain"), sem("scalar_chain")

        block = ctx.enter_context(nc.Block())

        def bcast_src(v, shape):
            return v.to_broadcast(shape)

        @block.sync
        def _(sp):
            sp.dma_start(dstI[:, 0:RCOLS], dst.rearrange("(r c) -> r c", c=RCOLS)).then_inc(s_dst, 16)
            full = (NT - 1) * P
            sp.wait_ge(s_const, 1)
            sp.dma_start(xn[:, 0:NT - 1, :], x[0:full, :].rearrange("(a p) d -> p a d", p=P)).then_inc(s_x, 16)
            sp.dma_start(xn[0:TAIL, NT - 1, :], x[full:N_NODES, :]).then_inc(s_x, 16)
            sp.dma_start(srcI[:, 0:RCOLS], src.rearrange("(r c) -> r c", c=RCOLS)).then_inc(s_src, 16)
            for w_sb, w in ((linW, lin_W), (gcnW, gcn_W), (gateW, gate_W)):
                sp.dma_start(w_sb[:, :, :], w.rearrange("(h p) n -> p h n", p=P)).then_inc(s_w, 16)
            nb = E * F // P
            sp.dma_start(VR[0:nb, :], b1.rearrange("e (f p) -> (e f) p", p=P)).then_inc(s_vec, 16)
            for k, v in enumerate((gcn_b, lin_b, gate_b, bn_gamma, bn_beta)):
                sp.dma_start(VR[nb + 2 * k:nb + 2 * k + 2, :], v.rearrange("(h p) -> h p", p=P)).then_inc(s_vec, 16)
            sp.dma_start(fgw[:, :, :], fgate_w.rearrange("(h p) e -> p h e", p=P)).then_inc(s_fg, 16)
            sp.dma_start(fgb[:, :], fgate_b.rearrange("(o e) -> o e", o=1).to_broadcast([P, E])).then_inc(s_fg, 16)
            sp.wait_ge(s_agg, G)
            sp.wait_ge(s_const, 3)
            sp.dma_start(comb[:, 0:NT - 1, D:2 * D], x[0:full, :].rearrange("(a p) d -> p a d", p=P)).then_inc(s_x2, 16)
            sp.dma_start(comb[0:TAIL, NT - 1, D:2 * D], x[full:N_NODES, :]).then_inc(s_x2, 16)
            sp.wait_ge(s_aggc, G)
            sp.dma_start(DB[:, 0:E * D], b2.rearrange("(o e) d -> o (e d)", o=1).to_broadcast([P, E * D])).then_inc(s_b2, 16)
            w1_v = w1.rearrange("e (h p) f -> e p h f", p=P)
            w2_v = w2.rearrange("e (f p) d -> e p f d", p=P)

            def load_weights(e):
                if e >= 1:
                    sp.wait_ge(s_wlow, 2 * e)
                sp.dma_start(w1s, w1_v[e]).then_inc(s_wl[0], 16)
                sp.dma_start(w2s, w2_v[e]).then_inc(s_wl[1], 16)

            sp.wait_ge(s_h, H * G)
            load_weights(0)
            sp.wait_ge(s_fillr, 1)
            sp.dma_start(buf_d.rearrange("(j p) c -> p j c", p=P),
                         fill.rearrange("p (o c) -> p o c", o=1).to_broadcast([P, E * SROW // P, CW])).then_inc(s_filled, 16)
            sp.wait_ge(s_x1, NT)
            sp.dma_start(out[0:full, :].rearrange("(a p) d -> p a d", p=P), comb[:, 0:NT - 1, D:2 * D]).then_inc(s_out0, 16)
            sp.dma_start(out[full:N_NODES, :], comb[0:TAIL, NT - 1, D:2 * D]).then_inc(s_out0, 16)
            buf_v = buf_d.rearrange("(e j p) c -> e p j c", p=P, j=4)

            def load_rows(e):
                if e >= 2:
                    sp.wait_ge(s_xbfree[e % 2], e // 2)
                sp.dma_start(xb[e % 2], buf_v[e]).then_inc(s_xb[e % 2], 16)

            load_weights(1)
            sp.wait_ge(s_disp, 16 * NT)
            load_rows(0)
            load_rows(1)
            for e in range(2, E):
                load_rows(e)
                load_weights(e)
            sp.wait_ge(s_out0, 32)
            sp.wait_ge(s_src, 16)

        @block.gpsimd
        def _(pool):
            g = nc.gpsimd
            n = [0]

            def step(ins):
                n[0] += 1
                ins.then_inc(pch, 1)

            def settle():
                pool.wait_ge(pch, n[0])

            g.memset(xn[:, NT - 1, :], 0.0).then_inc(s_const, 1)
            g.iota(iotaI, [[1, P]], base=0, channel_multiplier=0).then_inc(s_iota, 1)
            step(g.memset(ident[:, :], 0.0))
            step(g.memset(triH[:, :], 1.0))
            step(g.memset(ones[:, :], 1.0))
            step(g.memset(onesH[:, :], 1.0))
            step(g.iota(srcI[:, RCOLS:], [[ROWS, LOOPC]], base=0, channel_multiplier=1))
            step(g.iota(dstI[:, RCOLS:], [[ROWS, LOOPC]], base=0, channel_multiplier=1))
            step(g.iota(nodeI[:, :], [[P, NT]], base=0, channel_multiplier=1))
            step(g.iota(selfI[:, 0, :].rearrange("p (j r) -> p j r", r=WN), [[WN * ROWS, WB], [1, WN]], base=0,
                        channel_multiplier=WN))
            step(g.iota(wI[:, :], [[WN * ROWS, WB]], base=0, channel_multiplier=WN))
            step(g.memset(keyT[:, NW:WPAD], NOKEY))
            step(g.memset(lowT[:, NW:WPAD], NOKEY))
            settle()
            step(g.affine_select(out=ident[:, :], in_=ident[:, :], compare_op=ALU.not_equal, fill=1.0, base=0,
                                 pattern=[[-1, P]], channel_multiplier=1))
            step(g.affine_select(out=triH[:, :], in_=triH[:, :], compare_op=ALU.is_ge, fill=0.0, base=0,
                                 pattern=[[1, P]], channel_multiplier=-1))
            settle()
            g.memset(fb[:, 0:1], 1.0).then_inc(s_const, 1)
            pool.wait_ge(s_split, 2)
            for v in range(HI_POOL):
                ins = g.tensor_scalar(oh_hi[0:ROWS, v, :], hi16, float(v), None, ALU.is_equal)
                step(ins)
            settle()
            g.memset(fb[:, 1:2], 1.0).then_inc(s_ohhi, 1)
            pool.wait_ge(s_start, 1)
            for j in range(WB):
                g.indirect_dma_start(out=edges_s[0:ROWS, j, :], out_offset=None, in_=src_flat[:, 0:1],
                                     in_offset=bass.IndirectOffsetOnAxis(ap=wIdx[:, j:j + 1], axis=0),
                                     bounds_check=N_EDGES - 1, oob_is_err=False).then_inc(s_gs, 16)
                g.indirect_dma_start(out=edges_d[0:ROWS, j, :], out_offset=None, in_=dst_flat[:, 0:1],
                                     in_offset=bass.IndirectOffsetOnAxis(ap=wIdx[:, j:j + 1], axis=0),
                                     bounds_check=N_EDGES - 1, oob_is_err=False).then_inc(s_gd, 16)
            pool.wait_ge(s_dx, 1)
            pool.wait_ge(s_ln, 1)
            for a in range(NT):
                g.tensor_scalar(xsf[a % 2], xn[:, a, :], dinvx[:, 0, a:a + 1], None, ALU.mult).then_inc(s_xsf, 1)
                pool.wait_ge(s_xsf, a + 1)
                pool.wait_ge(s_hi, a + 1)
                g.tensor_tensor(xs[:, a, D:2 * D], xsf[a % 2], xs[:, a, 0:D], ALU.subtract).then_inc(s_lo, 1)
            pool.wait_ge(s_flag, 1)
            fast = pool.value_load(flagI[0:1, 0:1], min_val=0, max_val=1)
            for gr in range(G + 2):
                if gr < G:
                    with pool.If(fast == 1):
                        pool.nop()
                    with pool.Else():
                        if gr == 0:
                            g.iota(io480, [[1, GN]], base=0, channel_multiplier=0,
                                   allow_small_or_imprecise_dtypes=True).then_inc(s_io480, 1)
                            pool.wait_ge(s_lo, NT)
                            pool.wait_ge(s_src, 16)
                            g.dma_start(xs_d.rearrange("(a p) d -> p a d", p=P), xs).then_inc(s_tab, 16)
                            pool.wait_ge(s_tab, 16)
                        NC = RCOLS + LOOPC
                        with pool.Fori(0, NC) as c:
                            pool.wait_ge(s_gmm, c + gr * NC)
                            pool.sem_inc(s_ptick, 1)
                            g.tensor_copy(idxc[:, :], srcI[:, bass.ds(c, 1)]).then_inc(s_gidx, 1)
                            pool.wait_ge(s_gidx, c + (gr * NC + 1))
                            pool.sem_inc(s_ptick, 1)
                            g.indirect_dma_start(out=gath[0:ROWS, :], out_offset=None, in_=xs_d,
                                                 in_offset=bass.IndirectOffsetOnAxis(ap=idxc[:, 0:1], axis=0),
                                                 bounds_check=NPAD - 1, oob_is_err=False).then_inc(s_grow, 16)
                q = gr - 1
                if 0 <= q < G:
                    nn = GN if q < G - 1 else LASTN
                    pool.wait_ge(s_z, H * (q + 1))
                    pool.wait_ge(s_linc, H * 7)
                    if q >= 1:
                        pool.wait_ge(s_h, H * q)
                    for h in range(H):
                        g.tensor_tensor(mT[:, h, 0:nn], zT[q % 2][:, h, 0:nn],
                                        XL[:, h, GN * q:GN * q + nn], ALU.subtract).then_inc(s_zx, 1)
                    for h in range(H):
                        pool.wait_ge(s_zx, H * q + h + 1)
                        pool.wait_ge(s_g, H * q + h + 1)
                        g.tensor_tensor(mT[:, h, 0:nn], mT[:, h, 0:nn], gT[:, h, 0:nn], ALU.mult).then_inc(s_diff, 1)
            pool.wait_ge(s_agg, G)
            g.memset(comb[:, NT - 1, D:2 * D], 0.0).then_inc(s_const, 1)

            def weights_split(e, k):
                full, (high, low) = (w1s, w1r[e % 2]) if k == 0 else (w2s, w2r[e % 2])
                pool.wait_ge(s_wh, 2 * e + k + 1)
                g.tensor_tensor(low, full, high.bitcast(F32), ALU.subtract).then_inc(s_wlow, 1)

            weights_split(0, 0)
            weights_split(0, 1)
            pool.wait_ge(s_slot, 1)
            pool.wait_ge(s_filled, 16)
            for a in range(NT):
                g.indirect_dma_start(out=buf_d, out_offset=bass.IndirectOffsetOnAxis(ap=slotI[:, a:a + 1], axis=0),
                                     in_=comb[:, a, :], in_offset=None,
                                     bounds_check=E * SROW - 1, oob_is_err=False).then_inc(s_disp, 16)
            pool.wait_ge(s_out0, 32)
            for e in range(E):
                u = e % 2
                for j in range(4):
                    if e + 1 < E and j % 2 == 0:
                        weights_split(e + 1, j // 2)
                    pool.wait_ge(s_y, 4 * e + j + 1)
                    g.indirect_dma_start(out=out, out_offset=bass.IndirectOffsetOnAxis(ap=tokI[u][:, j:j + 1], axis=0),
                                         in_=yt[u][:, j, :], in_offset=None,
                                         bounds_check=N_NODES - 1, oob_is_err=False).then_inc(s_outs[u], 16)
            for u in range(2):
                pool.wait_ge(s_outs[u], 16 * 4 * E // 2)

        @block.vector
        def _(dve):
            v = nc.vector
            n = [0]

            def step(ins):
                n[0] += 1
                ins.then_inc(dch, 1)

            def settle():
                dve.wait_ge(dch, n[0])

            def link(ins):
                step(ins)
                settle()

            dve.wait_ge(s_iota, 1)
            link(v.tensor_copy(iotaH[:, :], iotaI))
            dve.wait_ge(s_dst, 16)
            step(v.tensor_single_scalar(tmpI, dstI[:, 0:RCOLS], P - 1, ALU.bitwise_and))
            step(v.tensor_single_scalar(tmpI2, dstI[:, 0:RCOLS], 7, ALU.arith_shift_right))
            settle()
            v.tensor_copy(hi16, tmpI2).then_inc(s_split, 1)
            v.tensor_copy(lo16, tmpI).then_inc(s_split, 1)
            dve.wait_ge(s_split, 2)
            for k in range(P):
                step(v.tensor_scalar(oh_lo[0:ROWS, k, :], lo16, float(k), None, ALU.is_equal))
            for k in range(HI_POOL, NT):
                step(v.tensor_scalar(oh_hi[0:ROWS, k, :], hi16, float(k), None, ALU.is_equal))
            settle()
            v.memset(fb[:, 2:3], 1.0).then_inc(s_ohlo, 1)

            def rsqrt(width, mark):
                val, sq, r, t = [rs[:, k, 0:width] for k in range(4)]
                settle()
                v.memset(fb[:, 3:4], 0.0).then_inc(s_sqi, 1)
                dve.wait_ge(s_sq, mark)
                link(v.reciprocal(r, sq))
                link(v.tensor_tensor(t, r, r, ALU.mult))
                link(v.tensor_tensor(t, t, val, ALU.mult))
                link(v.tensor_scalar(t, t, -0.5, 1.5, ALU.mult, ALU.add))
                link(v.tensor_tensor(r, r, t, ALU.mult))
                return r

            dve.wait_ge(s_x, 32)
            for a in range(NT):
                step(v.bn_stats(stats[:, a, :], xn[:, a, :]))
            settle()
            for a in range(NT):
                step(v.bn_aggr(mv[:, a, :], stats[:, a, :]))
            settle()
            dve.wait_ge(s_const, 2)
            dve.wait_ge(s_hist, 1)
            link(v.tensor_copy(degR[:, :], PS[0][:, 0:NT]))

            def spread(vec, done):
                for q in range(7):
                    m = min(4, NT - 4 * q)
                    if done + q >= 4:
                        dve.wait_ge(s_bc, done + q - 3)
                    v.tensor_tensor(diag[(done + q) % 4][:, 0:m, :], ident[:, :].unsqueeze(1).to_broadcast([P, m, P]),
                                    vec[:, 4 * q:4 * q + m].unsqueeze(2).to_broadcast([P, m, P]),
                                    ALU.mult).then_inc(s_diag, 1)

            spread(degR, 0)
            link(v.tensor_scalar(rs[:, 0, :], mv[:, :, 1], LN_EPS, None, ALU.add))
            r = rsqrt(NT, 1)
            step(v.memset(cs[:, 0:1], 0.0))
            dve.wait_ge(s_bcc, 7)
            link(v.tensor_reduce(cs[:, 1:NW + 1], degB[:, 0:N_NODES].rearrange("p (w r) -> p w r", r=WN),
                                 AX.X, ALU.add))
            link(v.tensor_tensor_scan(degB[:, 0:NW], cs[:, 0:NW], cs[:, 0:NW], 0.0, ALU.add, ALU.max))
            pick = XL[0:ROWS, 1, 700:700 + NW].rearrange("p (j w) -> p j w", w=ROWS)
            link(v.tensor_tensor(pick, degB[0:ROWS, 0:NW].rearrange("p (j w) -> p j w", w=ROWS),
                                 ident[0:ROWS, 0:ROWS].unsqueeze(1).to_broadcast([ROWS, WB, ROWS]), ALU.mult))
            link(v.tensor_reduce(wF[:, 0, :], pick, AX.X, ALU.add))
            link(v.tensor_scalar(wF[:, 0, :], wF[:, 0, :], float(N_EDGES - SLOTS), None, ALU.min))
            v.tensor_copy(wIdx[:, :], wF[:, 0, :]).then_inc(s_start, 1)
            for a in range(NT):
                step(v.tensor_scalar(xn[:, a, :], xn[:, a, :], mv[:, a, 0:1], r[:, a:a + 1], ALU.subtract, ALU.mult))
            settle()
            v.memset(fb[:, 3:4], 0.0).then_inc(s_ln, 1)
            link(v.tensor_scalar(rs[:, 0, :], degR[:, :], 1.0, None, ALU.add))
            r = rsqrt(NT, 2)
            link(v.tensor_scalar(dinvx[:, 0, :], r, XSC, None, ALU.mult))
            link(v.tensor_scalar(dinvx[:, 1, :], r, 1.0 / XSC, None, ALU.mult))
            v.memset(fb[:, 3:4], 0.0).then_inc(s_dx, 1)
            spread(dinvx[:, 1, :], 7)
            so = WB * WN
            step(v.tensor_single_scalar(selfI[:, 1, :], selfI[:, 0, :], P - 1, ALU.bitwise_and))
            step(v.tensor_single_scalar(selfI[:, 2, :], selfI[:, 0, :], 7, ALU.arith_shift_right))
            settle()
            low, high, dl, t0, valid, key = keyw
            self3 = lambda k: selfI[:, k, :].rearrange("p (j r) -> p j r", r=WN)
            step(v.tensor_copy(low[0:ROWS, :, SLOTS:P], self3(1)))
            step(v.tensor_copy(high[0:ROWS, :, SLOTS:P], self3(2)))
            step(v.tensor_copy(wF[:, 1, :], wI[:, :]))
            settle()
            first = wF[:, 1, :].unsqueeze(2)
            step(v.tensor_tensor(dl[0:ROWS, :, SLOTS:P], self3(0), first.to_broadcast([ROWS, WB, WN]), ALU.subtract))
            settle()
            step(v.scalar_tensor_tensor(key[0:ROWS, :, SLOTS:P], high[0:ROWS, :, SLOTS:P], float(WN),
                                        dl[0:ROWS, :, SLOTS:P], ALU.mult, ALU.add))
            S = slice(0, SLOTS)
            dve.wait_ge(s_gs, 16 * WB)
            dve.wait_ge(s_gd, 16 * WB)
            eI = [at(42048 + 2464 * k, WB * SLOTS, I32)[0:ROWS].rearrange("p (j s) -> p j s", s=SLOTS) for k in range(2)]
            es, ed = edges_s[0:ROWS], edges_d[0:ROWS]
            step(v.tensor_single_scalar(eI[0], es, P - 1, ALU.bitwise_and))
            step(v.tensor_single_scalar(eI[1], es, 7, ALU.arith_shift_right))
            step(v.tensor_tensor(dl[0:ROWS, :, S], ed, first.to_broadcast([ROWS, WB, SLOTS]), ALU.subtract))
            settle()
            step(v.tensor_copy(low[0:ROWS, :, S], eI[0]))
            step(v.tensor_copy(high[0:ROWS, :, S], eI[1]))
            step(v.tensor_scalar(t0[0:ROWS, :, S], dl[0:ROWS, :, S], 0.0, None, ALU.is_ge))
            settle()
            step(v.scalar_tensor_tensor(valid[0:ROWS, :, S], dl[0:ROWS, :, S], float(WN), t0[0:ROWS, :, S],
                                        ALU.is_lt, ALU.mult))
            step(v.scalar_tensor_tensor(key[0:ROWS, :, S], high[0:ROWS, :, S], float(WN), dl[0:ROWS, :, S],
                                        ALU.mult, ALU.add))
            settle()
            step(v.scalar_tensor_tensor(key[0:ROWS, :, S], key[0:ROWS, :, S], -NOKEY, valid[0:ROWS, :, S],
                                        ALU.add, ALU.mult))
            link(v.tensor_reduce(fb[0:ROWS, 0:1], valid[0:ROWS, :, S], AX.XY, ALU.add))
            link(v.tensor_scalar(key[0:ROWS, :, S], key[0:ROWS, :, S], NOKEY, None, ALU.add))
            v.memset(fb[:, 3:4], 0.0).then_inc(s_key, 1)
            dve.wait_ge(s_cnt, 1)
            link(v.tensor_scalar(flagF[:, :], PS[1][0:1, 0:1], float(N_EDGES), None, ALU.is_equal))
            v.tensor_copy(flagI[:, :], flagF[:, :]).then_inc(s_flag, 1)
            dve.wait_ge(s_flag, 1)
            fast = dve.value_load(flagI[0:1, 0:1], min_val=0, max_val=1)
            dve.wait_ge(s_keyc, 4)

            def onehot_group(gr):
                for k in range((GI if gr < G - 1 else LASTI) // 2):
                    pair = gr * GI // 2 + k
                    w = 8 * pair
                    if pair >= 2:
                        dve.wait_ge(s_bld, 2 * (pair - 1))
                    v.tensor_tensor(ohb[pair % 2], iotaH[:, :].unsqueeze(1).to_broadcast([P, 8, P]),
                                    lowT[:, w:w + 8].unsqueeze(2).to_broadcast([P, 8, P]), ALU.is_equal)
                    v.tensor_tensor(ohk[pair % 2], iotaH[:, 0:KEYS].unsqueeze(1).to_broadcast([P, 8, KEYS]),
                                    keyT[:, w:w + 8].unsqueeze(2).to_broadcast([P, 8, KEYS]),
                                    ALU.is_equal).then_inc(s_oh, 1)

            for gr in range(-1, G + 2):
                if gr + 1 < G:
                    with dve.If(fast == 1):
                        onehot_group(gr + 1)
                    with dve.Else():
                        dve.nop()
                if 0 <= gr < G:
                    with dve.If(fast == 1):
                        dve.nop()
                    with dve.Else():
                        if gr == 0:
                            dve.wait_ge(s_io480, 1)
                        NC = RCOLS + LOOPC
                        with dve.Fori(0, NC) as c:
                            dve.wait_ge(s_gmm, c + gr * NC)
                            v.tensor_scalar(dcol[:, :], dstI[:, bass.ds(c, 1)], float(-GN * gr), None,
                                            ALU.add).then_inc(s_dcol, 1)
                            dve.wait_ge(s_dcol, c + (gr * NC + 1))
                            v.tensor_scalar(dsel[0:ROWS, :], io480[0:ROWS, :], dcol[:, 0:1], None,
                                            ALU.is_equal).then_inc(s_sel, 1)
                q = gr - 2
                if 0 <= q < G:
                    nn = GN if q < G - 1 else LASTN
                    nv = min(GN, N_NODES - GN * q)
                    for h in range(H):
                        dve.wait_ge(s_diff, H * q + h + 1)
                        hx = XL[:, h, GN * q:GN * q + nn]
                        link(v.tensor_tensor(mT[:, h, 0:nn], mT[:, h, 0:nn], hx, ALU.add))
                        v.tensor_scalar(hx, mT[:, h, 0:nn], 0.0, None, ALU.max).then_inc(s_h, 1)
                        dve.wait_ge(s_h, H * q + h + 1)
                        step(v.bn_stats(bnst[:, h, q, :], XL[:, h, GN * q:GN * q + nv]))
                if 0 <= gr < G:
                    nn = GN if gr < G - 1 else LASTN
                    dve.wait_ge(s_agg, gr + 1)
                    if gr >= 2:
                        dve.wait_ge(s_gcn, gr - 1)
                    for h in range(H):
                        ins = v.tensor_tensor(aggT[gr % 2][:, h, 0:nn], PS[2 + 2 * (gr % 2) + h][:, 0:nn],
                                              DB[:, GN * gr:GN * gr + nn], ALU.mult)
                        if h == 0:
                            step(ins)
                    ins.then_inc(s_aggc, 1)
            settle()
            for h in range(H):
                step(v.bn_aggr(bnmv[:, h, :], bnst[:, h, :, :].rearrange("p g s -> p (g s)")))
            settle()
            link(v.tensor_scalar(rs[:, 0, 0:H], bnmv[:, :, 1], BN_EPS, None, ALU.add))
            r = rsqrt(H, 3)
            nb = E * F // P
            gamma, beta = VT[:, nb + 6:nb + 8], VT[:, nb + 8:nb + 10]
            link(v.tensor_tensor(bnc[:, 0, :], r, gamma, ALU.mult))
            link(v.tensor_tensor(bnc[:, 1, :], bnmv[:, :, 0], bnc[:, 0, :], ALU.mult))
            link(v.tensor_tensor(bnc[:, 2, :], beta, bnc[:, 1, :], ALU.subtract))
            for h in range(H):
                step(v.tensor_scalar(XL[:, h, :], XL[:, h, :], bnc[:, 0, h:h + 1], bnc[:, 2, h:h + 1],
                                     ALU.mult, ALU.add))
            settle()
            v.memset(fb[:, 3:4], 0.0).then_inc(s_bn, 1)
            dve.wait_ge(s_x2, 32)
            for a in range(NT):
                x1 = comb[:, a, D:2 * D]
                dve.wait_ge(s_yT, a + 1)
                v.tensor_tensor(x1, PS[a % 4][:, 0:D], x1, ALU.add).then_inc(s_x1, 1)
                dve.wait_ge(s_x1, a + 1)
                step(v.bn_stats(stats[:, a, :], x1))
            settle()
            for a in range(NT):
                step(v.bn_aggr(mv[:, a, :], stats[:, a, :]))
            settle()
            link(v.tensor_scalar(rs[:, 0, :], mv[:, :, 1], LN_EPS, None, ALU.add))
            r = rsqrt(NT, 4)
            for a in range(NT):
                v.tensor_scalar(comb[:, a, 0:D], comb[:, a, D:2 * D], mv[:, a, 0:1], r[:, a:a + 1],
                                ALU.subtract, ALU.mult).then_inc(s_xn2, 1)
            step(v.memset(fill[:, 0:CW - 1], 0.0))
            step(v.memset(fill[:, CW - 1:CW], NOROW))
            step(v.tensor_copy(rc(0), nodeI[:, :]))
            step(v.tensor_copy(iota8[:, :], iotaH[:, 0:E]))
            settle()
            v.memset(fb[:, 3:4], 0.0).then_inc(s_fillr, 1)
            node, live = rc(0), rc(1)
            link(v.tensor_scalar(live, node, float(N_NODES), None, ALU.is_lt))

            def over(vec):
                return vec.unsqueeze(2).to_broadcast([P, NT, E])

            L, ex, pr, eq = rt(0), rt(1), rt(2), rt(3)
            iota_b = iota8[:, :].unsqueeze(1).to_broadcast([P, NT, E])
            dve.wait_ge(s_fg, 32)
            dve.wait_ge(s_log, 1)
            link(v.tensor_tensor(L, PS[4][:, 0:NT * E].rearrange("p (a e) -> p a e", e=E),
                                 fgb[:, :].unsqueeze(1).to_broadcast([P, NT, E]), ALU.add))
            link(v.tensor_reduce(rc(2), L, AX.X, ALU.max))
            v.tensor_tensor(L, L, over(rc(2)), ALU.subtract).then_inc(s_expi, 1)
            dve.wait_ge(s_exp, 1)
            link(v.tensor_reduce(rc(3), ex, AX.X, ALU.add))
            link(v.reciprocal(rc(3), rc(3)))
            link(v.tensor_tensor(pr, ex, over(rc(3)), ALU.mult))
            link(v.tensor_reduce(rc(4), pr, AX.X, ALU.max))
            link(v.tensor_tensor(eq, pr, over(rc(4)), ALU.is_equal))
            link(v.scalar_tensor_tensor(eq, eq, -float(E), iota_b, ALU.mult, ALU.add))
            link(v.tensor_reduce(rc(5), eq, AX.X, ALU.min))
            link(v.tensor_scalar(rc(5), rc(5), float(E), None, ALU.add))
            link(v.tensor_tensor(eq, iota_b, over(rc(5)), ALU.is_equal))
            link(v.tensor_tensor(eq, eq, over(live), ALU.mult))
            v.tensor_copy(ohH, eq).then_inc(s_ohr, 1)
            dve.wait_ge(s_pos, 1)
            tot, before = rt(4), rt(5)
            link(v.tensor_copy(tot, PS[6][:, 0:NT * E].rearrange("p (a e) -> p a e", e=E)))
            step(v.memset(before[:, 0:1, :], 0.0))
            for e in range(E):
                step(v.tensor_tensor_scan(before[:, 1:NT, e], tot[:, 0:NT - 1, e], tot[:, 0:NT - 1, e], 0.0,
                                          ALU.add, ALU.max))
            settle()
            link(v.tensor_tensor(before, PS[5][:, 0:NT * E].rearrange("p (a e) -> p a e", e=E), before, ALU.add))
            link(v.tensor_tensor(before, before, eq, ALU.mult))
            link(v.tensor_reduce(rc(6), before, AX.X, ALU.add))
            link(v.tensor_scalar(rc(6), rc(6), -1.0, None, ALU.add))
            link(v.tensor_scalar(rc(7), rc(6), float(CAP), None, ALU.is_lt))
            link(v.tensor_tensor(rc(7), rc(7), live, ALU.mult))
            link(v.scalar_tensor_tensor(rc(6), rc(5), float(SROW), rc(6), ALU.mult, ALU.add))
            link(v.scalar_tensor_tensor(rc(6), rc(6), -NOROW, rc(7), ALU.add, ALU.mult))
            link(v.tensor_scalar(rc(6), rc(6), NOROW, None, ALU.add))
            step(v.tensor_copy(comb[:, :, 2 * D], rc(4)))
            step(v.tensor_copy(comb[:, :, 2 * D + 1], node))
            settle()
            v.tensor_copy(slotI[:, :], rc(6)).then_inc(s_slot, 1)

            dve.wait_ge(s_b2, 16)
            step(v.memset(zero_y, 0.0))
            settle()

            dve.wait_ge(s_disp, 16 * NT)
            dve.wait_ge(s_out0, 32)
            for part in range(2):
                v.memset(hidr[part][:, :, CAPE:512].bitcast(F32), 0.0).then_inc(s_pad, 1)

            def rows_low(e):
                for h in range(H):
                    dve.wait_ge(s_xbh, H * e + h + 1)
                    v.tensor_tensor(xbTr[e % 2][1][:, h, :], PS[h][:, :], xbTr[e % 2][0][:, h, :].bitcast(F32),
                                    ALU.subtract).then_inc(s_xbl, 1)

            rows_low(0)
            for e in range(E):
                u = e % 2
                for f in range(8):
                    dve.wait_ge(s_hidh, 8 * e + f + 1)
                    if e >= 1 and f == 0:
                        dve.wait_ge(s_down, 4 * e)
                    v.tensor_tensor(hidr[1][:, f, 0:CAPE], hidf[:, f, :], hidr[0][:, f, 0:CAPE].bitcast(F32),
                                    ALU.subtract).then_inc(s_hidl, 1)
                if e + 1 < E:
                    rows_low(e + 1)
                if e >= 2:
                    dve.wait_ge(s_outs[u], 16 * 4 * (e // 2))
                dve.wait_ge(s_xb[u], 16 * (e // 2 + 1))
                link(v.tensor_copy(tokI[u][:, :], xb[u][:, :, 2 * D + 1]))
                for j in range(4):
                    m = min(P, CAP - P * j)
                    y, t, mask = yt[u][:, j, :], tmp_y, tmp_m.bitcast(I32)
                    if m < P:
                        step(v.memset(y, 0.0))
                    dve.wait_ge(s_down, 4 * e + j + 1)
                    link(v.tensor_tensor(t[0:m], PS[4 + j][0:m, 0:D], b2B[0:m, e, :], ALU.add))
                    link(v.tensor_scalar(t[0:m], t[0:m], xb[u][0:m, j, 2 * D:2 * D + 1], None, ALU.mult))
                    step(v.tensor_scalar(y[0:m], t[0:m], POSINF, -POSINF, ALU.min, ALU.max))
                    link(v.tensor_scalar(mask[0:m], t[0:m], 0.0, 0.0, ALU.mult, ALU.is_equal))
                    link(v.copy_predicated(y[0:m], mask[0:m], t[0:m]))
                    link(v.tensor_tensor(mask[0:m], t[0:m], t[0:m], ALU.not_equal))
                    link(v.copy_predicated(y[0:m], mask[0:m], zero_y[0:m]))
                    ins = v.tensor_tensor(y[0:m], y[0:m], xb[u][0:m, j, D:2 * D], ALU.add)
                    ins.then_inc(s_y, 1)
                dve.wait_ge(s_y, 4 * e + 4)
                v.memset(fb[:, 3:4], 0.0).then_inc(s_xbfree[u], 1)

        @block.scalar
        def _(act):
            s = nc.scalar

            def root(mark, width):
                act.wait_ge(s_sqi, mark)
                s.activation(rs[:, 1, 0:width], rs[:, 0, 0:width], ACT.Sqrt).then_inc(s_sq, 1)

            nb = E * F // P
            gcnb, linb, gateb = (VT[:, nb + 2 * k:nb + 2 * k + 2] for k in range(3))
            root(1, NT)
            act.wait_ge(s_vT, 1)
            s.activation(VT[:, :], PS[7][:, 0:nb + 10], ACT.Copy).then_inc(s_vTc, 1)
            def spread_copied(to, done):
                for q in range(7):
                    n = min(512, NPAD - 512 * q)
                    act.wait_ge(s_bc, done + q + 1)
                    s.activation(to[:, 512 * q:512 * q + n], PS[(done + q) % 4][:, 0:n], ACT.Copy).then_inc(s_bcc, 1)

            def lin_copied(q):
                n = min(512, NPAD - 512 * q)
                act.wait_ge(s_lin, q + 1)
                for h in range(H):
                    s.activation(XL[:, h, 512 * q:512 * q + n], PS[6 + h][:, 0:n], ACT.Identity,
                                 bias=linb[:, h:h + 1]).then_inc(s_linc, 1)

            def ln_copied(q):
                n = min(512, NPAD - 512 * q)
                act.wait_ge(s_lnt, q + 1)
                for h in range(H):
                    s.activation(lnT[q % 2][:, h, 0:n], PS[4 + h][:, 0:n], ACT.Copy).then_inc(s_lnc, 1)

            spread_copied(degB, 0)
            root(2, NT)
            spread_copied(DB, 7)
            act.wait_ge(s_dx, 1)
            act.wait_ge(s_ln, 1)
            for a in range(NT):
                s.activation(xs[:, a, 0:D], xn[:, a, :], ACT.Copy, scale=dinvx[:, 0, a:a + 1]).then_inc(s_hi, 1)
            act.wait_ge(s_vTc, 1)
            ln_copied(0)
            for q in range(LIN_EARLY):
                ln_copied(q + 1)
                lin_copied(q)
            for k, to in enumerate((lowT, keyT)):
                act.wait_ge(s_keyp, 2 * k + 1)
                s.activation(to[:, 0:500], PS[2 * k][:, 0:500], ACT.Copy).then_inc(s_keyc, 1)
                act.wait_ge(s_keyp, 2 * k + 2)
                s.activation(to[:, 500:NW], PS[1 + 2 * k][:, 0:ROWS], ACT.Copy).then_inc(s_keyc, 1)
            act.wait_ge(s_flag, 1)
            fast = act.value_load(flagI[0:1, 0:1], min_val=0, max_val=1)

            def copy_built(gr, i):
                act.wait_ge(s_bld, GI * gr + i + 1)
                s.activation(A[gr % 2][:, :, 20 * i:20 * (i + 1)].rearrange("p a (w d) -> p w a d", d=WN),
                             PS[i % 2][:, 0:4 * KEYS].rearrange("p (w a d) -> p w a d", w=4, d=WN),
                             ACT.Copy).then_inc(s_ev, 1)

            def copy_group(gr):
                if gr >= 2:
                    act.wait_ge(s_agg, gr - 1)
                for i in range(GI if gr < G - 1 else LASTI):
                    copy_built(gr, i)

            with act.If(fast == 1):
                for i in range(GI):
                    copy_built(0, i)
                    if i % 6 == 5:
                        q = LIN_EARLY + i // 6
                        if q + 1 < 7:
                            ln_copied(q + 1)
                        lin_copied(q)
            with act.Else():
                for q in range(LIN_EARLY, 7):
                    if q + 1 < 7:
                        ln_copied(q + 1)
                    lin_copied(q)

            for gr in range(0, G + 1):
                if gr + 1 < G:
                    with act.If(fast == 1):
                        copy_group(gr + 1)
                    with act.Else():
                        act.nop()
                q = gr - 1
                if 0 <= q < G:
                    nn = GN if q < G - 1 else LASTN
                    for h in range(H):
                        act.wait_ge(s_gcn, q + 1)
                        s.activation(zT[q % 2][:, h, 0:nn], PS[6 + h][:, 0:nn], ACT.Tanh,
                                     bias=gcnb[:, h:h + 1]).then_inc(s_z, 1)
                q = gr - 1
                if 0 <= q < G:
                    nn = GN if q < G - 1 else LASTN
                    act.wait_ge(s_gate, q + 1)
                    if q >= 1:
                        act.wait_ge(s_h, H * q)
                    for h in range(H):
                        s.activation(gT[:, h, 0:nn], PS[6 + h][:, 0:nn], ACT.Sigmoid,
                                     bias=gateb[:, h:h + 1]).then_inc(s_g, 1)
            def weights_high(e):
                for k, (full, to) in enumerate(((w1s, w1r[e % 2][0]), (w2s, w2r[e % 2][0]))):
                    act.wait_ge(s_wl[k], 16 * (e + 1))
                    if e >= 2 and k == 0:
                        act.wait_ge(s_down, 4 * (e - 1))
                    s.activation(to, full, ACT.Copy).then_inc(s_wh, 1)

            root(3, H)
            weights_high(0)
            root(4, NT)
            for q in range(7):
                n = min(512, NPAD - 512 * q)
                act.wait_ge(s_xnp, q + 1)
                for h in range(H):
                    s.activation(xnT[q % 2][:, h, 0:n], PS[2 * (q % 2) + h][:, 0:n], ACT.Copy).then_inc(s_xnc, 1)
            act.wait_ge(s_expi, 1)
            s.activation(rt(1), rt(0), ACT.Exp).then_inc(s_exp, 1)

            def rows_high(e):
                act.wait_ge(s_xbp, e + 1)
                for h in range(H):
                    s.activation(xbTr[e % 2][0][:, h, :], PS[h][:, :], ACT.Copy).then_inc(s_xbh, 1)

            rows_high(0)
            for e in range(E):
                for f in range(8):
                    act.wait_ge(s_up, 8 * e + f + 1)
                    if e >= 1:
                        act.wait_ge(s_hidl, 8 * (e - 1) + f + 1)
                    s.activation(hidf[:, f, :], PS[2 + f % 2][:, 0:CAPE], ACT.Relu,
                                 bias=VT[:, 8 * e + f:8 * e + f + 1]).then_inc(s_hidf, 1)
                    act.wait_ge(s_hidf, 8 * e + f + 1)
                    if e >= 1 and f == 0:
                        act.wait_ge(s_down, 4 * e)
                    s.activation(hidr[0][:, f, 0:CAPE], hidf[:, f, :], ACT.Copy).then_inc(s_hidh, 1)
                if e + 1 < E:
                    rows_high(e + 1)
                    weights_high(e + 1)

        @block.tensor
        def _(pe):
            t = nc.tensor
            pe.wait_ge(s_const, 2)
            nb = E * F // P + 10
            pe.wait_ge(s_vec, 16 * 6)
            t.transpose(PS[7][:, 0:nb], VR[:, :], ident[0:nb, 0:nb]).then_inc(s_vT, 1)
            pe.wait_ge(s_ohlo, 1)
            pe.wait_ge(s_ohhi, 1)
            for c in range(RCOLS):
                ins = t.matmul(PS[0][:, 0:NT], oh_lo[0:ROWS, :, c], oh_hi[0:ROWS, :, c], start=(c == 0),
                               stop=(c == RCOLS - 1))
            ins.then_inc(s_hist, 1)

            def spread(done):
                for k in range(done, done + 7):
                    m = min(4, NT - 4 * (k % 7))
                    pe.wait_ge(s_diag, k + 1)
                    if k >= 4:
                        pe.wait_ge(s_bcc, k - 3)
                    t.matmul(PS[k % 4][:, 0:P * m], ones[:, :], diag[k % 4][:, 0:m, :].rearrange("p q n -> p (q n)"),
                             start=True, stop=True).then_inc(s_bc, 1)

            def ln_transposed(q):
                if q >= 1:
                    pe.wait_ge(s_lnc, H * q)
                for h in range(H):
                    for a in range(min(4, NT - 4 * q)):
                        ins = t.transpose(PS[4 + h][:, P * a:P * (a + 1)], xn[:, 4 * q + a, P * h:P * (h + 1)], ident[:, :])
                ins.then_inc(s_lnt, 1)

            def lin(q):
                pe.wait_ge(s_lnc, H * (q + 1))
                if q + 1 < 7:
                    ln_transposed(q + 1)
                if q >= 1:
                    pe.wait_ge(s_linc, H * q)
                n = P * min(4, NT - 4 * q)
                for h in range(H):
                    for k in range(H):
                        ins = t.matmul(PS[6 + h][:, 0:n], linW[:, k, P * h:P * (h + 1)], lnT[q % 2][:, k, 0:n],
                                       start=(k == 0), stop=(k == H - 1))
                ins.then_inc(s_lin, 1)

            spread(0)
            spread(7)
            pe.wait_ge(s_w, 48)
            pe.wait_ge(s_ln, 1)
            ln_transposed(0)
            for q in range(LIN_EARLY):
                lin(q)
            pe.wait_ge(s_key, 1)
            pe.wait_ge(s_bcc, 14)
            low, key = keyw[0], keyw[5]
            for k, w in enumerate((low, key)):
                for j in range(WB):
                    to = PS[2 * k][:, ROWS * j:ROWS * (j + 1)] if j < 4 else PS[1 + 2 * k][:, 0:ROWS]
                    ins = t.transpose(to, w[0:ROWS, j, :], ident[0:ROWS, 0:ROWS])
                    if j >= 3:
                        ins.then_inc(s_keyp, 1)
            pe.wait_ge(s_keyc, 4)
            t.matmul(PS[1][0:1, 0:1], fb[0:ROWS, 0:1], ones[0:ROWS, 0:1], start=True, stop=True).then_inc(s_cnt, 1)
            pe.wait_ge(s_flag, 1)
            fast = pe.value_load(flagI[0:1, 0:1], min_val=0, max_val=1)

            def build(gr, i):
                n = GI * gr + i
                pe.wait_ge(s_oh, n // 2 + 1)
                if n >= 2:
                    pe.wait_ge(s_ev, n - 1)
                for w in range(4):
                    ins = t.matmul(PS[n % 2][:, KEYS * w:KEYS * (w + 1)], ohb[n // 2 % 2][:, 4 * (n % 2) + w, :],
                                   ohk[n // 2 % 2][:, 4 * (n % 2) + w, :], start=True, stop=True)
                ins.then_inc(s_bld, 1)

            def aggregate(gr, a, start, stop):
                nn = GN if gr < G - 1 else LASTN
                for h in range(H):
                    for part in range(2):
                        first, last = start and part == 0, stop and part == 1
                        lo = D * part + P * h
                        ins = t.matmul(PS[2 + 2 * (gr % 2) + h][:, 0:nn], xs[:, a, lo:lo + P], A[gr % 2][:, a, 0:nn],
                                       start=first, stop=last)
                return ins

            def gcn(q):
                nn = GN if q < G - 1 else LASTN
                pe.wait_ge(s_aggc, q + 1)
                if q == 0:
                    pe.wait_ge(s_linc, H * 7)
                else:
                    pe.wait_ge(s_g, H * q)
                for h in range(H):
                    for k in range(H):
                        ins = t.matmul(PS[6 + h][:, 0:nn], gcnW[:, k, P * h:P * (h + 1)], aggT[q % 2][:, k, 0:nn],
                                       start=(k == 0), stop=(k == H - 1))
                ins.then_inc(s_gcn, 1)

            def gate(q):
                nn = GN if q < G - 1 else LASTN
                pe.wait_ge(s_z, H * (q + 1))
                for h in range(H):
                    for k in range(H):
                        ins = t.matmul(PS[6 + h][:, 0:nn], gateW[:, k, P * h:P * (h + 1)], zT[q % 2][:, k, 0:nn],
                                       start=(k == 0), stop=(k == H - 1))
                ins.then_inc(s_gate, 1)

            with pe.If(fast == 1):
                for i in range(GI):
                    build(0, i)
                    if i % 6 == 5:
                        lin(LIN_EARLY + i // 6)
            with pe.Else():
                for q in range(LIN_EARLY, 7):
                    lin(q)
            pe.wait_ge(s_lo, NT)
            for gr in range(G + 1):
                if gr < G:
                    nxt = gr + 1
                    nsteps = 0 if nxt >= G else GI if nxt < G - 1 else LASTI
                    if gr >= 2:
                        pe.wait_ge(s_aggc, gr - 1)
                    with pe.If(fast == 1):
                        pe.wait_ge(s_ev, GI * gr + (GI if gr < G - 1 else LASTI))
                        for a in range(NT):
                            if a < nsteps:
                                build(nxt, a)
                            ins = aggregate(gr, a, a == 0, a == NT - 1)
                        ins.then_inc(s_agg, 1)
                    with pe.Else():
                        NC = RCOLS + LOOPC
                        nn = GN if gr < G - 1 else LASTN

                        def general(c, at_row, at_sel, start, stop):
                            pe.wait_ge(s_grow, at_row)
                            pe.wait_ge(s_sel, at_sel)
                            for h in range(H):
                                for part in range(2):
                                    lo = D * part + P * h
                                    ins = t.matmul(PS[2 + 2 * (gr % 2) + h][:, 0:nn], gath[0:ROWS, lo:lo + P],
                                                   dsel[0:ROWS, 0:nn], start=start and part == 0, stop=stop and part == 1)
                            return ins

                        general(0, 16 * (gr * NC + 1), gr * NC + 1, True, False).then_inc(s_gmm, 1)
                        with pe.Fori(1, NC - 1) as c:
                            general(c, 16 * c + 16 * (gr * NC + 1), c + (gr * NC + 1), False, False).then_inc(s_gmm, 1)
                        general(NC - 1, 16 * (gr + 1) * NC, (gr + 1) * NC, False, True).then_inc(s_gmm, 1)
                        pe.wait_ge(s_gmm, (gr + 1) * NC)
                        t.matmul(PS[0][0:1, 0:1], ident[:, 0:1], ident[:, 0:1], start=True, stop=True).then_inc(s_agg, 1)
                q = gr - 1
                if 0 <= q < G:
                    gcn(q)
                    gate(q)
            pe.wait_ge(s_bn, 1)
            for a in range(NT):
                if a >= 4:
                    pe.wait_ge(s_x1, a - 3)
                for h in range(H):
                    ins = t.transpose(PS[a % 4][:, P * h:P * (h + 1)], XL[:, h, P * a:P * (a + 1)], ident[:, :])
                ins.then_inc(s_yT, 1)
            pe.wait_ge(s_fg, 32)
            pe.wait_ge(s_x1, NT)

            def logits(q):
                pe.wait_ge(s_xnc, H * (q + 1))
                for a in range(min(4, NT - 4 * q)):
                    for k in range(H):
                        ins = t.matmul(PS[4][:, E * (4 * q + a):E * (4 * q + a + 1)], xnT[q % 2][:, k, P * a:P * (a + 1)],
                                       fgw[:, k, :], start=(k == 0), stop=(k == H - 1))
                return ins

            for q in range(7):
                tiles = min(4, NT - 4 * q)
                pe.wait_ge(s_xn2, 4 * q + tiles)
                for h in range(H):
                    for a in range(tiles):
                        ins = t.transpose(PS[2 * (q % 2) + h][:, P * a:P * (a + 1)], comb[:, 4 * q + a, P * h:P * (h + 1)],
                                          ident[:, :])
                ins.then_inc(s_xnp, 1)
                if q >= 1:
                    logits(q - 1)
            logits(6).then_inc(s_log, 1)
            pe.wait_ge(s_ohr, 1)
            r = ohH.rearrange("p a e -> p (a e)")
            t.matmul(PS[5][:, 0:NT * E], triH[:, :], r, start=True, stop=True)
            t.matmul(PS[6][:, 0:NT * E], onesH[:, :], r, start=True, stop=True).then_inc(s_pos, 1)

            def rows_transposed(e):
                u = e % 2
                pe.wait_ge(s_xb[u], 16 * (e // 2 + 1))
                if e >= 1:
                    pe.wait_ge(s_xbl, H * e)
                for h in range(H):
                    for j in range(4):
                        ins = t.transpose(PS[h][:, P * j:P * (j + 1)], xb[u][:, j, P * h:P * (h + 1)], ident[:, :])
                ins.then_inc(s_xbp, 1)

            pe.wait_ge(s_pad, 2)
            rows_transposed(0)
            for e in range(E):
                u = e % 2
                pe.wait_ge(s_xbl, H * (e + 1))
                pe.wait_ge(s_wlow, 2 * e + 1)
                for f in range(8):
                    if 8 * e + f >= 2:
                        pe.wait_ge(s_hidf, 8 * e + f - 1)
                    ins = None
                    for k in range(H):
                        for part, (a, b) in enumerate(((0, 0), (0, 1), (1, 0))):
                            ins = t.matmul(PS[2 + f % 2][:, 0:CAPE], w1r[u][a][:, k, P * f:P * (f + 1)],
                                           xbTr[u][b][:, k, 0:CAPE],
                                           start=(k == 0 and part == 0), stop=(k == H - 1 and part == 2))
                    ins.then_inc(s_up, 1)
                if e + 1 < E:
                    rows_transposed(e + 1)
                pe.wait_ge(s_wlow, 2 * e + 2)
                for j in range(4):
                    if e >= 1:
                        pe.wait_ge(s_y, 4 * (e - 1) + j + 1)
                    for f in range(8):
                        if j == 0:
                            pe.wait_ge(s_hidl, 8 * e + f + 1)
                        for part, (a, b) in enumerate(((0, 0), (0, 1), (1, 0))):
                            ins = t.matmul(PS[4 + j][:, 0:D], hidr[a][:, f, P * j:P * (j + 1)],
                                           w2r[u][b][:, f, :],
                                           start=(f == 0 and part == 0), stop=(f == 7 and part == 2))
                    ins.then_inc(s_down, 1)


HI_POOL = 16
LIN_EARLY = 3

_INS = ["x", "src", "dst", "L0_gnn_gcn_W", "L0_gnn_gcn_b", "L0_gnn_lin_W", "L0_gnn_lin_b", "L0_gnn_gate_W",
        "L0_gnn_gate_b", "L0_gnn_bn_gamma", "L0_gnn_bn_beta", "L0_ffn_gate_w", "L0_ffn_gate_b", "L0_ffn_w1",
        "L0_ffn_b1", "L0_ffn_w2", "L0_ffn_b2"]


def kernel(**inputs):
    import numpy as np
    from concourse import bacc
    from concourse.bass_utils import run_bass_kernel_spmd

    nc = bacc.Bacc("TRN2", target_bir_lowering=False, num_devices=1)
    arrays, args = {}, []
    for name in _INS:
        a = np.ascontiguousarray(inputs[name])
        arrays[f"in_{name}"] = a
        args.append(nc.dram_tensor(f"in_{name}", a.shape, mybir.dt.from_np(a.dtype), kind="ExternalInput").ap())
    out = nc.dram_tensor("out", (N_NODES, D), F32, kind="ExternalOutput").ap()
    gnn_ffn(nc, *args, out)
    r = run_bass_kernel_spmd(nc, [arrays], core_ids=[0])
    return r.results[0]["out"]
```

```python
import concourse.bass as bass
from concourse import mybir
from contextlib import ExitStack

F32 = mybir.dt.float32
F32R = mybir.dt.float32r
F16 = mybir.dt.float16
I32 = mybir.dt.int32
ALU = mybir.AluOpType
ACT = mybir.ActivationFunctionType
AX = mybir.AxisListType

P = 128
N_NODES, N_EDGES, D = 3125, 50000, 256
E, F, CAP = 8, 1024, 489
LN_EPS = BN_EPS = 1e-5
H = D // P
NT = -(-N_NODES // P)
TAIL = N_NODES - (NT - 1) * P
NPAD = NT * P
ROWS, RCOLS = 125, 400
LOOPC = N_NODES // ROWS
WN = 5
NW = N_NODES // WN
WB = NW // ROWS
SLOTS = P - WN
KEYS = NT * WN
NOKEY = 1000.0
GI = 24
GW = 4 * GI
GN = GW * WN
G = -(-NW // GW)
LASTI = 2 * -(-(NW - (G - 1) * GW) // 8)
LASTN = LASTI * 4 * WN
WPAD = (G - 1) * GW + LASTI * 4
XSC = 64.0
SROW = 512
CAPE = CAP + CAP % 2
CW = 2 * D + 2
NOROW = 1.0e6
POSINF = 1.0e4



def gnn_ffn(nc, x, src, dst, gcn_W, gcn_b, lin_W, lin_b, gate_W, gate_b, bn_gamma, bn_beta,
            fgate_w, fgate_b, w1, b1, w2, b2, out):
    xs_d = nc.dram_tensor("xs_table", (NPAD, 2 * D), F16, kind="Internal").ap()
    buf_d = nc.dram_tensor("dispatch", (E * SROW, CW), F32, kind="Internal").ap()
    start_d = nc.dram_tensor("edge_starts", (NPAD,), F32, kind="Internal").ap()
    src_flat = src.rearrange("(n o) -> n o", o=1)
    dst_flat = dst.rearrange("(n o) -> n o", o=1)
    ctx = ExitStack()
    with ctx:
        def sb(name, shape, dt):
            return ctx.enter_context(nc.sbuf_tensor(name, shape, dt))

        def sem(name):
            return ctx.enter_context(nc.semaphore(name))

        XX_at = -(-nc.sbuf_base // 32) * 32
        XX = sb("XX", [P, NT * CW], F32)
        xn = XX[:, 0:NT * D].rearrange("p (a d) -> p a d", d=D)
        xs = XX[:, NT * D:2 * NT * D].bitcast(F16).rearrange("p (a d) -> p a d", d=2 * D)
        comb = XX[:, :].rearrange("p (a c) -> p a c", c=CW)
        XL = sb("XL", [P, H, NPAD], F32)
        DB = sb("DB", [P, NPAD], F32)
        R_at = -(-nc.sbuf_base // 32) * 32
        R = sb("R", [P, 51200], F16)

        def at(byte, n, dt):
            size = 2 if dt == F16 else 4
            v = R[:, byte // 2:(byte + n * size) // 2]
            return v if dt == F16 else v.bitcast(dt)

        oh_lo = at(0, P * RCOLS, F16).rearrange("p (v c) -> p v c", c=RCOLS)
        oh_hi = XX[:, NT * D:NT * D + NT * RCOLS // 2].bitcast(F16).rearrange("p (v c) -> p v c", c=RCOLS)
        A = [at(24000 * k, NT * GN, F16).rearrange("p (a n) -> p a n", n=GN) for k in range(2)]
        aggT = [at(60800 + 3840 * k, H * GN, F32).rearrange("p (h n) -> p h n", n=GN) for k in range(2)]
        zT = [at(68480 + 3840 * k, H * GN, F32).rearrange("p (h n) -> p h n", n=GN) for k in range(2)]
        gT = at(76160, H * GN, F32).rearrange("p (h n) -> p h n", n=GN)
        mT = at(80000, H * GN, F32).rearrange("p (h n) -> p h n", n=GN)
        keyw = [at(76160 + 2560 * k, WB * P, F32).rearrange("p (j s) -> p j s", s=P) for k in range(6)]
        diag = [at(30000 + 2048 * k, 4 * P, F32).rearrange("p (q n) -> p q n", n=P) for k in range(4)]
        ohb = [at(91520 + 2048 * k, 8 * P, F16).rearrange("p (w n) -> p w n", n=P) for k in range(2)]
        ohk = [at(95616 + 2000 * k, 8 * KEYS, F16).rearrange("p (w n) -> p w n", n=KEYS) for k in range(2)]
        ohb.append(at(87424, 8 * P, F16).rearrange("p (w n) -> p w n", n=P))
        ohk.append(at(89472, 8 * KEYS, F16).rearrange("p (w n) -> p w n", n=KEYS))
        lnT = [at(60800 + 4096 * k, H * 512, F32).rearrange("p (h n) -> p h n", n=512) for k in range(2)]
        xsf = [at(58000 + 1024 * k, D, F32) for k in range(2)]
        edges_s = at(24000, WB * SLOTS, I32).rearrange("p (j s) -> p j s", s=SLOTS)
        edges_d = at(26464, WB * SLOTS, I32).rearrange("p (j s) -> p j s", s=SLOTS)
        gath = at(0, 2 * D, F16)
        dsel = at(1024, GN, F16)
        io480 = at(2048, GN, F16)
        w1s = at(44416, H * F, F32).rearrange("p (h f) -> p h f", f=F)
        w2s = at(44416 + 8192, 8 * D, F32).rearrange("p (f d) -> p f d", d=D)
        w_r = [nc.alloc_sbuf_tensor_at(f"expert_weights_{n}", [P, 2, 2, 2048], F32R, offset=R_at + 60800 * k)
               for k, n in enumerate(("even", "odd"))]
        w1r = [[w_r[k][:, 0, part, :].rearrange("p (h f) -> p h f", f=F) for part in range(2)] for k in range(2)]
        w2r = [[w_r[k][:, 1, part, :].rearrange("p (f d) -> p f d", d=D) for part in range(2)] for k in range(2)]
        hid_r = nc.alloc_sbuf_tensor_at("expert_hidden", [P, 2, 8, 512], F32R, offset=XX_at)
        hidr = [hid_r[:, part] for part in range(2)]
        rows_r = nc.alloc_sbuf_tensor_at("expert_rows", [P, 2, 2, H, 512], F32R, offset=XX_at + 32768)
        xbTr = [[rows_r[:, k, part] for part in range(2)] for k in range(2)]
        xb = [at(93568 - 60800 * k, 4 * CW, F32).rearrange("p (j c) -> p j c", c=CW) for k in range(2)]
        xnT = [at(93568 + 4096 * k, H * 512, F32).rearrange("p (h s) -> p h s", s=512) for k in range(2)]
        xl_flat = XL[:, :, :].rearrange("p h n -> p (h n)")
        yt = [xl_flat[:, 1024 * k:1024 * (k + 1)].rearrange("p (j d) -> p j d", d=D) for k in range(2)]
        hidf = xl_flat[:, 2048:2048 + 8 * CAPE].rearrange("p (f s) -> p f s", s=CAPE)
        b2B = DB[:, 0:E * D].rearrange("p (e d) -> p e d", d=D)
        tmp_y = DB[:, E * D:E * D + D]
        tmp_m = DB[:, E * D + D:E * D + 2 * D]
        zero_y = DB[:, E * D + 2 * D:E * D + 3 * D]

        gcnW = sb("gcnW", [P, H, D], F32)
        linW = sb("linW", [P, H, D], F32)
        gateW = sb("gateW", [P, H, D], F32)
        ident = sb("ident", [P, P], F32)
        ones = sb("ones", [P, P], F32)
        onesH = sb("onesH", [P, P], F16)
        triH = sb("triH", [P, P], F16)
        iotaH = sb("iotaH", [P, P], F16)
        iotaI = R[:, 0:2 * P].bitcast(I32)
        srcI = sb("srcI", [ROWS, RCOLS + LOOPC], I32)
        dstI = sb("dstI", [ROWS, RCOLS + LOOPC], I32)
        lo16 = XL[0:ROWS, 0, 800:1000].bitcast(F16)
        hi16 = XL[0:ROWS, 0, 1000:1200].bitcast(F16)
        minus = XL[0:ROWS, 1, 0:LO_ACT]
        apart = [XL[0:ROWS, 1, 200 * (k + 1):200 * (k + 2)].bitcast(F16) for k in range(3)]
        tmpI = XL[0:ROWS, 0, 0:RCOLS].bitcast(I32)
        tmpI2 = XL[0:ROWS, 0, RCOLS:2 * RCOLS].bitcast(I32)
        VR = sb("VR", [E * F // P + 10, P], F32)
        VT = sb("VT", [P, E * F // P + 10], F32)
        fgw = sb("fgw", [P, H, E], F32)
        fgb = sb("fgb", [P, E], F32)
        keyT = sb("keyT", [P, WPAD], F32)
        lowT = sb("lowT", [P, WPAD], F32)
        stats = sb("stats", [P, NT, 6], F32)
        mv = sb("mv", [P, NT, 2], F32)
        rs = sb("rs", [P, 4, NT], F32)
        dinvx = sb("dinvx", [P, 2, NT], F32)
        degR = sb("degR", [P, NT], F32)
        wI = sb("wI", [ROWS, WB], I32)
        wIdx = sb("wIdx", [ROWS, WB], I32)
        selfI = sb("selfI", [ROWS, 3, WB * WN], I32)
        triF = XL[:, 0, 1300:1300 + P]
        pfx = sb("pfx", [NT, 2], F32)
        startF = XL[0:NT, 0, 1430:1430 + P]
        startW = XL[0:ROWS, 0, 1560:1560 + WB * WN].rearrange("p (j r) -> p j r", r=WN)
        wF = sb("wF", [ROWS, 2, WB], F32)
        fb = sb("fb", [P, 4], F32)
        flagF = sb("flagF", [1, 1], F32)
        flagI = sb("flagI", [1, 1], I32)
        idxc = sb("idxc", [ROWS, 1], I32)
        dcol = sb("dcol", [ROWS, 1], F32)
        bnst = sb("bnst", [P, H, G, 6], F32)
        bnmv = sb("bnmv", [P, H, 2], F32)
        bnc = sb("bnc", [P, 6, H], F32)
        fill = at(50000, CW, F32)
        nodeI = sb("nodeI", [P, NT], I32)
        slotI = sb("slotI", [P, NT], I32)
        iota8 = sb("iota8", [P, E], F32)
        tokI = [sb(f"tokI{k}", [P, 4], I32) for k in range(2)]
        def rt(k):
            return XL[:, 0, 200 * k:200 * k + NT * E].rearrange("p (a e) -> p a e", e=E)
        def rc(k):
            return XL[:, 1, NT * k:NT * (k + 1)]
        ohH = XL[:, 1, 1000:1100].bitcast(F16).rearrange("p (a e) -> p a e", e=E)
        ycopy = [t[:, 0:D] for t in (keyT, lowT)]

        beside = []
        for q in range(1, 7):
            beside += ([("T", q + 1, 0)] if q < 6 else []) + [("L", q, 0), ("L", q, 1)]
        beside += [("S", q, 0) for q in range(7)]
        S_FROM = len(beside) - 7
        def steps_at(gr, a):
            n = 0 if gr + 1 >= G else GI if gr + 1 < G - 1 else LASTI
            upto = lambda a: max(0, min(n, (a - FIRST_BUILD + 1) * n // (NT - 2 - FIRST_BUILD)))
            return range(upto(a - 1), upto(a))

        hi0, hi1 = CHUNKS[0][1], CHUNKS[1][1]
        ys = lambda lo, hi: [("y", a) for a in range(lo, hi)]
        middle = (ys(0, hi0 + 3) + [("N", 0), ("T", 0)] + ys(hi0 + 3, hi0 + 5) + [("T", 1)] + ys(hi0 + 5, hi0 + 7) +
                  [("L", 0)] + ys(hi0 + 7, hi1 + 1) + [("L", 1)] + ys(hi1 + 1, hi1 + 3) + [("E", 0), ("R", 0)] +
                  [("N", 1), ("T", 2)] + ys(hi1 + 3, hi1 + 5) + [("T", 3)] + ys(hi1 + 5, hi1 + 7) +
                  [("L", 2)] + ys(hi1 + 7, NT) + [("L", 3)] +
                  [("N", 2), ("E", 1), ("T", 4), ("T", 5), ("L", 4), ("R", 1), ("T", 6), ("L", 5), ("L", 6),
                   ("E", 2), ("R", 2)])

        all_pairs = range(((G - 1) * GI + LASTI) // 2)
        of_pool = [n for n in all_pairs if n >= GI // 2 and n % (GI // 2) in (5, 11)]
        of_dve = [n for n in all_pairs if n not in of_pool]

        def place(n):
            if n in of_pool:
                k = of_pool.index(n)
                return 2, k + 1, of_pool[k - 1] if k >= 1 else None
            k = of_dve.index(n)
            return k % 2, k + 1, of_dve[k - 2] if k >= 2 else None

        PS = [ctx.enter_context(nc.psum_tensor(f"PS{k}", [P, 512], F32)) for k in range(8)]

        s_dst, s_src, s_x, s_w, s_vec, s_fg, s_b2 = [sem(n) for n in (
            "dst_loaded", "src_loaded", "x_loaded", "weights_loaded", "vectors_loaded", "router_loaded",
            "b2_loaded")]
        s_x2 = [sem(f"x_reloaded{k}") for k in range(2)]
        s_const = sem("consts_ready")
        s_iota = sem("iota_ready")
        s_split = sem("dst_split")
        s_ohlo, s_ohhi = sem("onehot_low_ready"), sem("onehot_high_ready")
        s_minus, s_apart, s_ohact = (sem("values_ready"), sem("distance_ready"), sem("onehot_low_ready_scalar"))
        s_hist = sem("histogram_done")
        s_diag, s_bc, s_bcc = sem("diag_ready"), sem("broadcast_done"), sem("broadcast_copied")
        s_sq, s_sqi = sem("sqrt_done"), sem("sqrt_input_ready")
        s_deg, s_pfx, s_tot, s_st = (sem("degrees_ready"), sem("degrees_summed"), sem("tile_totals_ready"),
                                     sem("starts_ready"))
        s_st_d, s_wst = sem("starts_stored"), sem("window_starts_loaded")
        s_start, s_gs, s_gd = sem("window_starts_ready"), sem("sources_gathered"), sem("dests_gathered")
        s_key, s_keyp, s_keyc = sem("keys_ready"), sem("keys_transposed"), sem("keys_copied")
        s_cnt, s_flag = sem("matched_counted"), sem("flag_ready")
        s_ln, s_lnt, s_lnc, s_lin, s_linc = (sem("ln_ready"), sem("ln_transposed"), sem("ln_copied"),
                                             sem("lin_done"), sem("lin_copied"))
        s_lo2 = sem("last_source_low_ready")
        s_dx, s_hi, s_lo = sem("source_scale_ready"), sem("source_high_ready"), sem("source_low_ready")
        s_vT, s_vTc = sem("vectors_transposed"), sem("vectors_copied")
        s_ohp = sem("window_onehots_ready_gpsimd")
        s_oh, s_bld, s_ev = sem("window_onehots_ready"), sem("windows_built"), sem("adjacency_copied")
        s_agg, s_aggc = sem("aggregated"), sem("aggregate_scaled")
        s_gcn, s_z, s_gate, s_g = sem("gcn_done"), sem("z_ready"), sem("gate_done"), sem("g_ready")
        s_diff, s_h = sem("mix_difference_ready"), sem("h_ready")
        s_tab, s_gidx, s_grow, s_sel, s_gmm, s_io480 = (sem("table_stored"), sem("gather_index_ready"),
                sem("rows_gathered"), sem("selector_ready"), sem("general_step_done"), sem("iota480_ready"))
        s_dcol = sem("dest_column_ready")
        s_xsf, s_zx = sem("source_scaled"), sem("z_minus_xl")
        s_ptick = sem("pool_tick")
        s_bnc, s_bn0, s_bn1 = sem("bn_coefficients_ready"), sem("bn_applied_first_half"), sem("bn_applied_second_half")
        s_yT, s_yc, s_x1, s_x1p = sem("y_transposed"), sem("y_copied"), sem("x1_even_ready"), sem("x1_odd_ready")
        s_nmr, s_xn2o = sem("ln2_scales_ready"), sem("ln2_odd_ready")
        s_xn2, s_xnp, s_xnc, s_log = sem("ln2_ready"), sem("ln2_transposed"), sem("ln2_copied"), sem("logits_done")
        s_expi, s_exp, s_ohr, s_pos = (sem("exp_input_ready"), sem("exp_done"), sem("route_ready"),
                                       sem("positions_done"))
        s_fillr, s_filled, s_slot, s_disp = sem("fill_ready"), sem("buffer_filled"), sem("slots_ready"), sem("dispatched")
        s_out0, s_outs = sem("residual_stored"), [sem(f"rows_stored{k}") for k in range(2)]
        s_wl = [sem(f"expert_w{k + 1}_loaded") for k in range(2)]
        s_xb = [sem(f"expert_rows{k}") for k in range(2)]
        s_xr = [sem(f"expert_residuals{k}") for k in range(2)]
        s_xbfree = [sem(f"expert_rows_used{k}") for k in range(2)]
        s_xbp, s_xbh, s_xbl = sem("rows_transposed"), sem("rows_high_ready"), sem("rows_low_ready")
        s_wh, s_wlow = sem("weights_high_ready"), sem("weights_low_ready")
        s_up, s_hidf, s_hidh, s_hidl = (sem("up_done"), sem("hidden_ready"), sem("hidden_high_ready"),
                                        sem("hidden_low_ready"))
        s_down, s_y, s_pad = sem("down_done"), sem("y_ready"), sem("hidden_padded")
        dch, pch, ach = sem("vector_chain"), sem("pool_chain"), sem("scalar_chain")

        block = ctx.enter_context(nc.Block())

        @block.sync
        def _(sp):
            sp.dma_start(dstI[:, 0:RCOLS], dst.rearrange("(r c) -> r c", c=RCOLS)).then_inc(s_dst, 16)
            full = (NT - 1) * P
            sp.wait_ge(s_const, 1)
            sp.dma_start(xn[:, 0:NT - 1, :], x[0:full, :].rearrange("(a p) d -> p a d", p=P)).then_inc(s_x, 16)
            sp.dma_start(xn[0:TAIL, NT - 1, :], x[full:N_NODES, :]).then_inc(s_x, 16)
            sp.dma_start(srcI[:, 0:RCOLS], src.rearrange("(r c) -> r c", c=RCOLS)).then_inc(s_src, 16)
            for w_sb, w in ((linW, lin_W), (gcnW, gcn_W), (gateW, gate_W)):
                sp.dma_start(w_sb[:, :, :], w.rearrange("(h p) n -> p h n", p=P)).then_inc(s_w, 16)
            nb = E * F // P
            sp.dma_start(VR[0:nb, :], b1.rearrange("e (f p) -> (e f) p", p=P)).then_inc(s_vec, 16)
            for k, v in enumerate((gcn_b, lin_b, gate_b, bn_gamma, bn_beta)):
                sp.dma_start(VR[nb + 2 * k:nb + 2 * k + 2, :], v.rearrange("(h p) -> h p", p=P)).then_inc(s_vec, 16)
            sp.dma_start(fgw[:, :, :], fgate_w.rearrange("(h p) e -> p h e", p=P)).then_inc(s_fg, 16)
            sp.dma_start(fgb[:, :], fgate_b.rearrange("(o e) -> o e", o=1).to_broadcast([P, E])).then_inc(s_fg, 16)
            sp.wait_ge(s_st, 1)
            sp.dma_start(start_d.rearrange("(a p) -> a p", p=P), startF[:, :]).then_inc(s_st_d, 16)
            sp.wait_ge(s_st_d, 16)
            sp.dma_start(startW, start_d[0:N_NODES].rearrange("(j p r) -> p j r", p=ROWS, r=WN)).then_inc(s_wst, 16)
            sp.wait_ge(s_gs, 16 * WB)
            sp.wait_ge(s_gd, 16 * WB)
            sp.wait_ge(s_fillr, 2)
            sp.dma_start(buf_d.rearrange("(j p) c -> p j c", p=P),
                         fill.rearrange("p (o c) -> p o c", o=1).to_broadcast([P, E * SROW // P, CW])).then_inc(s_filled, 16)
            w1_v = w1.rearrange("e (h p) f -> e p h f", p=P)
            w2_v = w2.rearrange("e (f p) d -> e p f d", p=P)

            def load_weights(e):
                if e >= 1:
                    sp.wait_ge(s_wlow, 2 * e)
                sp.dma_start(w1s, w1_v[e]).then_inc(s_wl[0], 16)
                sp.dma_start(w2s, w2_v[e]).then_inc(s_wl[1], 16)

            m = P * X_EARLY
            sp.wait_ge(s_lnt, 7)
            sp.wait_ge(s_lo, LO_POOL)
            sp.wait_ge(s_lo2, NT - LO_POOL)
            sp.dma_start(comb[:, 0:X_EARLY, D:2 * D], x[0:m, :].rearrange("(a p) d -> p a d", p=P)).then_inc(s_x2[0], 16)
            sp.wait_ge(s_filled, 16)
            sp.wait_ge(s_agg, G - 1)
            load_weights(0)
            sp.wait_ge(s_agg, G)
            sp.wait_ge(s_const, 3)
            sp.dma_start(comb[:, X_EARLY:NT - 1, D:2 * D], x[m:full, :].rearrange("(a p) d -> p a d", p=P)).then_inc(s_x2[1], 16)
            sp.dma_start(comb[0:TAIL, NT - 1, D:2 * D], x[full:N_NODES, :]).then_inc(s_x2[1], 16)
            sp.wait_ge(s_aggc, G)
            sp.dma_start(DB[:, 0:E * D], b2.rearrange("(o e) d -> o (e d)", o=1).to_broadcast([P, E * D])).then_inc(s_b2, 16)
            sp.wait_ge(s_x1, (NT + 1) // 2)
            sp.wait_ge(s_x1p, NT // 2)
            sp.dma_start(out[0:full, :].rearrange("(a p) d -> p a d", p=P), comb[:, 0:NT - 1, D:2 * D]).then_inc(s_out0, 16)
            sp.dma_start(out[full:N_NODES, :], comb[0:TAIL, NT - 1, D:2 * D]).then_inc(s_out0, 16)
            buf_v = buf_d.rearrange("(e j p) c -> e p j c", p=P, j=4)

            def load_rows(e):
                if e >= 2:
                    sp.wait_ge(s_xbfree[e % 2], e // 2)
                sp.dma_start(xb[e % 2][:, :, 0:D], buf_v[e][:, :, 0:D]).then_inc(s_xb[e % 2], 16)
                sp.dma_start(xb[e % 2][:, :, D:CW], buf_v[e][:, :, D:CW]).then_inc(s_xr[e % 2], 16)

            load_weights(1)
            sp.wait_ge(s_disp, 16 * NT)
            load_rows(0)
            sp.wait_ge(s_xb[0], 16)
            load_rows(1)
            for e in range(2, E):
                load_rows(e)
                load_weights(e)
            sp.wait_ge(s_out0, 32)
            sp.wait_ge(s_src, 16)

        @block.gpsimd
        def _(pool):
            g = nc.gpsimd
            n = [0]

            def step(ins):
                n[0] += 1
                ins.then_inc(pch, 1)

            def settle():
                pool.wait_ge(pch, n[0])

            g.memset(xn[:, NT - 1, :], 0.0).then_inc(s_const, 1)
            g.iota(iotaI, [[1, P]], base=0, channel_multiplier=0).then_inc(s_iota, 1)
            g.iota(minus, [[-1, LO_ACT]], base=LO_ACT - P, channel_multiplier=0,
                   allow_small_or_imprecise_dtypes=True).then_inc(s_minus, 1)
            step(g.memset(ident[:, :], 0.0))
            step(g.memset(triH[:, :], 1.0))
            step(g.memset(ones[:, :], 1.0))
            step(g.memset(triF[:, :], 1.0))
            step(g.memset(onesH[:, :], 1.0))
            step(g.iota(srcI[:, RCOLS:], [[ROWS, LOOPC]], base=0, channel_multiplier=1))
            step(g.iota(dstI[:, RCOLS:], [[ROWS, LOOPC]], base=0, channel_multiplier=1))
            step(g.iota(nodeI[:, :], [[P, NT]], base=0, channel_multiplier=1))
            step(g.iota(selfI[:, 0, :].rearrange("p (j r) -> p j r", r=WN), [[WN * ROWS, WB], [1, WN]], base=0,
                        channel_multiplier=WN))
            step(g.iota(wI[:, :], [[WN * ROWS, WB]], base=0, channel_multiplier=WN))
            step(g.memset(keyT[:, NW:WPAD], NOKEY))
            step(g.memset(lowT[:, NW:WPAD], NOKEY))
            settle()
            step(g.affine_select(out=ident[:, :], in_=ident[:, :], compare_op=ALU.not_equal, fill=1.0, base=0,
                                 pattern=[[-1, P]], channel_multiplier=1))
            step(g.affine_select(out=triF[:, :], in_=triF[:, :], compare_op=ALU.is_ge, fill=0.0, base=-1,
                                 pattern=[[1, P]], channel_multiplier=-1))
            step(g.affine_select(out=triH[:, :], in_=triH[:, :], compare_op=ALU.is_ge, fill=0.0, base=0,
                                 pattern=[[1, P]], channel_multiplier=-1))
            settle()
            g.memset(fb[:, 0:1], 1.0).then_inc(s_const, 1)
            pool.wait_ge(s_split, 2)
            for v in range(HI_POOL):
                ins = g.tensor_scalar(oh_hi[0:ROWS, v, :], hi16, float(v), None, ALU.is_equal)
                step(ins)
            settle()
            g.memset(fb[:, 1:2], 1.0).then_inc(s_ohhi, 1)
            pool.wait_ge(s_hist, 1)
            g.memset(fill[:, 0:CW - 1], 0.0).then_inc(s_fillr, 1)
            g.memset(fill[:, CW - 1:CW], NOROW).then_inc(s_fillr, 1)
            pool.wait_ge(s_start, 1)
            for j in range(WB):
                g.indirect_dma_start(out=edges_s[0:ROWS, j, :], out_offset=None, in_=src_flat[:, 0:1],
                                     in_offset=bass.IndirectOffsetOnAxis(ap=wIdx[:, j:j + 1], axis=0),
                                     bounds_check=N_EDGES - 1, oob_is_err=False).then_inc(s_gs, 16)
                g.indirect_dma_start(out=edges_d[0:ROWS, j, :], out_offset=None, in_=dst_flat[:, 0:1],
                                     in_offset=bass.IndirectOffsetOnAxis(ap=wIdx[:, j:j + 1], axis=0),
                                     bounds_check=N_EDGES - 1, oob_is_err=False).then_inc(s_gd, 16)
            pool.wait_ge(s_dx, 1)
            pool.wait_ge(s_ln, 1)
            for a in range(LO_POOL):
                g.tensor_scalar(xsf[a % 2], xn[:, a, :], dinvx[:, 0, a:a + 1], None, ALU.mult).then_inc(s_xsf, 1)
                pool.wait_ge(s_xsf, a + 1)
                pool.wait_ge(s_hi, a + 1)
                g.tensor_tensor(xs[:, a, D:2 * D], xsf[a % 2], xs[:, a, 0:D], ALU.subtract).then_inc(s_lo, 1)
            pool.wait_ge(s_flag, 1)
            fast = pool.value_load(flagI[0:1, 0:1], min_val=0, max_val=1)

            def onehots(pair):
                last = place(pair)[2]
                if last is not None:
                    pool.wait_ge(s_bld, 2 * (last + 1))
                for k in range(8):
                    w = 8 * pair + k
                    g.tensor_scalar(ohb[2][:, k, :], iotaH[:, :], lowT[:, w:w + 1], None, ALU.is_equal)
                    ins = g.tensor_scalar(ohk[2][:, k, :], iotaH[:, 0:KEYS], keyT[:, w:w + 1], None, ALU.is_equal)
                ins.then_inc(s_ohp, 1)

            def z_less_xl(q):
                nn = GN if q < G - 1 else LASTN
                pool.wait_ge(s_z, H * (q + 1))
                pool.wait_ge(s_linc, H * 7)
                if q >= 1:
                    pool.wait_ge(s_h, H * q)
                for h in range(H):
                    g.tensor_tensor(mT[:, h, 0:nn], zT[q % 2][:, h, 0:nn],
                                    XL[:, h, GN * q:GN * q + nn], ALU.subtract).then_inc(s_zx, 1)

            def times_g(q):
                nn = GN if q < G - 1 else LASTN
                for h in range(H):
                    pool.wait_ge(s_zx, H * q + h + 1)
                    pool.wait_ge(s_g, H * q + h + 1)
                    g.tensor_tensor(mT[:, h, 0:nn], mT[:, h, 0:nn], gT[:, h, 0:nn], ALU.mult).then_inc(s_diff, 1)

            for gr in range(G):
                q = gr - 1
                with pool.If(fast == 1):
                    mine = [pair for pair in of_pool if pair // (GI // 2) == gr + 1]
                    for k in range(2):
                        if k < len(mine):
                            onehots(mine[k])
                        if q >= 0:
                            (z_less_xl, times_g)[k](q)
                with pool.Else():
                    if gr == 0:
                        g.iota(io480, [[1, GN]], base=0, channel_multiplier=0,
                               allow_small_or_imprecise_dtypes=True).then_inc(s_io480, 1)
                        pool.wait_ge(s_lo, LO_POOL)
                        pool.wait_ge(s_lo2, NT - LO_POOL)
                        pool.wait_ge(s_src, 16)
                        g.dma_start(xs_d.rearrange("(a p) d -> p a d", p=P), xs).then_inc(s_tab, 16)
                        pool.wait_ge(s_tab, 16)
                    NC = RCOLS + LOOPC
                    with pool.Fori(0, NC) as c:
                        pool.wait_ge(s_gmm, c + gr * NC)
                        pool.sem_inc(s_ptick, 1)
                        g.tensor_copy(idxc[:, :], srcI[:, bass.ds(c, 1)]).then_inc(s_gidx, 1)
                        pool.wait_ge(s_gidx, c + (gr * NC + 1))
                        pool.sem_inc(s_ptick, 1)
                        g.indirect_dma_start(out=gath[0:ROWS, :], out_offset=None, in_=xs_d,
                                             in_offset=bass.IndirectOffsetOnAxis(ap=idxc[:, 0:1], axis=0),
                                             bounds_check=NPAD - 1, oob_is_err=False).then_inc(s_grow, 16)
                    if q >= 0:
                        z_less_xl(q)
                        times_g(q)
            pool.wait_ge(s_agg, G)
            g.memset(comb[:, NT - 1, D:2 * D], 0.0).then_inc(s_const, 1)
            z_less_xl(G - 1)
            times_g(G - 1)

            def weights_split(e, k):
                full, (high, low) = (w1s, w1r[e % 2]) if k == 0 else (w2s, w2r[e % 2])
                pool.wait_ge(s_wh, 2 * e + k + 1)
                g.tensor_tensor(low, full, high.bitcast(F32), ALU.subtract).then_inc(s_wlow, 1)

            weights_split(0, 0)
            weights_split(0, 1)
            def x1_odd(a):
                pool.wait_ge(*((s_x2[0], 16) if a < X_EARLY else (s_x2[1], 32)))
                pool.wait_ge(s_yc, a // 2 + 1)
                x1 = comb[:, a, D:2 * D]
                g.tensor_tensor(x1, ycopy[a // 2 % 2], x1, ALU.add).then_inc(s_x1p, 1)

            def dispatched(a):
                pool.wait_ge(s_slot, 1 + sum(a >= hi for _, hi in CHUNKS))
                if a == 0:
                    pool.wait_ge(s_filled, 16)
                g.indirect_dma_start(out=buf_d, out_offset=bass.IndirectOffsetOnAxis(ap=slotI[:, a:a + 1], axis=0),
                                     in_=comb[:, a, :], in_offset=None,
                                     bounds_check=E * SROW - 1, oob_is_err=False).then_inc(s_disp, 16)

            for a in range(1, hi1, 2):
                x1_odd(a)
            for a in range(hi0):
                dispatched(a)
                if a % 2 == 1 and hi1 + a + 2 < NT:
                    x1_odd(hi1 + a + 2)
                if a == 0:
                    x1_odd(hi1 + 1)
            for a in range(hi0, NT):
                dispatched(a)
            pool.wait_ge(s_out0, 32)
            for e in range(E):
                u = e % 2
                for j in range(4):
                    if e + 1 < E and j % 2 == 0:
                        weights_split(e + 1, j // 2)
                    pool.wait_ge(s_y, 4 * e + j + 1)
                    g.indirect_dma_start(out=out, out_offset=bass.IndirectOffsetOnAxis(ap=tokI[u][:, j:j + 1], axis=0),
                                         in_=yt[u][:, j, :], in_offset=None,
                                         bounds_check=N_NODES - 1, oob_is_err=False).then_inc(s_outs[u], 16)
            for u in range(2):
                pool.wait_ge(s_outs[u], 16 * 4 * E // 2)

        @block.vector
        def _(dve):
            v = nc.vector
            n = [0]

            def step(ins):
                n[0] += 1
                ins.then_inc(dch, 1)

            def settle():
                dve.wait_ge(dch, n[0])

            def link(ins):
                step(ins)
                settle()

            dve.wait_ge(s_iota, 1)
            link(v.tensor_copy(iotaH[:, :], iotaI))
            dve.wait_ge(s_dst, 16)
            step(v.tensor_single_scalar(tmpI, dstI[:, 0:RCOLS], P - 1, ALU.bitwise_and))
            step(v.tensor_single_scalar(tmpI2, dstI[:, 0:RCOLS], 7, ALU.arith_shift_right))
            settle()
            v.tensor_copy(hi16, tmpI2).then_inc(s_split, 1)
            v.tensor_copy(lo16, tmpI).then_inc(s_split, 1)
            dve.wait_ge(s_split, 2)
            for k in range(P - LO_ACT):
                step(v.tensor_scalar(oh_lo[0:ROWS, k, :], lo16, float(k), None, ALU.is_equal))
            for k in range(HI_POOL, NT):
                step(v.tensor_scalar(oh_hi[0:ROWS, k, :], hi16, float(k), None, ALU.is_equal))
            settle()
            v.memset(fb[:, 2:3], 1.0).then_inc(s_ohlo, 1)

            def rsqrt(width, mark, lo=0):
                val, sq, r, t = [rs[:, k, lo:lo + width] for k in range(4)]
                settle()
                v.memset(fb[:, 3:4], 0.0).then_inc(s_sqi, 1)
                dve.wait_ge(s_sq, mark)
                link(v.reciprocal(r, sq))
                link(v.tensor_tensor(t, r, r, ALU.mult))
                link(v.tensor_tensor(t, t, val, ALU.mult))
                link(v.tensor_scalar(t, t, -0.5, 1.5, ALU.mult, ALU.add))
                link(v.tensor_tensor(r, r, t, ALU.mult))
                return r

            dve.wait_ge(s_x, 32)
            for a in range(NT):
                step(v.bn_stats(stats[:, a, :], xn[:, a, :]))
            settle()
            for a in range(NT):
                step(v.bn_aggr(mv[:, a, :], stats[:, a, :]))
            settle()
            dve.wait_ge(s_const, 2)
            dve.wait_ge(s_hist, 1)
            v.tensor_copy(degR[:, :], PS[0][:, 0:NT]).then_inc(s_deg, 1)
            dve.wait_ge(s_deg, 1)
            dve.wait_ge(s_pfx, 1)
            v.tensor_copy(pfx[:, 0:1], PS[3][0:NT, 0:1]).then_inc(s_tot, 1)
            dve.wait_ge(s_pfx, 2)
            link(v.tensor_copy(pfx[:, 1:2], PS[1][0:NT, 0:1]))
            v.tensor_scalar(startF[:, :], PS[2][0:NT, 0:P], pfx[:, 1:2], None, ALU.add).then_inc(s_st, 1)

            link(v.tensor_scalar(rs[:, 0, :], mv[:, :, 1], LN_EPS, None, ALU.add))
            r = rsqrt(NT, 1)

            def ln_rows(lo, hi):
                for a in range(lo, hi):
                    step(v.tensor_scalar(xn[:, a, :], xn[:, a, :], mv[:, a, 0:1], r[:, a:a + 1], ALU.subtract, ALU.mult))

            ln_rows(0, 6)
            dve.wait_ge(s_wst, 16)
            link(v.tensor_scalar(wF[:, 0, :], startW[:, :, 0], float(N_EDGES - SLOTS), None, ALU.min))
            v.tensor_copy(wIdx[:, :], wF[:, 0, :]).then_inc(s_start, 1)
            ln_rows(6, NT)
            settle()
            v.memset(fb[:, 3:4], 0.0).then_inc(s_ln, 1)

            def spread(lo, hi):
                vec = dinvx[:, 1, :]
                for q in range(lo, hi):
                    m = min(4, NT - 4 * q)
                    if q >= 4:
                        dve.wait_ge(s_bc, q - 3)
                    v.tensor_tensor(diag[q % 4][:, 0:m, :], ident[:, :].unsqueeze(1).to_broadcast([P, m, P]),
                                    vec[:, 4 * q:4 * q + m].unsqueeze(2).to_broadcast([P, m, P]),
                                    ALU.mult).then_inc(s_diag, 1)

            link(v.tensor_scalar(rs[:, 0, :], degR[:, :], 1.0, None, ALU.add))
            r = rsqrt(NT, 2)
            link(v.tensor_scalar(dinvx[:, 0, :], r, XSC, None, ALU.mult))
            link(v.tensor_scalar(dinvx[:, 1, :], r, 1.0 / XSC, None, ALU.mult))
            v.memset(fb[:, 3:4], 0.0).then_inc(s_dx, 1)
            so = WB * WN
            step(v.tensor_single_scalar(selfI[:, 1, :], selfI[:, 0, :], P - 1, ALU.bitwise_and))
            step(v.tensor_single_scalar(selfI[:, 2, :], selfI[:, 0, :], 7, ALU.arith_shift_right))
            settle()
            low, high, dl, t0, valid, key = keyw
            self3 = lambda k: selfI[:, k, :].rearrange("p (j r) -> p j r", r=WN)
            step(v.tensor_copy(low[0:ROWS, :, SLOTS:P], self3(1)))
            step(v.tensor_copy(high[0:ROWS, :, SLOTS:P], self3(2)))
            step(v.tensor_copy(wF[:, 1, :], wI[:, :]))
            settle()
            first = wF[:, 1, :].unsqueeze(2)
            step(v.tensor_tensor(dl[0:ROWS, :, SLOTS:P], self3(0), first.to_broadcast([ROWS, WB, WN]), ALU.subtract))
            settle()
            step(v.scalar_tensor_tensor(key[0:ROWS, :, SLOTS:P], high[0:ROWS, :, SLOTS:P], float(WN),
                                        dl[0:ROWS, :, SLOTS:P], ALU.mult, ALU.add))
            S = slice(0, SLOTS)
            dve.wait_ge(s_gs, 16 * WB)
            dve.wait_ge(s_gd, 16 * WB)
            eI = [at(42048 + 2464 * k, WB * SLOTS, I32)[0:ROWS].rearrange("p (j s) -> p j s", s=SLOTS) for k in range(2)]
            es, ed = edges_s[0:ROWS], edges_d[0:ROWS]
            step(v.tensor_single_scalar(eI[0], es, P - 1, ALU.bitwise_and))
            step(v.tensor_single_scalar(eI[1], es, 7, ALU.arith_shift_right))
            step(v.tensor_tensor(dl[0:ROWS, :, S], ed, first.to_broadcast([ROWS, WB, SLOTS]), ALU.subtract))
            settle()
            step(v.tensor_copy(low[0:ROWS, :, S], eI[0]))
            step(v.tensor_copy(high[0:ROWS, :, S], eI[1]))
            step(v.tensor_scalar(t0[0:ROWS, :, S], dl[0:ROWS, :, S], 0.0, None, ALU.is_ge))
            settle()
            step(v.scalar_tensor_tensor(valid[0:ROWS, :, S], dl[0:ROWS, :, S], float(WN), t0[0:ROWS, :, S],
                                        ALU.is_lt, ALU.mult))
            step(v.scalar_tensor_tensor(key[0:ROWS, :, S], high[0:ROWS, :, S], float(WN), dl[0:ROWS, :, S],
                                        ALU.mult, ALU.add))
            settle()
            step(v.scalar_tensor_tensor(key[0:ROWS, :, S], key[0:ROWS, :, S], -NOKEY, valid[0:ROWS, :, S],
                                        ALU.add, ALU.mult))
            link(v.tensor_reduce(fb[0:ROWS, 0:1], valid[0:ROWS, :, S], AX.XY, ALU.add))
            link(v.tensor_scalar(key[0:ROWS, :, S], key[0:ROWS, :, S], NOKEY, None, ALU.add))
            v.memset(fb[:, 3:4], 0.0).then_inc(s_key, 1)
            dve.wait_ge(s_cnt, 1)
            link(v.tensor_scalar(flagF[:, :], PS[1][0:1, 0:1], float(N_EDGES), None, ALU.is_equal))
            v.tensor_copy(flagI[:, :], flagF[:, :]).then_inc(s_flag, 1)
            dve.wait_ge(s_flag, 1)
            fast = dve.value_load(flagI[0:1, 0:1], min_val=0, max_val=1)
            dve.wait_ge(s_keyc, 4)

            def onehots(n):
                at_, _, last = place(n)
                w = 8 * n
                if last is not None:
                    dve.wait_ge(s_bld, 2 * (last + 1))
                v.tensor_tensor(ohb[at_], iotaH[:, :].unsqueeze(1).to_broadcast([P, 8, P]),
                                lowT[:, w:w + 8].unsqueeze(2).to_broadcast([P, 8, P]), ALU.is_equal)
                v.tensor_tensor(ohk[at_], iotaH[:, 0:KEYS].unsqueeze(1).to_broadcast([P, 8, KEYS]),
                                keyT[:, w:w + 8].unsqueeze(2).to_broadcast([P, 8, KEYS]),
                                ALU.is_equal).then_inc(s_oh, 1)

            def group_pairs(gr):
                return [pair for pair in of_dve if pair // (GI // 2) == gr]

            for gr in range(-1, G + 1):
                if gr + 1 < G:
                    with dve.If(fast == 1):
                        for pair in group_pairs(gr + 1)[0 if gr == -1 else 2:]:
                            onehots(pair)
                            if gr == -1 and pair == S_FROM // 2:
                                spread(0, 4)
                            if gr == -1 and pair == S_FROM // 2 + 1:
                                spread(4, 7 - (S_FROM + 1) % 2)
                            if gr == -1 and pair == S_FROM // 2 + 2:
                                spread(7 - (S_FROM + 1) % 2, 7)
                    with dve.Else():
                        if gr == -1:
                            spread(0, 7)
                        else:
                            dve.nop()
                if gr == -1:
                    for a in range(LO_POOL, NT):
                        dve.wait_ge(s_hi, a + 1)
                        v.scalar_tensor_tensor(xs[:, a, D:2 * D], xn[:, a, :], dinvx[:, 0, a:a + 1],
                                               xs[:, a, 0:D], ALU.mult, ALU.subtract).then_inc(s_lo2, 1)
                if 0 <= gr < G:
                    with dve.If(fast == 1):
                        dve.nop()
                    with dve.Else():
                        if gr == 0:
                            dve.wait_ge(s_io480, 1)
                        NC = RCOLS + LOOPC
                        with dve.Fori(0, NC) as c:
                            dve.wait_ge(s_gmm, c + gr * NC)
                            v.tensor_scalar(dcol[:, :], dstI[:, bass.ds(c, 1)], float(-GN * gr), None,
                                            ALU.add).then_inc(s_dcol, 1)
                            dve.wait_ge(s_dcol, c + (gr * NC + 1))
                            v.tensor_scalar(dsel[0:ROWS, :], io480[0:ROWS, :], dcol[:, 0:1], None,
                                            ALU.is_equal).then_inc(s_sel, 1)
                q = gr - 1
                if 0 <= q < G:
                    nn = GN if q < G - 1 else LASTN
                    nv = min(GN, N_NODES - GN * q)
                    for h in range(H):
                        dve.wait_ge(s_diff, H * q + h + 1)
                        hx = XL[:, h, GN * q:GN * q + nn]
                        link(v.tensor_tensor(mT[:, h, 0:nn], mT[:, h, 0:nn], hx, ALU.add))
                        v.tensor_scalar(hx, mT[:, h, 0:nn], 0.0, None, ALU.max).then_inc(s_h, 1)
                        dve.wait_ge(s_h, H * q + h + 1)
                        step(v.bn_stats(bnst[:, h, q, :], XL[:, h, GN * q:GN * q + nv]))
                if gr + 2 < G:
                    with dve.If(fast == 1):
                        for pair in group_pairs(gr + 2)[0:2]:
                            onehots(pair)
                    with dve.Else():
                        dve.nop()
                if 0 <= gr < G:
                    nn = GN if gr < G - 1 else LASTN
                    dve.wait_ge(s_agg, gr + 1)
                    if gr >= 2:
                        dve.wait_ge(s_gcn, gr - 1)
                    for h in range(H):
                        ins = v.tensor_tensor(aggT[gr % 2][:, h, 0:nn], PS[2 + 2 * (gr % 2) + h][:, 0:nn],
                                              DB[:, GN * gr:GN * gr + nn], ALU.mult)
                        if h == 0:
                            step(ins)
                    ins.then_inc(s_aggc, 1)
            settle()
            for h in range(H):
                step(v.bn_aggr(bnmv[:, h, :], bnst[:, h, :, :].rearrange("p g s -> p (g s)")))
            settle()
            link(v.tensor_scalar(rs[:, 0, 0:H], bnmv[:, :, 1], BN_EPS, None, ALU.add))
            r = rsqrt(H, 3)
            nb = E * F // P
            gamma, beta = VT[:, nb + 6:nb + 8], VT[:, nb + 8:nb + 10]
            link(v.tensor_tensor(bnc[:, 0, :], r, gamma, ALU.mult))
            link(v.tensor_tensor(bnc[:, 1, :], bnmv[:, :, 0], bnc[:, 0, :], ALU.mult))
            link(v.tensor_tensor(bnc[:, 2, :], beta, bnc[:, 1, :], ALU.subtract))
            settle()
            v.memset(fb[:, 3:4], 0.0).then_inc(s_bnc, 1)
            for c in range(BN_PARTS):
                m = NPAD // BN_PARTS
                v.tensor_scalar(XL[:, 0, m * c:m * (c + 1)], XL[:, 0, m * c:m * (c + 1)], bnc[:, 0, 0:1], bnc[:, 2, 0:1],
                                ALU.mult, ALU.add).then_inc(s_bn0, 1)

            def x1_rows(lo, hi):
                dve.wait_ge(s_x2[0], 16)
                if hi > X_EARLY:
                    dve.wait_ge(s_x2[1], 32)
                for a in range(lo, hi + 1):
                    x1 = comb[:, min(a, NT - 1), D:2 * D]
                    if a < hi and a % 2 == 0:
                        dve.wait_ge(s_yT, a + 1)
                        v.tensor_tensor(x1, PS[a % 3][:, 0:D], x1, ALU.add).then_inc(s_x1, 1)
                    if a % 2 == 0 and a > lo:
                        dve.wait_ge(s_x1p, a // 2)
                        step(v.bn_stats(stats[:, a - 1, :], comb[:, a - 1, D:2 * D]))
                    if a < hi and a % 2 == 0:
                        dve.wait_ge(s_x1, a // 2 + 1)
                        step(v.bn_stats(stats[:, a, :], x1))
                settle()

            def ln2_rows(lo, hi, mark):
                for a in range(lo, hi):
                    step(v.bn_aggr(mv[:, a, :], stats[:, a, :]))
                settle()
                link(v.tensor_scalar(rs[:, 0, lo:hi], mv[:, lo:hi, 1], LN_EPS, None, ALU.add))
                r = rsqrt(hi - lo, mark, lo)
                link(v.tensor_tensor(rs[:, 3, lo:hi], mv[:, lo:hi, 0], r, ALU.mult))
                v.tensor_scalar(rs[:, 3, lo:hi], rs[:, 3, lo:hi], -1.0, None, ALU.mult).then_inc(s_nmr, 1)
                for a in range(lo, hi, 2):
                    v.tensor_scalar(comb[:, a, 0:D], comb[:, a, D:2 * D], mv[:, a, 0:1], r[:, a - lo:a - lo + 1],
                                    ALU.subtract, ALU.mult).then_inc(s_xn2, 1)

            def route(c):
                lo, hi = CHUNKS[c]
                m = hi - lo
                A3 = lambda k: rt(k)[:, lo:hi, :]
                A1 = lambda k: rc(k)[:, lo:hi]

                def over(vec):
                    return vec.unsqueeze(2).to_broadcast([P, m, E])

                L, ex, pr, eq, tot, before, rank = [A3(k) for k in range(7)]
                node, live = A1(0), A1(1)
                iota_b = iota8[:, :].unsqueeze(1).to_broadcast([P, m, E])
                if c == 0:
                    step(v.tensor_copy(rc(0), nodeI[:, :]))
                    step(v.tensor_copy(iota8[:, :], iotaH[:, 0:E]))
                    settle()
                    link(v.tensor_scalar(rc(1), rc(0), float(N_NODES), None, ALU.is_lt))
                    step(v.tensor_copy(comb[:, :, 2 * D + 1], rc(0)))
                    dve.wait_ge(s_fg, 32)
                dve.wait_ge(s_log, c + 1)
                link(v.tensor_tensor(L, PS[(3, 3, 6)[c]][:, E * lo:E * hi].rearrange("p (a e) -> p a e", e=E),
                                     fgb[:, :].unsqueeze(1).to_broadcast([P, m, E]), ALU.add))
                link(v.tensor_reduce(A1(2), L, AX.X, ALU.max))
                v.tensor_tensor(L, L, over(A1(2)), ALU.subtract).then_inc(s_expi, 1)
                dve.wait_ge(s_exp, c + 1)
                link(v.tensor_reduce(A1(3), ex, AX.X, ALU.add))
                link(v.reciprocal(A1(3), A1(3)))
                link(v.tensor_tensor(pr, ex, over(A1(3)), ALU.mult))
                link(v.tensor_reduce(A1(4), pr, AX.X, ALU.max))
                link(v.tensor_tensor(eq, pr, over(A1(4)), ALU.is_equal))
                step(v.tensor_copy(comb[:, lo:hi, 2 * D], A1(4)))
                link(v.scalar_tensor_tensor(eq, eq, -float(E), iota_b, ALU.mult, ALU.add))
                link(v.tensor_reduce(A1(5), eq, AX.X, ALU.min))
                link(v.tensor_scalar(A1(5), A1(5), float(E), None, ALU.add))
                link(v.tensor_tensor(eq, iota_b, over(A1(5)), ALU.is_equal))
                link(v.tensor_tensor(eq, eq, over(live), ALU.mult))
                v.tensor_copy(ohH[:, lo:hi, :], eq).then_inc(s_ohr, 1)
                dve.wait_ge(s_pos, c + 1)
                link(v.tensor_copy(tot, PS[7][:, 256 + E * lo:256 + E * hi].rearrange("p (a e) -> p a e", e=E)))
                step(v.memset(rt(5)[:, 0:1, :], 0.0))
                for e in range(E):
                    step(v.tensor_tensor_scan(rt(5)[:, 1:hi, e], rt(4)[:, 0:hi - 1, e], rt(4)[:, 0:hi - 1, e], 0.0,
                                              ALU.add, ALU.max))
                settle()
                link(v.tensor_tensor(rank, PS[7][:, E * lo:E * hi].rearrange("p (a e) -> p a e", e=E), before, ALU.add))
                link(v.tensor_tensor(rank, rank, eq, ALU.mult))
                link(v.tensor_reduce(A1(6), rank, AX.X, ALU.add))
                link(v.tensor_scalar(A1(6), A1(6), -1.0, None, ALU.add))
                link(v.tensor_scalar(A1(7), A1(6), float(CAP), None, ALU.is_lt))
                link(v.tensor_tensor(A1(7), A1(7), live, ALU.mult))
                link(v.scalar_tensor_tensor(A1(6), A1(5), float(SROW), A1(6), ALU.mult, ALU.add))
                link(v.scalar_tensor_tensor(A1(6), A1(6), -NOROW, A1(7), ALU.add, ALU.mult))
                link(v.tensor_scalar(A1(6), A1(6), NOROW, None, ALU.add))
                v.tensor_copy(slotI[:, lo:hi], A1(6)).then_inc(s_slot, 1)

            x1_rows(*CHUNKS[0])
            ln2_rows(*CHUNKS[0], 4)
            x1_rows(*CHUNKS[1])
            route(0)
            ln2_rows(*CHUNKS[1], 5)
            x1_rows(*CHUNKS[2])
            ln2_rows(*CHUNKS[2], 6)
            route(1)
            route(2)

            dve.wait_ge(s_b2, 16)
            step(v.memset(zero_y, 0.0))
            settle()

            dve.wait_ge(s_disp, 16 * NT)
            dve.wait_ge(s_out0, 32)
            for part in range(2):
                v.memset(hidr[part][:, :, CAPE:512].bitcast(F32), 0.0).then_inc(s_pad, 1)

            def rows_low(e):
                for h in range(H):
                    dve.wait_ge(s_xbh, H * e + h + 1)
                    v.tensor_tensor(xbTr[e % 2][1][:, h, :], PS[h][:, :], xbTr[e % 2][0][:, h, :].bitcast(F32),
                                    ALU.subtract).then_inc(s_xbl, 1)

            rows_low(0)
            for e in range(E):
                u = e % 2
                for f in range(8):
                    dve.wait_ge(s_hidh, 8 * e + f + 1)
                    if e >= 1 and f == 0:
                        dve.wait_ge(s_down, 4 * e)
                    v.tensor_tensor(hidr[1][:, f, 0:CAPE], hidf[:, f, :], hidr[0][:, f, 0:CAPE].bitcast(F32),
                                    ALU.subtract).then_inc(s_hidl, 1)
                if e + 1 < E:
                    rows_low(e + 1)
                if e >= 2:
                    dve.wait_ge(s_outs[u], 16 * 4 * (e // 2))
                dve.wait_ge(s_xr[u], 16 * (e // 2 + 1))
                link(v.tensor_copy(tokI[u][:, :], xb[u][:, :, 2 * D + 1]))
                for j in range(4):
                    m = min(P, CAP - P * j)
                    y, t, mask = yt[u][:, j, :], tmp_y, tmp_m.bitcast(I32)
                    if m < P:
                        step(v.memset(y, 0.0))
                    dve.wait_ge(s_down, 4 * e + j + 1)
                    link(v.tensor_tensor(t[0:m], PS[4 + j][0:m, 0:D], b2B[0:m, e, :], ALU.add))
                    link(v.tensor_scalar(t[0:m], t[0:m], xb[u][0:m, j, 2 * D:2 * D + 1], None, ALU.mult))
                    step(v.tensor_scalar(y[0:m], t[0:m], POSINF, -POSINF, ALU.min, ALU.max))
                    link(v.tensor_scalar(mask[0:m], t[0:m], 0.0, 0.0, ALU.mult, ALU.is_equal))
                    link(v.copy_predicated(y[0:m], mask[0:m], t[0:m]))
                    link(v.tensor_tensor(mask[0:m], t[0:m], t[0:m], ALU.not_equal))
                    link(v.copy_predicated(y[0:m], mask[0:m], zero_y[0:m]))
                    ins = v.tensor_tensor(y[0:m], y[0:m], xb[u][0:m, j, D:2 * D], ALU.add)
                    ins.then_inc(s_y, 1)
                dve.wait_ge(s_y, 4 * e + 4)
                v.memset(fb[:, 3:4], 0.0).then_inc(s_xbfree[u], 1)

        @block.scalar
        def _(act):
            s = nc.scalar

            def root(mark, width, lo=0):
                act.wait_ge(s_sqi, mark)
                s.activation(rs[:, 1, lo:lo + width], rs[:, 0, lo:lo + width], ACT.Sqrt).then_inc(s_sq, 1)

            act.wait_ge(s_minus, 1)
            act.wait_ge(s_const, 2)
            act.wait_ge(s_split, 2)
            for k in range(LO_ACT + 1):
                if k < LO_ACT:
                    if k >= 3:
                        act.wait_ge(s_ohact, k - 2)
                    s.activation(apart[k % 3], lo16, ACT.Abs, bias=minus[:, k:k + 1]).then_inc(s_apart, 1)
                if k >= 1:
                    act.wait_ge(s_apart, k)
                    s.activation(oh_lo[0:ROWS, P - LO_ACT + k - 1, :], apart[(k - 1) % 3], ACT.Relu, scale=-1.0,
                                 bias=ones[0:ROWS, 0:1]).then_inc(s_ohact, 1)
            nb = E * F // P
            gcnb, linb, gateb = (VT[:, nb + 2 * k:nb + 2 * k + 2] for k in range(3))
            root(1, NT)
            act.wait_ge(s_vT, 1)
            s.activation(VT[:, :], PS[7][:, 0:nb + 10], ACT.Copy).then_inc(s_vTc, 1)

            def spread_copied(q):
                n = min(512, NPAD - 512 * q)
                act.wait_ge(s_bc, q + 1)
                s.activation(DB[:, 512 * q:512 * q + n], PS[2 + q % 2][:, 0:n], ACT.Copy).then_inc(s_bcc, 1)

            def lin_copied(q, h):
                n = min(512, NPAD - 512 * q)
                act.wait_ge(s_lin, H * q + h + 1)
                s.activation(XL[:, h, 512 * q:512 * q + n], PS[6 + h][:, 0:n], ACT.Identity,
                             bias=linb[:, h:h + 1]).then_inc(s_linc, 1)

            def ln_copied(q):
                n = min(512, NPAD - 512 * q)
                act.wait_ge(s_lnt, q + 1)
                for h in range(H):
                    s.activation(lnT[q % 2][:, h, 0:n], PS[4 + h][:, 0:n], ACT.Copy).then_inc(s_lnc, 1)

            root(2, NT)
            act.wait_ge(s_vTc, 1)
            ln_copied(0)
            act.wait_ge(s_dx, 1)
            act.wait_ge(s_ln, 1)

            def high_parts(lo, hi):
                for a in range(lo, hi):
                    s.activation(xs[:, a, 0:D], xn[:, a, :], ACT.Copy, scale=dinvx[:, 0, a:a + 1]).then_inc(s_hi, 1)

            high_parts(0, HI_EARLY // 2)
            ln_copied(1)
            lin_copied(0, 0)
            lin_copied(0, 1)
            high_parts(HI_EARLY // 2, HI_EARLY)
            for k, to in enumerate((lowT, keyT)):
                act.wait_ge(s_keyp, 2 * k + 1)
                s.activation(to[:, 0:500], PS[2 * k][:, 0:500], ACT.Copy).then_inc(s_keyc, 1)
                act.wait_ge(s_keyp, 2 * k + 2)
                s.activation(to[:, 500:NW], PS[1 + 2 * k][:, 0:ROWS], ACT.Copy).then_inc(s_keyc, 1)
            act.wait_ge(s_flag, 1)
            fast = act.value_load(flagI[0:1, 0:1], min_val=0, max_val=1)

            def copy_built(gr, i):
                act.wait_ge(s_bld, GI * gr + i + 1)
                s.activation(A[gr % 2][:, :, 20 * i:20 * (i + 1)].rearrange("p a (w d) -> p w a d", d=WN),
                             PS[i % 2][:, 0:4 * KEYS].rearrange("p (w a d) -> p w a d", w=4, d=WN),
                             ACT.Copy).then_inc(s_ev, 1)

            def beside_copied(kind, q, h):
                if kind == "T":
                    ln_copied(q)
                elif kind == "L":
                    lin_copied(q, h)
                else:
                    spread_copied(q)

            with act.If(fast == 1):
                for i in range(GI):
                    copy_built(0, i)
                    if HI_EARLY + i < NT:
                        high_parts(HI_EARLY + i, HI_EARLY + i + 1)
                    beside_copied(*beside[i])
            with act.Else():
                high_parts(HI_EARLY, NT)
                for unit in beside:
                    beside_copied(*unit)

            def weights_high(e, k):
                full, to = ((w1s, w1r[e % 2][0]), (w2s, w2r[e % 2][0]))[k]
                act.wait_ge(s_wl[k], 16 * (e + 1))
                if e >= 2 and k == 0:
                    act.wait_ge(s_down, 4 * (e - 1))
                s.activation(to, full, ACT.Copy).then_inc(s_wh, 1)

            def tanh(q):
                nn = GN if q < G - 1 else LASTN
                act.wait_ge(s_gcn, q + 1)
                for h in range(H):
                    s.activation(zT[q % 2][:, h, 0:nn], PS[6 + h][:, 0:nn], ACT.Tanh,
                                 bias=gcnb[:, h:h + 1]).then_inc(s_z, 1)

            def sigmoid(q):
                nn = GN if q < G - 1 else LASTN
                act.wait_ge(s_gate, q + 1)
                if q >= 1:
                    act.wait_ge(s_h, H * q)
                for h in range(H):
                    s.activation(gT[:, h, 0:nn], PS[6 + h][:, 0:nn], ACT.Sigmoid,
                                 bias=gateb[:, h:h + 1]).then_inc(s_g, 1)

            for gr in range(0, G):
                with act.If(fast == 1):
                    if gr >= 1 and gr + 1 < G:
                        act.wait_ge(s_agg, gr)
                    for a in range(NT):
                        for i in steps_at(gr, a):
                            copy_built(gr + 1, i)
                        if gr >= 1 and a == GCN_AT + 1:
                            tanh(gr - 1)
                        if gr >= 1 and a == GATE_AT + 1:
                            sigmoid(gr - 1)
                with act.Else():
                    if gr >= 1:
                        tanh(gr - 1)
                        sigmoid(gr - 1)
            tanh(G - 1)
            weights_high(0, 0)
            sigmoid(G - 1)
            weights_high(0, 1)
            root(3, H)
            act.wait_ge(s_bnc, 1)
            for c in range(BN_PARTS):
                m = NPAD // BN_PARTS
                s.activation(XL[:, 1, m * c:m * (c + 1)], XL[:, 1, m * c:m * (c + 1)], ACT.Identity,
                             bias=bnc[:, 2, 1:2], scale=bnc[:, 0, 1:2]).then_inc(s_bn1, 1)

            def y_copied(a):
                act.wait_ge(s_yT, a + 1)
                if a >= 5:
                    act.wait_ge(s_x1p, a // 2 - 1)
                s.activation(ycopy[a // 2 % 2], PS[a % 3][:, 0:D], ACT.Copy).then_inc(s_yc, 1)

            def ln2_odd(c, lo, hi):
                act.wait_ge(s_nmr, c + 1)
                for a in range(lo + 1, hi, 2):
                    s.activation(comb[:, a, 0:D], comb[:, a, D:2 * D], ACT.Identity, bias=rs[:, 3, a:a + 1],
                                 scale=rs[:, 2, a:a + 1]).then_inc(s_xn2o, 1)

            def ln2_copied(q):
                n = min(512, NPAD - 512 * q)
                act.wait_ge(s_xnp, q + 1)
                for h in range(H):
                    s.activation(xnT[q % 2][:, h, 0:n], PS[4 + h][:, 0:n], ACT.Copy).then_inc(s_xnc, 1)

            def exps(c):
                lo, hi = CHUNKS[c]
                act.wait_ge(s_expi, c + 1)
                s.activation(rt(1)[:, lo:hi, :], rt(0)[:, lo:hi, :], ACT.Exp).then_inc(s_exp, 1)

            for kind, k in middle:
                if kind == "y" and k % 2:
                    y_copied(k)
                if kind == "N":
                    lo, hi = CHUNKS[k]
                    root(4 + k, hi - lo, lo)
                    ln2_odd(k, lo, hi)
                if kind == "T":
                    ln2_copied(k)
                if kind == "E":
                    exps(k)

            def rows_high(e):
                for h in range(H):
                    act.wait_ge(s_xbp, H * e + h + 1)
                    s.activation(xbTr[e % 2][0][:, h, :], PS[h][:, :], ACT.Copy).then_inc(s_xbh, 1)

            rows_high(0)
            for e in range(E):
                for f in range(8):
                    act.wait_ge(s_up, 8 * e + f + 1)
                    if e >= 1:
                        act.wait_ge(s_hidl, 8 * (e - 1) + f + 1)
                    s.activation(hidf[:, f, :], PS[2 + f % 2][:, 0:CAPE], ACT.Relu,
                                 bias=VT[:, 8 * e + f:8 * e + f + 1]).then_inc(s_hidf, 1)
                    act.wait_ge(s_hidf, 8 * e + f + 1)
                    if e >= 1 and f == 0:
                        act.wait_ge(s_down, 4 * e)
                    s.activation(hidr[0][:, f, 0:CAPE], hidf[:, f, :], ACT.Copy).then_inc(s_hidh, 1)
                if e + 1 < E:
                    rows_high(e + 1)
                    weights_high(e + 1, 0)
                    weights_high(e + 1, 1)

        @block.tensor
        def _(pe):
            t = nc.tensor
            pe.wait_ge(s_const, 2)
            nb = E * F // P + 10
            pe.wait_ge(s_vec, 16 * 6)
            t.transpose(PS[7][:, 0:nb], VR[:, :], ident[0:nb, 0:nb]).then_inc(s_vT, 1)
            pe.wait_ge(s_ohlo, 1)
            pe.wait_ge(s_ohact, LO_ACT)
            pe.wait_ge(s_ohhi, 1)
            for c in range(RCOLS):
                ins = t.matmul(PS[0][:, 0:NT], oh_lo[0:ROWS, :, c], oh_hi[0:ROWS, :, c], start=(c == 0),
                               stop=(c == RCOLS - 1))
            ins.then_inc(s_hist, 1)

            def spread(k):
                m = min(4, NT - 4 * k)
                pe.wait_ge(s_diag, k + 1)
                if k >= 2:
                    pe.wait_ge(s_bcc, k - 1)
                t.matmul(PS[2 + k % 2][:, 0:P * m], ones[:, :], diag[k % 4][:, 0:m, :].rearrange("p q n -> p (q n)"),
                         start=True, stop=True).then_inc(s_bc, 1)

            def ln_transposed(q):
                if q >= 1:
                    pe.wait_ge(s_lnc, H * q)
                for h in range(H):
                    for a in range(min(4, NT - 4 * q)):
                        ins = t.transpose(PS[4 + h][:, P * a:P * (a + 1)], xn[:, 4 * q + a, P * h:P * (h + 1)], ident[:, :])
                ins.then_inc(s_lnt, 1)

            def lin(q, h):
                pe.wait_ge(s_lnc, H * (q + 1))
                if q >= 1:
                    pe.wait_ge(s_linc, H * (q - 1) + h + 1)
                n = P * min(4, NT - 4 * q)
                for k in range(H):
                    ins = t.matmul(PS[6 + h][:, 0:n], linW[:, k, P * h:P * (h + 1)], lnT[q % 2][:, k, 0:n],
                                   start=(k == 0), stop=(k == H - 1))
                ins.then_inc(s_lin, 1)

            def beside_step(kind, q, h):
                if kind == "T":
                    ln_transposed(q)
                elif kind == "L":
                    lin(q, h)
                else:
                    spread(q)

            pe.wait_ge(s_deg, 1)
            t.matmul(PS[2][0:NT, 0:P], degR[:, :], triF[:, :], start=True, stop=True)
            t.matmul(PS[3][0:NT, 0:1], degR[:, :], ones[:, 0:1], start=True, stop=True).then_inc(s_pfx, 1)
            pe.wait_ge(s_tot, 1)
            t.matmul(PS[1][0:NT, 0:1], triF[0:NT, 0:NT], pfx[:, 0:1], start=True, stop=True).then_inc(s_pfx, 1)
            pe.wait_ge(s_w, 48)
            pe.wait_ge(s_ln, 1)
            ln_transposed(0)
            ln_transposed(1)
            lin(0, 0)
            lin(0, 1)
            pe.wait_ge(s_key, 1)
            low, key = keyw[0], keyw[5]
            for k, w in enumerate((low, key)):
                for j in range(WB):
                    to = PS[2 * k][:, ROWS * j:ROWS * (j + 1)] if j < 4 else PS[1 + 2 * k][:, 0:ROWS]
                    ins = t.transpose(to, w[0:ROWS, j, :], ident[0:ROWS, 0:ROWS])
                    if j >= 3:
                        ins.then_inc(s_keyp, 1)
            pe.wait_ge(s_keyc, 4)
            t.matmul(PS[1][0:1, 0:1], fb[0:ROWS, 0:1], ones[0:ROWS, 0:1], start=True, stop=True).then_inc(s_cnt, 1)
            pe.wait_ge(s_flag, 1)
            fast = pe.value_load(flagI[0:1, 0:1], min_val=0, max_val=1)

            def build(gr, i):
                n = GI * gr + i
                at_, count, _ = place(n // 2)
                pe.wait_ge(s_ohp if at_ == 2 else s_oh, count)
                if n >= 2:
                    pe.wait_ge(s_ev, n - 1)
                for w in range(4):
                    ins = t.matmul(PS[n % 2][:, KEYS * w:KEYS * (w + 1)], ohb[at_][:, 4 * (n % 2) + w, :],
                                   ohk[at_][:, 4 * (n % 2) + w, :], start=True, stop=True)
                ins.then_inc(s_bld, 1)

            def aggregate(gr, a, start, stop):
                nn = GN if gr < G - 1 else LASTN
                for h in range(H):
                    for part in range(2):
                        first, last = start and part == 0, stop and part == 1
                        lo = D * part + P * h
                        ins = t.matmul(PS[2 + 2 * (gr % 2) + h][:, 0:nn], xs[:, a, lo:lo + P], A[gr % 2][:, a, 0:nn],
                                       start=first, stop=last)
                return ins

            def gcn(q):
                nn = GN if q < G - 1 else LASTN
                pe.wait_ge(s_aggc, q + 1)
                if q == 0:
                    pe.wait_ge(s_linc, H * 7)
                else:
                    pe.wait_ge(s_g, H * q)
                for h in range(H):
                    for k in range(H):
                        ins = t.matmul(PS[6 + h][:, 0:nn], gcnW[:, k, P * h:P * (h + 1)], aggT[q % 2][:, k, 0:nn],
                                       start=(k == 0), stop=(k == H - 1))
                ins.then_inc(s_gcn, 1)

            def gate(q):
                nn = GN if q < G - 1 else LASTN
                pe.wait_ge(s_z, H * (q + 1))
                for h in range(H):
                    for k in range(H):
                        ins = t.matmul(PS[6 + h][:, 0:nn], gateW[:, k, P * h:P * (h + 1)], zT[q % 2][:, k, 0:nn],
                                       start=(k == 0), stop=(k == H - 1))
                ins.then_inc(s_gate, 1)

            with pe.If(fast == 1):
                for i in range(GI):
                    build(0, i)
                    beside_step(*beside[i])
            with pe.Else():
                for unit in beside:
                    beside_step(*unit)
            pe.wait_ge(s_bcc, 7)
            for gr in range(G):
                if gr >= 2:
                    pe.wait_ge(s_aggc, gr - 1)
                with pe.If(fast == 1):
                    pe.wait_ge(s_ev, GI * gr + (GI if gr < G - 1 else LASTI))
                    for a in range(NT):
                        for i in steps_at(gr, a):
                            build(gr + 1, i)
                        if gr == 0:
                            pe.wait_ge(*((s_lo, a + 1) if a < LO_POOL else (s_lo2, a + 1 - LO_POOL)))
                        ins = aggregate(gr, a, a == 0, a == NT - 1)
                        if gr >= 1 and a == GCN_AT:
                            gcn(gr - 1)
                        if gr >= 1 and a == GATE_AT:
                            gate(gr - 1)
                    ins.then_inc(s_agg, 1)
                with pe.Else():
                    NC = RCOLS + LOOPC
                    nn = GN if gr < G - 1 else LASTN

                    def general(c, at_row, at_sel, start, stop):
                        pe.wait_ge(s_grow, at_row)
                        pe.wait_ge(s_sel, at_sel)
                        for h in range(H):
                            for part in range(2):
                                lo = D * part + P * h
                                ins = t.matmul(PS[2 + 2 * (gr % 2) + h][:, 0:nn], gath[0:ROWS, lo:lo + P],
                                               dsel[0:ROWS, 0:nn], start=start and part == 0, stop=stop and part == 1)
                        return ins

                    general(0, 16 * (gr * NC + 1), gr * NC + 1, True, False).then_inc(s_gmm, 1)
                    with pe.Fori(1, NC - 1) as c:
                        general(c, 16 * c + 16 * (gr * NC + 1), c + (gr * NC + 1), False, False).then_inc(s_gmm, 1)
                    general(NC - 1, 16 * (gr + 1) * NC, (gr + 1) * NC, False, True).then_inc(s_gmm, 1)
                    pe.wait_ge(s_gmm, (gr + 1) * NC)
                    t.matmul(PS[0][0:1, 0:1], ident[:, 0:1], ident[:, 0:1], start=True, stop=True).then_inc(s_agg, 1)
                    if gr >= 1:
                        gcn(gr - 1)
                        gate(gr - 1)
            gcn(G - 1)
            gate(G - 1)
            def y_transposed(a):
                m = NPAD // BN_PARTS
                pe.wait_ge(s_bn0, -(-P * (a + 1) // m))
                pe.wait_ge(s_bn1, -(-P * (a + 1) // m))
                if a >= 3:
                    pe.wait_ge(s_yc if (a - 3) % 2 else s_x1, (a - 3) // 2 + 1)
                for h in range(H):
                    ins = t.transpose(PS[a % 3][:, P * h:P * (h + 1)], XL[:, h, P * a:P * (a + 1)], ident[:, :])
                ins.then_inc(s_yT, 1)

            def ln2_transposed(q):
                tiles = min(4, NT - 4 * q)
                pe.wait_ge(s_xn2, -(-(4 * q + tiles) // 2))
                pe.wait_ge(s_xn2o, (4 * q + tiles) // 2)
                for h in range(H):
                    if q >= 1:
                        pe.wait_ge(s_xnc, H * (q - 1) + h + 1)
                    for a in range(tiles):
                        ins = t.transpose(PS[4 + h][:, P * a:P * (a + 1)], comb[:, 4 * q + a, P * h:P * (h + 1)],
                                          ident[:, :])
                ins.then_inc(s_xnp, 1)

            def logits(q):
                pe.wait_ge(s_xnc, H * (q + 1))
                c = sum(4 * q >= hi for _, hi in CHUNKS)
                for a in range(min(4, NT - 4 * q)):
                    for k in range(H):
                        ins = t.matmul(PS[(3, 3, 6)[c]][:, E * (4 * q + a):E * (4 * q + a + 1)], xnT[q % 2][:, k, P * a:P * (a + 1)],
                                       fgw[:, k, :], start=(k == 0), stop=(k == H - 1))
                return ins

            def ranks(c):
                lo, hi = CHUNKS[c]
                pe.wait_ge(s_ohr, c + 1)
                r = ohH[:, lo:hi, :]
                t.matmul(PS[7][:, E * lo:E * hi], triH[:, :], r, start=True, stop=True)
                t.matmul(PS[7][:, 256 + E * lo:256 + E * hi], onesH[:, :], r, start=True, stop=True).then_inc(s_pos, 1)

            pe.wait_ge(s_fg, 32)
            for kind, k in middle:
                if kind == "y":
                    y_transposed(k)
                if kind == "T":
                    ln2_transposed(k)
                if kind == "L":
                    ins = logits(k)
                    if 4 * k + 4 in [hi for _, hi in CHUNKS] or k == 6:
                        ins.then_inc(s_log, 1)
                if kind == "R":
                    ranks(k)

            def rows_transposed(e):
                u = e % 2
                pe.wait_ge(s_xb[u], 16 * (e // 2 + 1))
                if e >= 1:
                    pe.wait_ge(s_xbl, H * e)
                for h in range(H):
                    for j in range(4):
                        ins = t.transpose(PS[h][:, P * j:P * (j + 1)], xb[u][:, j, P * h:P * (h + 1)], ident[:, :])
                    ins.then_inc(s_xbp, 1)

            pe.wait_ge(s_pad, 2)
            rows_transposed(0)
            for e in range(E):
                u = e % 2
                pe.wait_ge(s_xbl, H * (e + 1))
                pe.wait_ge(s_wlow, 2 * e + 1)
                for f in range(8):
                    if 8 * e + f >= 2:
                        pe.wait_ge(s_hidf, 8 * e + f - 1)
                    ins = None
                    for k in range(H):
                        for part, (a, b) in enumerate(((0, 0), (0, 1), (1, 0))):
                            ins = t.matmul(PS[2 + f % 2][:, 0:CAPE], w1r[u][a][:, k, P * f:P * (f + 1)],
                                           xbTr[u][b][:, k, 0:CAPE],
                                           start=(k == 0 and part == 0), stop=(k == H - 1 and part == 2))
                    ins.then_inc(s_up, 1)
                if e + 1 < E:
                    rows_transposed(e + 1)
                pe.wait_ge(s_wlow, 2 * e + 2)
                for j in range(4):
                    if e >= 1:
                        pe.wait_ge(s_y, 4 * (e - 1) + j + 1)
                    for f in range(8):
                        if j == 0:
                            pe.wait_ge(s_hidl, 8 * e + f + 1)
                        for part, (a, b) in enumerate(((0, 0), (0, 1), (1, 0))):
                            ins = t.matmul(PS[4 + j][:, 0:D], hidr[a][:, f, P * j:P * (j + 1)],
                                           w2r[u][b][:, f, :],
                                           start=(f == 0 and part == 0), stop=(f == 7 and part == 2))
                    ins.then_inc(s_down, 1)


LO_ACT = 17
HI_POOL = 16
GCN_AT, GATE_AT = 8, 15
X_EARLY = 12
CHUNKS = ((0, 8), (8, 16), (16, NT))
BN_PARTS = 5
LO_POOL = 20
HI_EARLY = 10
FIRST_BUILD = 2

_INS = ["x", "src", "dst", "L0_gnn_gcn_W", "L0_gnn_gcn_b", "L0_gnn_lin_W", "L0_gnn_lin_b", "L0_gnn_gate_W",
        "L0_gnn_gate_b", "L0_gnn_bn_gamma", "L0_gnn_bn_beta", "L0_ffn_gate_w", "L0_ffn_gate_b", "L0_ffn_w1",
        "L0_ffn_b1", "L0_ffn_w2", "L0_ffn_b2"]


def kernel(**inputs):
    import numpy as np
    from concourse import bacc
    from concourse.bass_utils import run_bass_kernel_spmd

    nc = bacc.Bacc("TRN2", target_bir_lowering=False, num_devices=1)
    arrays, args = {}, []
    for name in _INS:
        a = np.ascontiguousarray(inputs[name])
        arrays[f"in_{name}"] = a
        args.append(nc.dram_tensor(f"in_{name}", a.shape, mybir.dt.from_np(a.dtype), kind="ExternalInput").ap())
    out = nc.dram_tensor("out", (N_NODES, D), F32, kind="ExternalOutput").ap()
    gnn_ffn(nc, *args, out)
    r = run_bass_kernel_spmd(nc, [arrays], core_ids=[0])
    return r.results[0]["out"]
```
